# Optimizing a Trainium2 kernel written in Bass

```python
import numpy as np
import jax
import jax.numpy as jnp

def _softmax(x, axis=-1):
    return jax.nn.softmax(x, axis=axis)

def _gelu(x):
    return jax.nn.gelu(x, approximate=True)

def _silu(x):
    return jax.nn.silu(x)

def _sigmoid(x):
    return jax.nn.sigmoid(x)

def _layernorm(x, axis=-1, eps=1e-05):
    m = jnp.mean(x, axis=axis, keepdims=True)
    v = jnp.var(x, axis=axis, keepdims=True)
    return (x - m) / jnp.sqrt(v + eps)

def _scatter_add(tgt, idx, src, axis=0):
    return tgt.at[idx].add(src)

def _segment_sum(src, seg, n):
    return jax.ops.segment_sum(src, seg, n)
kernel_name = 'mk_xattn_ffn_d1_seqx_r8_a387e3'

def setup_inputs(seed: int=0):
    np.random.seed(seed)
    _w = jnp.asarray

    def _rec_inputs():
        import jax
        import jax.numpy as jnp
        _rk = jax.random.key(seed)
        x = 7.22e-05 + 1 * jax.random.normal(jax.random.fold_in(_rk, 1), (4, 512, 128), jnp.float32)
        _lenS = 512 - jax.random.randint(jax.random.fold_in(_rk, 7), (4,), 0, max(1, 512 // 4) + 1, jnp.int32)
        _lenS2 = 154 - jax.random.randint(jax.random.fold_in(_rk, 8), (4,), 0, max(1, 154 // 4) + 1, jnp.int32)
        _ctx_1024P = jax.random.normal(jax.random.fold_in(_rk, 11), (4, 16, 128), jnp.float32)
        _ctx_1024c = jax.random.dirichlet(jax.random.fold_in(_rk, 511), 0.3 * jnp.ones((16,), jnp.float32), (4, 154))
        _ctx_1024t = jnp.einsum('bsk,bkd->bsd', _ctx_1024c, _ctx_1024P)
        _ctx_1024t = _ctx_1024t * jax.lax.rsqrt(jnp.mean(jnp.square(_ctx_1024t)) + 1e-12) * 0.953939
        ctx_1024 = 2.81802e-05 + 1.00001 * (_ctx_1024t + 0.3 * jax.random.normal(jax.random.fold_in(_rk, 611), (4, 154, 128), jnp.float32))
        return (x, ctx_1024)
    x, ctx_1024 = _rec_inputs()

    def _L0_xattn_setup():
        import jax, jax.numpy as jnp
        import numpy as np
        B, NT, NM, C, H, FF = (8, 128, 256, 128, 8, 512)

        def _ln(x, g, b):
            m = x.mean(-1, keepdims=True)
            v = jnp.mean((x - m) ** 2, axis=-1, keepdims=True)
            return (x - m) / jnp.sqrt(v + 1e-05) * g + b
        key = jax.random.key(seed)
        ks = jax.random.split(key, 8)
        w = lambda k, shape, s=0.02: jax.random.normal(k, shape, dtype=jnp.float32) * s
        return {'tgt': jax.random.normal(ks[0], (B, NT, C), dtype=jnp.float32), 'memory': jax.random.normal(ks[1], (B, NM, C), dtype=jnp.float32), 'qkv_w': w(ks[2], (3 * C, C)), 'qkv_b': jnp.zeros((3 * C,), jnp.float32), 'sa_out_w': w(ks[3], (C, C)), 'sa_out_b': jnp.zeros((C,), jnp.float32), 'in_proj_w': w(ks[4], (3 * C, C)), 'in_proj_b': jnp.zeros((3 * C,), jnp.float32), 'mha_out_w': w(ks[5], (C, C)), 'mha_out_b': jnp.zeros((C,), jnp.float32), 'lin1_w': w(ks[6], (FF, C)), 'lin1_b': jnp.zeros((FF,), jnp.float32), 'lin2_w': w(ks[7], (C, FF)), 'lin2_b': jnp.zeros((C,), jnp.float32), 'ln1_g': jnp.ones((C,), jnp.float32), 'ln1_b': jnp.zeros((C,), jnp.float32), 'ln2_g': jnp.ones((C,), jnp.float32), 'ln2_b': jnp.zeros((C,), jnp.float32), 'ln3_g': jnp.ones((C,), jnp.float32), 'ln3_b': jnp.zeros((C,), jnp.float32)}
    _L0_xattn_all = _L0_xattn_setup()
    _L0_xattn_in = {k: v for k, v in _L0_xattn_all.items() if k in ('qkv_w', 'qkv_b', 'sa_out_w', 'sa_out_b', 'in_proj_w', 'in_proj_b', 'mha_out_w', 'mha_out_b', 'lin1_w', 'lin1_b', 'lin2_w', 'lin2_b', 'ln1_g', 'ln1_b', 'ln2_g', 'ln2_b', 'ln3_g', 'ln3_b')}
    del _L0_xattn_all

    def _L0_ffn_setup():
        import jax, jax.numpy as jnp
        import numpy as np
        E = 8
        K = 2
        LN_EPS = 1e-05

        def _expert_ffn(x, w1, b1, gate, w2, b2):
            h = jax.nn.gelu((x @ w1 + b1) * gate, approximate=False)
            return h @ w2 + b2
        key = jax.random.key(seed)
        B, S, D, F = (4, 256, 128, 512)
        F2 = F // 2
        ks = jax.random.split(key, 8)
        s = 0.02
        return {'hidden_states': jax.random.normal(ks[0], (B, S, D), jnp.float32), 'router_w': jax.random.normal(ks[1], (D, E), jnp.float32) * s, 'router_b': jnp.zeros((E,), jnp.float32), 'w1': jax.random.normal(ks[2], (E, D, F), jnp.float32) * s, 'b1': jnp.zeros((E, F), jnp.float32), 'gate': jnp.ones((E, F), jnp.float32), 'w2': jax.random.normal(ks[3], (E, F, D), jnp.float32) * s, 'b2': jnp.zeros((E, D), jnp.float32), 'sw1': jax.random.normal(ks[4], (D, F2), jnp.float32) * s, 'sb1': jnp.zeros((F2,), jnp.float32), 'sgate': jnp.ones((F2,), jnp.float32), 'sw2': jax.random.normal(ks[5], (F2, D), jnp.float32) * s, 'sb2': jnp.zeros((D,), jnp.float32), 'shared_weight': jnp.float32(0.5), 'ln_g': jnp.ones((D,), jnp.float32), 'ln_b': jnp.zeros((D,), jnp.float32)}
    _L0_ffn_all = _L0_ffn_setup()
    _L0_ffn_in = {k: v for k, v in _L0_ffn_all.items() if k in ('router_w', 'router_b', 'w1', 'b1', 'gate', 'w2', 'b2', 'sw1', 'sb1', 'sgate', 'sw2', 'sb2', 'shared_weight', 'ln_g', 'ln_b')}
    del _L0_ffn_all
    return {'x': x, 'ctx_1024': ctx_1024, 'L0_xattn_qkv_w': _L0_xattn_in['qkv_w'], 'L0_xattn_qkv_b': _L0_xattn_in['qkv_b'], 'L0_xattn_sa_out_w': _L0_xattn_in['sa_out_w'], 'L0_xattn_sa_out_b': _L0_xattn_in['sa_out_b'], 'L0_xattn_in_proj_w': _L0_xattn_in['in_proj_w'], 'L0_xattn_in_proj_b': _L0_xattn_in['in_proj_b'], 'L0_xattn_mha_out_w': _L0_xattn_in['mha_out_w'], 'L0_xattn_mha_out_b': _L0_xattn_in['mha_out_b'], 'L0_xattn_lin1_w': _L0_xattn_in['lin1_w'], 'L0_xattn_lin1_b': _L0_xattn_in['lin1_b'], 'L0_xattn_lin2_w': _L0_xattn_in['lin2_w'], 'L0_xattn_lin2_b': _L0_xattn_in['lin2_b'], 'L0_xattn_ln1_g': _L0_xattn_in['ln1_g'], 'L0_xattn_ln1_b': _L0_xattn_in['ln1_b'], 'L0_xattn_ln2_g': _L0_xattn_in['ln2_g'], 'L0_xattn_ln2_b': _L0_xattn_in['ln2_b'], 'L0_xattn_ln3_g': _L0_xattn_in['ln3_g'], 'L0_xattn_ln3_b': _L0_xattn_in['ln3_b'], 'L0_ffn_router_w': _L0_ffn_in['router_w'], 'L0_ffn_router_b': _L0_ffn_in['router_b'], 'L0_ffn_w1': _L0_ffn_in['w1'], 'L0_ffn_b1': _L0_ffn_in['b1'], 'L0_ffn_gate': _L0_ffn_in['gate'], 'L0_ffn_w2': _L0_ffn_in['w2'], 'L0_ffn_b2': _L0_ffn_in['b2'], 'L0_ffn_sw1': _L0_ffn_in['sw1'], 'L0_ffn_sb1': _L0_ffn_in['sb1'], 'L0_ffn_sgate': _L0_ffn_in['sgate'], 'L0_ffn_sw2': _L0_ffn_in['sw2'], 'L0_ffn_sb2': _L0_ffn_in['sb2'], 'L0_ffn_shared_weight': _L0_ffn_in['shared_weight'], 'L0_ffn_ln_g': _L0_ffn_in['ln_g'], 'L0_ffn_ln_b': _L0_ffn_in['ln_b']}

def reference(x, ctx_1024, L0_xattn_qkv_w, L0_xattn_qkv_b, L0_xattn_sa_out_w, L0_xattn_sa_out_b, L0_xattn_in_proj_w, L0_xattn_in_proj_b, L0_xattn_mha_out_w, L0_xattn_mha_out_b, L0_xattn_lin1_w, L0_xattn_lin1_b, L0_xattn_lin2_w, L0_xattn_lin2_b, L0_xattn_ln1_g, L0_xattn_ln1_b, L0_xattn_ln2_g, L0_xattn_ln2_b, L0_xattn_ln3_g, L0_xattn_ln3_b, L0_ffn_router_w, L0_ffn_router_b, L0_ffn_w1, L0_ffn_b1, L0_ffn_gate, L0_ffn_w2, L0_ffn_b2, L0_ffn_sw1, L0_ffn_sb1, L0_ffn_sgate, L0_ffn_sw2, L0_ffn_sb2, L0_ffn_shared_weight, L0_ffn_ln_g, L0_ffn_ln_b):
    import jax
    import jax.numpy as jnp

    def _L0_xattn_ref(tgt, memory, qkv_w, qkv_b, sa_out_w, sa_out_b, in_proj_w, in_proj_b, mha_out_w, mha_out_b, lin1_w, lin1_b, lin2_w, lin2_b, ln1_g, ln1_b, ln2_g, ln2_b, ln3_g, ln3_b):
        import jax, jax.numpy as jnp
        import numpy as np
        B, NT, NM, C, H, FF = (8, 128, 256, 128, 8, 512)

        def _ln(x, g, b):
            m = x.mean(-1, keepdims=True)
            v = jnp.mean((x - m) ** 2, axis=-1, keepdims=True)
            return (x - m) / jnp.sqrt(v + 1e-05) * g + b
        Bx, N, Cx = tgt.shape
        qkv = tgt @ qkv_w.T + qkv_b
        q, k, v = jnp.split(qkv, 3, axis=-1)
        scores = jnp.einsum('bnc,bmc->bnm', q, k) * jnp.sqrt(jnp.float32(Cx))
        diag = jnp.eye(N, dtype=bool)
        scores = jnp.where(diag[None, :, :], scores, -jnp.inf)
        attn = jax.nn.softmax(scores, axis=-1)
        sa = jnp.einsum('bnm,bmc->bnc', attn, v) @ sa_out_w.T + sa_out_b
        x = _ln(tgt + sa, ln1_g, ln1_b)
        d = Cx // H
        wq, wk, wv = jnp.split(in_proj_w, 3, axis=0)
        bq, bk, bv = jnp.split(in_proj_b, 3, axis=0)
        qh = (x @ wq.T + bq).reshape(Bx, N, H, d).transpose(0, 2, 1, 3)
        kh = (memory @ wk.T + bk).reshape(Bx, -1, H, d).transpose(0, 2, 1, 3)
        vh = (memory @ wv.T + bv).reshape(Bx, -1, H, d).transpose(0, 2, 1, 3)
        a = jax.nn.softmax(jnp.einsum('bhnd,bhmd->bhnm', qh, kh) / jnp.sqrt(jnp.float32(d)), axis=-1)
        ca = jnp.einsum('bhnm,bhmd->bhnd', a, vh).transpose(0, 2, 1, 3).reshape(Bx, N, Cx)
        ca = ca @ mha_out_w.T + mha_out_b
        x = _ln(x + ca, ln2_g, ln2_b)
        ff = jax.nn.relu(x @ lin1_w.T + lin1_b) @ lin2_w.T + lin2_b
        return _ln(x + ff, ln3_g, ln3_b)

    def _L0_ffn_ref(hidden_states, router_w, router_b, w1, b1, gate, w2, b2, sw1, sb1, sgate, sw2, sb2, shared_weight, ln_g, ln_b):
        import jax, jax.numpy as jnp
        import numpy as np
        E = 8
        K = 2
        LN_EPS = 1e-05

        def _expert_ffn(x, w1, b1, gate, w2, b2):
            h = jax.nn.gelu((x @ w1 + b1) * gate, approximate=False)
            return h @ w2 + b2
        x = hidden_states
        logits = jnp.einsum('bsd,de->bse', x, router_w) + router_b
        probs = jax.nn.softmax(logits, axis=-1)
        topk_p, topk_i = jax.lax.top_k(probs, K)
        topk_p = topk_p / jnp.sum(topk_p, axis=-1, keepdims=True)
        combine = jnp.sum(jax.nn.one_hot(topk_i, E, dtype=x.dtype) * topk_p[..., None], axis=-2)
        moe = jnp.zeros_like(x)
        for e in range(E):
            moe = moe + combine[..., e:e + 1] * _expert_ffn(x, w1[e], b1[e], gate[e], w2[e], b2[e])
        shared = _expert_ffn(x, sw1, sb1, sgate, sw2, sb2) * jax.nn.sigmoid(shared_weight)
        y = moe + shared
        mu = jnp.mean(y, axis=-1, keepdims=True)
        var = jnp.var(y, axis=-1, keepdims=True)
        return (y - mu) * jax.lax.rsqrt(var + LN_EPS) * ln_g + ln_b
    x = x + _L0_xattn_ref(_layernorm(x, axis=-1), ctx_1024, L0_xattn_qkv_w, L0_xattn_qkv_b, L0_xattn_sa_out_w, L0_xattn_sa_out_b, L0_xattn_in_proj_w, L0_xattn_in_proj_b, L0_xattn_mha_out_w, L0_xattn_mha_out_b, L0_xattn_lin1_w, L0_xattn_lin1_b, L0_xattn_lin2_w, L0_xattn_lin2_b, L0_xattn_ln1_g, L0_xattn_ln1_b, L0_xattn_ln2_g, L0_xattn_ln2_b, L0_xattn_ln3_g, L0_xattn_ln3_b)
    x = x + _L0_ffn_ref(_layernorm(x, axis=-1), L0_ffn_router_w, L0_ffn_router_b, L0_ffn_w1, L0_ffn_b1, L0_ffn_gate, L0_ffn_w2, L0_ffn_b2, L0_ffn_sw1, L0_ffn_sb1, L0_ffn_sgate, L0_ffn_sw2, L0_ffn_sb2, L0_ffn_shared_weight, L0_ffn_ln_g, L0_ffn_ln_b)
    return x

_drawn_inputs = setup_inputs


def setup_inputs(seed=0):
    import zlib

    import numpy as np

    out = dict(_drawn_inputs(seed))
    spreads = {'L0_xattn_qkv_b': (0.0, 0.272),
     'L0_xattn_sa_out_b': (0.0, 0.1),
     'L0_xattn_in_proj_b': (0.0, 0.1),
     'L0_xattn_mha_out_b': (0.0, 0.1),
     'L0_xattn_lin1_b': (0.0, 0.1),
     'L0_xattn_lin2_b': (0.0, 0.1),
     'L0_xattn_ln1_g': (1.0, 0.2),
     'L0_xattn_ln1_b': (0.0, 0.1),
     'L0_xattn_ln2_g': (1.0, 0.2),
     'L0_xattn_ln2_b': (0.0, 0.1),
     'L0_xattn_ln3_g': (1.0, 0.2),
     'L0_xattn_ln3_b': (0.0, 0.1),
     'L0_ffn_router_b': (0.0, 0.1),
     'L0_ffn_b1': (0.0, 0.1),
     'L0_ffn_gate': (1.0, 0.2),
     'L0_ffn_b2': (0.0, 0.1),
     'L0_ffn_sb1': (0.0, 0.1),
     'L0_ffn_sgate': (1.0, 0.6),
     'L0_ffn_sb2': (0.0, 0.1),
     'L0_ffn_ln_g': (1.0, 0.2),
     'L0_ffn_ln_b': (0.0, 0.1)}
    factors = {}
    for name, (base, spread) in spreads.items():
        noise = np.random.default_rng([zlib.crc32(name.encode()), seed]).standard_normal(out[name].shape)
        drawn = base * np.exp(spread * noise) if base else spread * noise
        out[name] = jnp.asarray(drawn.astype(out[name].dtype))
    for name, factor in factors.items():
        out[name] = (out[name] * factor).astype(out[name].dtype)
    return out
```

```python
from contextlib import ExitStack

import concourse.bass as bass
from concourse import mybir

ALU = mybir.AluOpType
ACT = mybir.ActivationFunctionType
AX = mybir.AxisListType
F32 = mybir.dt.float32
F32R = mybir.dt.float32r
U32 = mybir.dt.uint32
I32 = mybir.dt.int32

P = 128
EPS = 1e-5
DVE_STEPS = 138
COMB_STEPS = 30
PREP_STEPS = 12


class Chain:

    def __init__(self, eng, sem, per=0, turn=0, done=0):
        self.eng, self.sem, self.per, self.turn, self.done, self.n = eng, sem, per, turn, done, 0

    def step(self, instruction):
        instruction.then_inc(self.sem, 1)
        self.n += 1

    def settle(self):
        self.eng.wait_ge(self.sem, self.turn * self.per + self.done + self.n)

    def link(self, instruction):
        self.step(instruction)
        self.settle()


def xattn_moe_kernel(
    nc, x, ctx_1024, qkv_w, qkv_b, sa_out_w, sa_out_b, in_proj_w, in_proj_b, mha_out_w, mha_out_b,
    lin1_w, lin1_b, lin2_w, lin2_b, ln1_g, ln1_b, ln2_g, ln2_b, ln3_g, ln3_b,
    router_w, router_b, w1, b1, gate, w2, b2, sw1, sb1, sgate, sw2, sb2, shared_weight, ln_g, ln_b,
    out,
):
    B, S, D = x.shape
    M = ctx_1024.shape[1]
    E, _, F = w1.shape
    FF = lin1_w.shape[0]
    FS = sw1.shape[1]
    H = 8
    DH = D // H
    TB = S // P
    NT = B * TB
    MT = M - P
    HG = 4
    Q = P // HG
    MP = P + Q
    FC = F // P
    FFC = FF // P
    FSC = FS // P
    WE = F + FC
    K2 = 2
    TOKENS = NT * P
    REG = TOKENS + P
    TILES = 40
    ROW = 132
    W_COL, I_COL = D, D + 1
    U = 2
    RU = 6
    WB = 3
    assert D == P and S % P == 0 and B % U == 0 and H * DH == P
    assert RU % WB == 0 and RU % 2 == 0
    assert TILES >= K2 * NT + E - 1 and DH < Q and MT <= Q

    C_B2 = 0
    C_SB2 = C_B2 + E * D
    C_BR = C_SB2 + D
    C_L2 = C_BR + E
    C_MO = C_L2 + D
    C_QK = C_MO + D
    C_END = C_QK + 2 * D

    IDLE = TILES - K2 * NT
    assert NT == IDLE + E
    rows = nc.dram_tensor("dispatched_rows", [E * REG + IDLE * P, ROW], F32).ap()
    pads = nc.dram_tensor("padding_rows", [E * P, ROW], F32).ap()
    results = nc.dram_tensor("expert_results", [K2 * TOKENS + NT * P, D], F32).ap()

    with ExitStack() as ctx:
        def sb(name, shape, dt=F32):
            return ctx.enter_context(nc.sbuf_tensor(name, shape, dt))

        def sem(name):
            return ctx.enter_context(nc.semaphore(name))

        def sides(name):
            return [sem(f"{name}{u}") for u in range(U)]

        def pair(name, shape, dt=F32):
            return [sb(f"{name}{u}", shape, dt) for u in range(U)]

        SL = TB * P
        GS = HG + 1
        pT = pair("pT", [P, GS, SL])
        kb = pair("kb", [P, H * MP])
        kbr = pair("kbr", [P, H, M], F32R)

        class Space:

            def __init__(self, ap):
                self.ap, self.at = ap, 0

            def cut(self, n, p=P):
                self.at += n
                assert self.at <= self.ap.shape[1]
                return self.ap[0:p, self.at - n:self.at]

        flat = [pT[u][:, :, :].rearrange("p g n -> p (g n)") for u in range(U)]

        early = Space(flat[0])
        wqkv = early.cut(3 * D).rearrange("p (k c) -> p k c", k=3)
        wsao = early.cut(D)
        winp = early.cut(3 * D).rearrange("p (k c) -> p k c", k=3)
        wmo = early.cut(D)
        wl1 = early.cut(FFC * D).rearrange("p (k c) -> p k c", k=FFC)
        wl2 = early.cut(FF)
        early = Space(flat[1])
        ctx_main = early.cut(B * D).rearrange("p (b c) -> p b c", b=B)
        ctx_tail = early.cut(B * D, MT).rearrange("p (b c) -> p b c", b=B)
        sel0 = early.cut(H * P).rearrange("p (h c) -> p h c", h=H)

        w1g = sb("w1g", [P, E, WE])
        wbuf = sb("wbuf", [P, WB, WE])
        w2s = sb("w2s", [P, E * F])
        GH = 2
        gate_bc = sb("gate_bc", [P, GH * F])
        sw1s = sb("sw1s", [P, FS])
        sw2s = sb("sw2s", [P, FSC, D])
        wr = sb("wr", [P, E])
        T_SAO, T_Q, T_K, T_V, T_MO, T_L1, T_L2 = 0, 1, 2, 3, 4, 5, 5 + FFC
        NTR = T_L2 + FFC
        wt = sb("wt", [P, NTR, D])
        mm = sb("mm", [P, 2 * D])
        cT = sb("cT", [P, B, M])
        cTr = sb("cTr", [P, B, HG, Q])
        kT = sb("kT", [P, B, MP])
        vmain = sb("vmain", [P, B, H * Q])
        vtail = sb("vtail", [P, B, H * Q])
        col_bq2 = sb("col_bq2", [P, 1])
        col_bk2 = sb("col_bk2", [P, 1])
        col_l1b = sb("col_l1b", [P, FFC])
        col_sg = sb("col_sg", [P, FSC])
        col_sb1 = sb("col_sb1", [P, FSC])
        col_sbg = sb("col_sbg", [P, FSC])
        col_sw = sb("col_sw", [P, 1])
        sig = sb("sig", [P, 1])
        qkvb = sb("qkvb", [P, 3])
        BC = ("sab", "vb2", "g1", "b1", "g2", "b2", "g3", "b3", "g4", "b4")
        bc = {name: sb("bc_" + name, [P, D]) for name in BC}
        b1row = sb("b1row", [E * FC, P])
        grow = sb("grow", [E * FC, P])
        N2 = E * D // P
        NV = N2 + 5
        bcol = sb("bcol", [P, NV])
        bcol_hi = sb("bcol_hi", [P, NV], F32R)
        bcol_lo = sb("bcol_lo", [P, NV], F32R)
        br_row = sb("br_row", [2, E])
        br_hi = sb("br_hi", [2, E], F32R)
        mrow = sb("mrow", [2, 1])
        brow = sb("brow", [P, C_END], F32R)
        ident = sb("ident", [P, P])
        before = sb("before", [P, P])
        onef = sb("onef", [P, P])
        one2 = sb("one2", [P, P], F32R)
        mask8 = sb("mask8", [P, H])
        mask32 = sb("mask32", [P, H])
        sel = sb("sel", [P, H, P], F32R)
        selt = sb("selt", [P, H, Q], F32R)
        nhalf = sb("nhalf", [P, TB])
        down8 = sb("down8", [P, E])
        upto8 = sb("upto8", [P, E])
        ebase = sb("ebase", [P, E])
        thr = sb("thr", [P, NT])
        tile_c = sb("tile_c", [P, TILES])
        smask = sb("smask", [P, E, NT])
        x_all = sb("x_all", [P, NT, D])
        nT_all = sb("nT_all", [P, NT, D])
        row_buf = [sb(f"row_buf{k}", [P, NT, ROW]) for k in range(K2)]
        lg_all = sb("lg_all", [P, NT, E])
        st = pair("st", [P, TB, 6])
        mv = pair("mv", [P, TB, 2])
        ve = pair("ve", [P, TB])
        rstd = pair("rstd", [P, TB])
        h0 = pair("h0", [P, TB, D])
        h0b = pair("h0b", [P, TB, D])
        y = pair("y", [P, TB, D])
        actT = pair("actT", [P, SL])
        sdot = pair("sdot", [P, TB])
        nsc = pair("nsc", [P, TB])
        esc = pair("esc", [P, TB])
        rsc = pair("rsc", [P, TB])
        psc = pair("psc", [P, TB])
        qT = pair("qT", [P, SL])
        qTr = pair("qTr", [P, SL], F32R)
        vm = pair("vm", [P, H * Q])
        vt = pair("vt", [P, H * Q])
        nmax = pair("nmax", [P, TB, H])
        nmT = pair("nmT", [P, SL], F32R)
        rden = pair("rden", [P, TB, H])
        x1, x2 = h0, h0b
        assert 2 * HG == H
        flat3 = lambda ap: ap.rearrange("p t d -> p (t d)")
        av = [[flat3(h0b[u][:, :, :]), flat3(y[u][:, :, :])] for u in range(U)]
        junk = pair("junk", [P, D])
        xt = [kb[0][:, k * ROW:(k + 1) * ROW] for k in range(RU)]
        yt = [h0b[k % U][:, k // U, :] for k in range(RU)]
        hT = [pT[u][:, 1] for u in range(U)]
        hs = [pT[u][:, 0:FSC] for u in range(U)]
        xtT = [actT[u][:, 0:P] for u in range(U)]
        late = Space(flat[0][:, 2 * SL:])
        lgm, pr, oh0, oh1, key, picks, tot, incl, slot, cmp, tmp = [late.cut(NT * E) for _ in range(11)]
        late = Space(flat[1][:, 2 * SL:])
        tcmp = late.cut(TILES * E).rearrange("p (j e) -> p j e", j=TILES)
        teid, toff, tdum = [late.cut(TILES) for _ in range(3)]
        m0, ssum, rs16, m1, kmax, ws, wrs, wk0, wk1, sl16 = [late.cut(NT) for _ in range(10)]
        cnt, ntl, tend, tval = [late.cut(E) for _ in range(4)]
        oh = [oh0, oh1]
        wk = [wk0, wk1]
        te = lambda ap: ap.rearrange("p (t e) -> p t e", e=E)
        et = lambda ap: ap.rearrange("p (e t) -> p e t", t=NT)
        idx = sb("idx", [P, K2, NT], U32)
        meta = sb("meta", [P, 2, TILES], I32)
        cnti = sb("cnti", [P, E], I32)
        yk = [[qT[u][:, :].rearrange("p (t d) -> p t d", d=D) for u in range(U)],
              [y[u][:, :, :] for u in range(U)]]
        fin = h0

        quad = [ctx.enter_context(nc.psum_tensor(f"quad{u}", [P, 4, 512], F32)) for u in range(U)]
        bank = [[quad[u][:, k, :] for k in range(4)] for u in range(U)]


        in_x, in_w, in_ctx, in_late = sem("in_x"), sem("in_w"), sem("in_ctx"), sem("in_late")
        in_vec, in_col = sem("in_vec"), sem("in_col")
        in_w1, in_w2, in_gate, gate_used = sem("in_w1"), sem("in_w2"), sem("in_gate"), sem("gate_used")
        pool_consts, dve_consts = sem("pool_consts"), sem("dve_consts")
        wt_ps, wt_sb, cT_ps, cT_sb = sem("wt_ps"), sem("wt_sb"), sem("cT_ps"), sem("cT_sb")
        k_ps, k_sb, v_ps, v_sb = sem("k_ps"), sem("k_sb"), sem("v_ps"), sem("v_sb")
        mm_pr, mm_sb, bcol_set, brow_set = sem("mm_pr"), sem("mm_sb"), sem("bcol_set"), sem("brow_set")
        prep_done, unread = sem("prep_done"), sem("unread")
        dve_prep, act_prep = sem("dve_prep"), sem("act_prep")
        dve_link, dve_comb = sem("dve_link"), sem("dve_comb")
        ln_var, ln_rstd = sides("ln_var"), sides("ln_rstd")
        h0_set, h0b_set, x0b_set = sides("h0_set"), sides("h0b_set"), sides("x0b_set")
        tr_ps, tr_sb = sides("tr_ps"), sides("tr_sb")
        mm_ps, sc_set, esc_set, x1_set = sides("mm_ps"), sides("sc_set"), sides("esc_set"), sides("x1_set")
        q_ps, q_sb, qr_sb, kb_set = sides("q_ps"), sides("q_sb"), sides("qr_sb"), sides("kb_set")
        s_ps, max_set, nm_ps, nm_sb = sides("s_ps"), sides("max_set"), sides("nm_ps"), sides("nm_sb")
        st_ps, e_set, av_ps, av_sb = sides("st_ps"), sides("e_set"), sides("av_ps"), sides("av_sb")
        avT_ps, ca_set, y2_ps, x2_set = sides("avT_ps"), sides("ca_set"), sides("y2_ps"), sides("x2_set")
        l1_ps, l1_sb, y3_ps = sides("l1_ps"), sides("l1_sb"), sides("y3_ps")
        n_set, row_set, nT_set = sides("n_set"), sides("row_set"), sides("nT_set")
        lg_ps, lg_set = sides("lg_ps"), sides("lg_set")
        max0_set, ex_set, picks_set, rank_ps = sem("max0_set"), sem("ex_set"), sem("picks_set"), sem("rank_ps")
        dve_rout, slots_set, meta_set = sem("dve_rout"), sem("slots_set"), sem("meta_set")
        rows_out, pads_out, pads_set = sem("rows_out"), sem("pads_out"), sem("pads_set")
        hs_ps, hs_set, sh_ps, sh_set = sides("hs_ps"), sides("hs_set"), sides("sh_ps"), sides("sh_set")
        xt_in, y_set, y_out = ([sem(f"{s}{k}") for k in range(RU)] for s in ("xt_in", "y_set", "y_out"))
        xt_ps, xt_sb, w_sb, up_ps = sem("xt_ps"), sem("xt_sb"), sem("w_sb"), sem("up_ps")
        h_set, dn_ps, b1_set, b1_ps = sem("h_set"), sem("dn_ps"), sem("b1_set"), sem("b1_ps")
        yk_in, fin_set, fin_out = sides("yk_in"), sides("fin_set"), sides("fin_out")
        cv_var, cv_rstd = sides("cv_var"), sides("cv_rstd")

        TURNS = B // U
        ETURNS = TILES // RU
        assert TILES - ETURNS * RU >= 2
        N_COL = 14
        SEGS = (C_SB2, C_L2, C_MO, C_QK, C_QK + D)
        x_v = x.rearrange("b (t p) d -> p (b t) d", p=P)
        out_v = out.rearrange("b (t p) d -> p (b t) d", p=P)
        res_v = results.rearrange("(t p) d -> p t d", p=P)

        def column(v):
            return v.rearrange("(c p) -> p c", p=P)

        def apart(eng):
            eng.sem_inc(unread, 1)

        block = ctx.enter_context(nc.Block())

        @block.sync
        def _(sp):
            for b in range(B):
                sp.dma_start(x_all[:, b * TB:(b + 1) * TB, :],
                             x_v[:, b * TB:(b + 1) * TB, :]).then_inc(in_x, 16)
            sp.dma_start(wqkv, qkv_w.rearrange("(k p) c -> p k c", p=P)).then_inc(in_w, 16)
            sp.dma_start(wsao, sa_out_w).then_inc(in_w, 16)
            sp.dma_start(winp, in_proj_w.rearrange("(k p) c -> p k c", p=P)).then_inc(in_w, 16)
            sp.dma_start(wmo, mha_out_w).then_inc(in_w, 16)
            sp.dma_start(wl1, lin1_w.rearrange("(k p) c -> p k c", p=P)).then_inc(in_w, 16)
            sp.dma_start(wl2, lin2_w).then_inc(in_w, 16)
            sp.dma_start(ctx_main, ctx_1024[:, 0:P, :].rearrange("b m c -> m b c")).then_inc(in_ctx, 16)
            sp.dma_start(ctx_tail, ctx_1024[:, P:M, :].rearrange("b m c -> m b c")).then_inc(in_ctx, 16)
            sp.wait_ge(pads_set, 1)
            sp.dma_start(rows[E * REG:, :].rearrange("(t p) r -> p t r", p=P),
                         row_buf[1][:, E:NT, :]).then_inc(pads_out, 16)
            sp.dma_start(pads.rearrange("(t p) r -> p t r", p=P), row_buf[1][:, 0:E, :]).then_inc(pads_out, 16)
            sp.dma_start(sw1s[:, :], sw1).then_inc(in_late, 16)
            sp.dma_start(sw2s[:, :, :], sw2.rearrange("(c p) d -> p c d", p=P)).then_inc(in_late, 16)
            sp.dma_start(wr[:, :], router_w).then_inc(in_late, 16)
            sp.wait_ge(bcol_set, 2)
            sp.wait_ge(pool_consts, 1)
            for r, part in enumerate((bcol_hi, bcol_lo)):
                def put(at, n, cols):
                    sp.dma_start(brow[r:r + 1, at:at + n].bitcast(F32), cols.bitcast(F32)).then_inc(brow_set, 16)

                for k, at in enumerate(SEGS):
                    put(at, D, part[:, N2 + k:N2 + k + 1])
                put(C_B2, E * D, part[:, 0:N2])
            for e in range(E):
                sp.dma_start(w1g[:, e, 0:F], w1[e]).then_inc(in_w1, 16)
            for g in range(E // GH):
                if g:
                    sp.wait_ge(gate_used, g)
                sp.dma_start(gate_bc[:, :], gate[g * GH:(g + 1) * GH, :].rearrange("e f -> (e f)")
                             .partition_broadcast(P)).then_inc(in_gate, 16)
            for e in range(E):
                sp.dma_start(w2s[:, e * F:(e + 1) * F].rearrange("p (c d) -> p c d", d=D),
                             w2[e].rearrange("(c p) d -> p c d", p=P)).then_inc(in_w2, 16)
            sp.wait_ge(meta_set, 1)
            for e in range(E):
                n = sp.value_load(cnti[0:1, e:e + 1], min_val=0, max_val=TOKENS)
                sp.dma_start(rows[bass.ds(n + e * REG, P), :], pads[e * P:(e + 1) * P, :]).then_inc(pads_out, 16)
            sp.wait_ge(pads_out, 16 * (E + 2))
            sp.wait_ge(rows_out, 16 * K2 * NT)

            def load_tile(j, k):
                at = sp.value_load(meta[0:1, 1, bass.ds(j, 1)], min_val=0, max_val=E * REG + (IDLE - 1) * P)
                sp.dma_start(xt[k], rows[bass.ds(at, P), :]).then_inc(xt_in[k], 16)

            for k in range(RU):
                load_tile(k, k)
            with sp.Fori(1, ETURNS) as it:
                for k in range(RU):
                    sp.wait_ge(y_out[k], it * 16)
                    load_tile(it * RU + k, k)
            for k in range(TILES - ETURNS * RU):
                sp.wait_ge(y_out[k], 16 * ETURNS)
                load_tile(ETURNS * RU + k, k)
            for k in range(RU):
                sp.wait_ge(y_out[k], 16 * len(range(k, TILES, RU)))

            def load_results(b, u):
                for k in range(K2):
                    sp.dma_start(yk[k][u], res_v[:, bass.ds(b * TB + k * NT, TB), :]).then_inc(yk_in[u], 16)

            def store(b, u):
                sp.dma_start(out_v[:, bass.ds(b * TB, TB), :], fin[u][:, :, :]).then_inc(fin_out[u], 16)

            for u in range(U):
                load_results(u, u)
            with sp.Fori(0, TURNS - 1) as it:
                for u in range(U):
                    sp.wait_ge(fin_set[u], it + 1)
                    store(it * U + u, u)
                    load_results((it + 1) * U + u, u)
            for u in range(U):
                sp.wait_ge(fin_set[u], TURNS)
                store((TURNS - 1) * U + u, u)
            for u in range(U):
                sp.wait_ge(fin_out[u], 16 * TURNS)

        @block.gpsimd
        def _(pool):
            g = nc.gpsimd
            g.memset(brow[:, :].bitcast(F32), 0.0).then_inc(pool_consts, 1)
            link = Chain(pool, pool_consts, done=1)
            link.step(g.memset(ident[:, :], 0.0))
            link.step(g.memset(before[:, :], 1.0))
            link.step(g.memset(sel0, 0.0))
            link.step(g.memset(mask8[:, :], 1.0))
            link.step(g.memset(mask32[:, :], 1.0))
            link.step(g.memset(smask[:, :, :], 1.0))
            link.step(g.memset(row_buf[1][:, :, :], 0.0))
            link.step(g.memset(row_buf[0][:, :, I_COL + 1:ROW], 0.0))
            link.step(g.memset(nhalf[:, :], -0.5))
            link.step(g.memset(onef[:, :], 1.0))
            link.step(g.memset(mrow[:, :], 0.0))
            link.settle()
            link.step(g.affine_select(out=ident[:, :], in_=ident[:, :], compare_op=ALU.not_equal, fill=1.0,
                                      base=0, pattern=[[-1, P]], channel_multiplier=1))
            link.step(g.affine_select(out=before[:, :], in_=before[:, :], compare_op=ALU.is_gt, fill=0.0,
                                      base=0, pattern=[[1, P]], channel_multiplier=-1))
            link.step(g.affine_select(out=sel0, in_=sel0, compare_op=ALU.not_equal, fill=1.0,
                                      base=0, pattern=[[-1, H], [0, P]], channel_multiplier=1))
            link.step(g.affine_select(out=mask8[:, :], in_=mask8[:, :], compare_op=ALU.is_ge, fill=0.0,
                                      base=0, pattern=[[-DH, H]], channel_multiplier=1))
            m32 = mask32[:, :].rearrange("p (g h) -> p g h", g=2)
            link.step(g.affine_select(out=m32, in_=m32, compare_op=ALU.is_ge, fill=0.0,
                                      base=0, pattern=[[0, 2], [-Q, HG]], channel_multiplier=1))
            link.step(g.memset(smask[:, :, 0:1], 0.0))
            link.step(g.affine_select(out=mrow[:, :], in_=mrow[:, :], compare_op=ALU.not_equal, fill=-1.0,
                                      base=-1, pattern=[[0, 1]], channel_multiplier=1))
            link.settle()
            g.iota(row_buf[1][:, :, I_COL:I_COL + 1].bitcast(I32), pattern=[[P, NT]],
                   base=K2 * TOKENS, channel_multiplier=1).then_inc(pads_set, 1)
            link.step(g.affine_select(out=mask8[:, :], in_=mask8[:, :], compare_op=ALU.is_ge, fill=0.0,
                                      base=DH - 1, pattern=[[DH, H]], channel_multiplier=-1))
            link.step(g.affine_select(out=m32, in_=m32, compare_op=ALU.is_ge, fill=0.0,
                                      base=MT - 1, pattern=[[0, 2], [Q, HG]], channel_multiplier=-1))
            ex = dict(allow_small_or_imprecise_dtypes=True)
            link.step(g.iota(down8[:, :], pattern=[[-1, E]], base=E, channel_multiplier=0, **ex))
            link.step(g.iota(upto8[:, :], pattern=[[1, E]], base=0, channel_multiplier=0, **ex))
            link.step(g.iota(ebase[:, :], pattern=[[REG, E]], base=0, channel_multiplier=0, **ex))
            link.step(g.iota(thr[:, :], pattern=[[P, NT]], base=0, channel_multiplier=0, **ex))
            link.step(g.iota(tile_c[:, :], pattern=[[1, TILES]], base=0, channel_multiplier=0, **ex))
            link.step(g.memset(kT[:, :, :], 0.0))
            link.step(g.memset(cTr[:, :, :, :], 0.0))
            link.step(g.memset(vmain[:, :, :], 0.0))
            link.step(g.memset(vtail[:, :, :], 0.0))
            for u in range(U):
                link.step(g.memset(nmT[u][:, :].bitcast(F32), 0.0))
            pool.wait_ge(pads_out, 16 * 2)
            for k in range(K2):
                link.step(g.iota(row_buf[k][:, :, I_COL:I_COL + 1].bitcast(I32), pattern=[[P, NT]],
                                 base=k * TOKENS, channel_multiplier=1))
            link.settle()
            g.memset(vmain[:, :, :].rearrange("p b (h q) -> p (b h) q", q=Q)[:, :, DH:DH + 1], 1.0)\
             .then_inc(prep_done, 1)

            def rstd_of(u, var_sem, rstd_sem, n):
                pool.wait_ge(var_sem[u], n)
                g.tensor_tensor(rstd[u][:, :], ve[u][:, :], nhalf[:, :], ALU.pow).then_inc(rstd_sem[u], 1)

            def wide(name):
                return bc[name][:, :].unsqueeze(1).to_broadcast([P, TB, D])

            pool.wait_ge(in_vec, 16 * len(BC))
            pool.wait_ge(k_sb, 2)
            pool.wait_ge(v_sb, 3)
            with pool.Fori(0, TURNS) as it:
                for u in range(U):
                    b = it * U + u
                    kv = kT[:, bass.ds(b, 1), :].rearrange("p b m -> p (b m)")
                    g.tensor_tensor(kbr[u][:, :, :], kv[:, 0:M].unsqueeze(1).to_broadcast([P, H, M]),
                                    mask8[:, :].unsqueeze(2).to_broadcast([P, H, M]), ALU.mult)\
                     .then_inc(kb_set[u], 1)
                for u in range(U):
                    rstd_of(u, ln_var, ln_rstd, it * 5 + 1)
                for u in range(U):
                    b = it * U + u
                    pool.wait_ge(h0_set[u], it + 1)
                    g.tensor_tensor(h0b[u][:, :, :], h0[u][:, :, :], wide("sab"), ALU.add).then_inc(h0b_set[u], 1)
                for u in range(U):
                    rstd_of(u, ln_var, ln_rstd, it * 5 + 2)
                for u in range(U):
                    b = it * U + u
                    kv = kT[:, bass.ds(b, 1), :].rearrange("p b m -> p (b m)")
                    g.tensor_tensor(kb[u][:, 0:H * P].rearrange("p (h m) -> p h m", h=H),
                                    kv[:, 0:P].unsqueeze(1).to_broadcast([P, H, P]),
                                    mask8[:, :].unsqueeze(2).to_broadcast([P, H, P]), ALU.mult)\
                     .then_inc(kb_set[u], 1)
                    g.tensor_tensor(kb[u][:, H * P:].rearrange("p (h m) -> p h m", h=H),
                                    kv[:, P:MP].unsqueeze(1).to_broadcast([P, H, Q]),
                                    mask8[:, :].unsqueeze(2).to_broadcast([P, H, Q]), ALU.mult)\
                     .then_inc(kb_set[u], 1)
                    g.tensor_copy(vm[u][:, :], vmain[:, bass.ds(b, 1), :].rearrange("p b m -> p (b m)"))\
                     .then_inc(kb_set[u], 1)
                    g.tensor_copy(vt[u][:, :], vtail[:, bass.ds(b, 1), :].rearrange("p b m -> p (b m)"))\
                     .then_inc(kb_set[u], 1)
                    xs = x_all[:, bass.ds(b * TB, TB), :]
                    g.tensor_tensor(xs, xs, wide("b3"), ALU.add).then_inc(x0b_set[u], 1)
                for nth in (3, 4, 5):
                    for u in range(U):
                        rstd_of(u, ln_var, ln_rstd, it * 5 + nth)
                for u in range(U):
                    b = it * U + u
                    pool.wait_ge(n_set[u], it + 1)
                    for k in range(K2):
                        g.tensor_copy(row_buf[k][:, bass.ds(b * TB, TB), 0:D], y[u][:, :, :])\
                         .then_inc(row_set[u], 1)
            pool.wait_ge(in_w1, 16 * E)
            for e in range(E):
                if e % GH == 0:
                    pool.wait_ge(in_gate, 16 * (e // GH + 1))
                ins = g.tensor_tensor(w1g[:, e, 0:F], w1g[:, e, 0:F],
                                      gate_bc[:, (e % GH) * F:(e % GH + 1) * F], ALU.mult)
                if e % GH == GH - 1:
                    ins.then_inc(gate_used, 1)
            pool.wait_ge(slots_set, 1)
            for u in range(U):
                pool.wait_ge(row_set[u], K2 * TURNS)
            for t in range(NT):
                for k in range(K2):
                    pool.indirect_dma_start(rows[:, :], bass.IndirectOffsetOnAxis(idx[:, k, t:t + 1], 0),
                                            row_buf[k][:, t, :], None).then_inc(rows_out, 16)

            def store_tile(turn, k):
                pool.wait_ge(y_set[k], turn + 1)
                apart(pool)
                pool.indirect_dma_start(
                    results[:, :], bass.IndirectOffsetOnAxis(xt[k][:, I_COL:I_COL + 1].bitcast(U32), 0),
                    yt[k], None).then_inc(y_out[k], 16)

            with pool.Fori(0, ETURNS) as it:
                for k in range(RU):
                    store_tile(it, k)
            for k in range(TILES - ETURNS * RU):
                store_tile(ETURNS, k)
            with pool.Fori(0, TURNS) as it:
                for u in range(U):
                    rstd_of(u, cv_var, cv_rstd, it + 1)

        @block.scalar
        def _(act):
            a = nc.scalar
            flatv = lambda v: v.rearrange("e f -> (e f)").rearrange("(p c) -> p c", p=P)
            act.dma_start(qkvb[:, :], column(qkv_b), allow_slow_non_contiguous=True).then_inc(in_col, 16)
            act.dma_start(col_bq2[:, :], column(in_proj_b[0:D])).then_inc(in_col, 16)
            act.dma_start(col_bk2[:, :], column(in_proj_b[D:2 * D])).then_inc(in_col, 16)
            act.dma_start(col_l1b[:, :], column(lin1_b), allow_slow_non_contiguous=True).then_inc(in_col, 16)
            act.dma_start(b1row[:, :], b1.rearrange("e (c p) -> (e c) p", p=P)).then_inc(in_col, 16)
            act.dma_start(grow[:, :], gate.rearrange("e (c p) -> (e c) p", p=P)).then_inc(in_col, 16)
            act.dma_start(bcol[:, 0:N2], flatv(b2)).then_inc(in_col, 16)
            for k, vec in enumerate((sb2, lin2_b, mha_out_b)):
                act.dma_start(bcol[:, N2 + k:N2 + k + 1], column(vec)).then_inc(in_col, 16)
            act.dma_start(col_sg[:, :], column(sgate), allow_slow_non_contiguous=True).then_inc(in_col, 16)
            act.dma_start(col_sb1[:, :], column(sb1), allow_slow_non_contiguous=True).then_inc(in_col, 16)
            act.dma_start(col_sw[:, :], shared_weight.partition_broadcast(P)).then_inc(in_col, 16)
            act.dma_start(br_row[:, :], router_b.partition_broadcast(2)).then_inc(in_col, 16)
            vecs = dict(sab=sa_out_b, vb2=in_proj_b[2 * D:3 * D], g1=ln1_g, b1=ln1_b, g2=ln2_g, b2=ln2_b,
                        g3=ln3_g, b3=ln3_b, g4=ln_g, b4=ln_b)
            for name in BC:
                act.dma_start(bc[name][:, :], vecs[name].partition_broadcast(P)).then_inc(in_vec, 16)
            act.wait_ge(in_col, 16 * N_COL)
            a.activation(sig[:, :], col_sw[:, :], ACT.Exp, scale=-1.0).then_inc(act_prep, 1)
            act.wait_ge(prep_done, 1)
            for k in range(2):
                act.wait_ge(k_ps, k + 1)
                a.activation(kT[:, 2 * k:2 * k + 2, 0:M],
                             bank[0][2 + k][:, 0:2 * M].rearrange("p (b m) -> p b m", b=2),
                             ACT.Identity, bias=col_bk2[:, :]).then_inc(k_sb, 1)

            def evacuate(u, turn, nth, src, dst):
                act.wait_ge(tr_ps[u], turn * 5 + nth)
                a.copy(dst, src).then_inc(tr_sb[u], 1)

            with act.Fori(0, TURNS) as it:
                for u in range(U):
                    evacuate(u, it, 1, bank[u][0], actT[u][:, :])
                for u in range(U):
                    act.wait_ge(sc_set[u], it + 1)
                    for t in range(TB):
                        ins = a.activation(esc[u][:, t:t + 1], sdot[u][:, t:t + 1], ACT.Exp,
                                           bias=nsc[u][:, t:t + 1], scale=float(D) ** 0.5)
                    ins.then_inc(esc_set[u], 1)
                for u in range(U):
                    evacuate(u, it, 2, bank[u][0], actT[u][:, :])
                for u in range(U):
                    act.wait_ge(q_sb[u], it + 1)
                    a.copy(qTr[u][:, :], qT[u][:, :]).then_inc(qr_sb[u], 1)
                for gr in range(2):
                    for r in range(3):
                        n = gr * 3 + r
                        for u in range(U):
                            act.wait_ge(st_ps[u], it * 6 + n + 1)
                            for i in range(2 if r < 2 else 1):
                                ins = a.activation(pT[u][:, 2 * r + i, :], bank[u][2 * (n % 2) + i], ACT.Exp)
                            ins.then_inc(e_set[u], 1)
                    for u in range(U):
                        act.wait_ge(av_ps[u], it * 2 + gr + 1)
                        a.copy(av[u][gr], bank[u][1 + 2 * gr]).then_inc(av_sb[u], 1)
                for u in range(U):
                    evacuate(u, it, 3, bank[u][2], actT[u][:, :])
                for u in range(U):
                    evacuate(u, it, 4, bank[u][0], actT[u][:, :])
                for c in range(FFC):
                    for u in range(U):
                        act.wait_ge(l1_ps[u], it * FFC + c + 1)
                        a.activation(pT[u][:, c, :], bank[u][c], ACT.Relu,
                                     bias=col_l1b[:, c:c + 1]).then_inc(l1_sb[u], 1)
                for u in range(U):
                    b = it * U + u
                    evacuate(u, it, 5, bank[u][0], actT[u][:, :])
                    a.copy(flat3(nT_all[:, bass.ds(b * TB, TB), :]), bank[u][0]).then_inc(nT_set[u], 1)
            act.wait_ge(max0_set, 1)
            a.activation(pr, lgm, ACT.Exp).then_inc(ex_set, 1)
            with act.Fori(0, TURNS) as it:
                for u in range(U):
                    act.wait_ge(hs_ps[u], it + 1)
                    for c in range(FSC):
                        ins = a.activation(hs[u][:, c, :], bank[u][c], ACT.Gelu,
                                           bias=col_sbg[:, c:c + 1], scale=col_sg[:, c:c + 1])
                    ins.then_inc(hs_set[u], 1)
            for u in range(U):
                act.wait_ge(sh_ps[u], TURNS)

            def gelu_tile(j, k):
                for c in range(FC):
                    if c % 2 == 0:
                        act.wait_ge(up_ps, j * (FC // 2) + c // 2 + 1)
                    a.activation(hT[k % 2][:, c * P:(c + 1) * P],
                                 bank[k % 2][1 + c // 2][:, c % 2 * P:(c % 2 + 1) * P], ACT.Gelu,
                                 bias=wbuf[:, k % WB, F + c:F + c + 1]).then_inc(h_set, 1)

            with act.Fori(0, ETURNS) as it:
                for k in range(RU):
                    gelu_tile(it * RU + k, k)
            for k in range(TILES - ETURNS * RU):
                gelu_tile(ETURNS * RU + k, k)

        @block.vector
        def _(dve):
            v = nc.vector
            prep = Chain(dve, dve_prep)
            dve.wait_ge(prep_done, 1)
            prep.step(v.tensor_copy(sel[:, :, :], sel0))
            prep.step(v.tensor_copy(selt[:, :, :], sel0[:, :, 0:Q]))
            prep.step(v.memset(one2[:, :].bitcast(F32), 0.0))
            prep.settle()
            prep.step(v.memset(selt[:, :, MT:Q].bitcast(F32), 0.0))
            prep.step(v.memset(one2[0:2, :].bitcast(F32), 1.0))
            for k in range(4):
                dve.wait_ge(wt_ps, k + 1)
                n = min(4, NTR - 4 * k)
                v.tensor_copy(wt[:, 4 * k:4 * k + n, :],
                              bank[0][k][:, 0:n * P].rearrange("p (k c) -> p k c", c=P)).then_inc(wt_sb, 1)
            for k in range(2):
                dve.wait_ge(cT_ps, k + 1)
                src = bank[1][k][:, 0:2 * M].rearrange("p (b m) -> p b m", b=2)
                v.tensor_copy(cT[:, 2 * k:2 * k + 2, :], src)
                for r in range(HG):
                    ins = v.tensor_copy(cTr[:, 2 * k:2 * k + 2, r, 0:MT], src[:, :, P:M])
                ins.then_inc(cT_sb, 1)
            dve.wait_ge(in_col, 16 * N_COL)
            v.tensor_tensor(b1row[:, :], b1row[:, :], grow[:, :], ALU.mult).then_inc(b1_set, 1)
            dve.wait_ge(mm_pr, 1)
            v.tensor_copy(mm[:, :], bank[1][2][:, 0:2 * D]).then_inc(mm_sb, 1)
            prep.step(v.tensor_copy(bcol[:, NV - 2:NV], bank[1][3][:, 0:2]))
            dve.wait_ge(b1_ps, 1)
            prep.step(v.tensor_copy(w1g[:, :, F:WE],
                                    bank[1][2][:, 0:E * FC].rearrange("p (e c) -> p e c", c=FC)))
            prep.step(v.tensor_copy(br_hi[:, :], br_row[:, :]))
            prep.step(v.tensor_tensor(col_sbg[:, :], col_sb1[:, :], col_sg[:, :], ALU.mult))
            dve.wait_ge(act_prep, 1)
            prep.step(v.tensor_scalar(sig[:, :], sig[:, :], 1.0, None, ALU.add))
            prep.settle()
            v.tensor_copy(bcol_hi[:, :], bcol[:, :]).then_inc(bcol_set, 1)
            prep.step(v.reciprocal(sig[:, :], sig[:, :]))
            prep.step(v.scalar_tensor_tensor(out=brow[0:2, C_BR:C_BR + E], in0=br_hi[:, :].bitcast(F32),
                                             scalar=mrow[:, :], in1=br_row[:, :], op0=ALU.mult, op1=ALU.add))
            dve.wait_ge(bcol_set, 1)
            v.tensor_tensor(bcol_lo[:, :], bcol[:, :], bcol_hi[:, :].bitcast(F32), ALU.subtract)\
             .then_inc(bcol_set, 1)
            bv = bc["vb2"][:, :].rearrange("p (h d) -> p h d", d=DH)
            dve.wait_ge(in_vec, 16 * len(BC))
            dve.wait_ge(v_ps, 2)
            for b in range(B):
                for k, dst in enumerate((vmain, vtail)):
                    ins = v.tensor_tensor(dst[:, b, :].rearrange("p (h q) -> p h q", q=Q)[:, :, 0:DH],
                                          bank[0][k][:, b * D:(b + 1) * D].rearrange("p (h d) -> p h d", d=DH),
                                          bv, ALU.add)
            ins.then_inc(v_sb, 1)
            dve.wait_ge(v_sb, 1)
            for b in range(B):
                tail = vtail[:, b, :].rearrange("p (h q) -> p h q", q=Q)
                ins = v.memset(tail[:, :, DH:DH + 1], 1.0)
            ins.then_inc(v_sb, 1)
            dve.wait_ge(v_sb, 2)
            for b in range(B):
                tail = vtail[:, b, :].rearrange("p (h q) -> p h q", q=Q)
                ins = v.tensor_tensor(tail, tail, mask32[:, :].unsqueeze(2).to_broadcast([P, H, Q]), ALU.mult)
            ins.then_inc(v_sb, 1)
            prep.settle()

            def stats(sources, var_sem, link):
                apart(dve)
                for u, src in sources:
                    for t in range(TB):
                        link.step(v.bn_stats(st[u][:, t, :], src(t)))
                link.settle()
                apart(dve)
                for u, _ in sources:
                    for t in range(TB):
                        link.step(v.bn_aggr(mv[u][:, t, :], st[u][:, t, :]))
                link.settle()
                for u, _ in sources:
                    v.tensor_scalar(ve[u][:, :], mv[u][:, :, 1], EPS, None, ALU.add).then_inc(var_sem[u], 1)

            def tiles_of(b, t):
                return x_all[:, bass.ds(b * TB + t, 1), :].rearrange("p t d -> p (t d)")

            def normed(u, src, dst, done):
                for t in range(TB):
                    ins = v.tensor_scalar(dst[:, t, :], src(t), mv[u][:, t, 0:1], rstd[u][:, t:t + 1],
                                          ALU.subtract, ALU.mult)
                ins.then_inc(done, 1)

            def scaled(u, gain, link):
                for t in range(TB):
                    link.step(v.scalar_tensor_tensor(out=y[u][:, t, :], in0=y[u][:, t, :],
                                                     scalar=mv[u][:, t, 0:1], in1=bc[gain][:, :],
                                                     op0=ALU.subtract, op1=ALU.mult))

            dve.wait_ge(in_x, 16 * B)
            with dve.Fori(0, TURNS) as it:
                link = Chain(dve, dve_link, DVE_STEPS, it)
                both = range(U)
                stats([(u, lambda t, u=u: tiles_of(it * U + u, t)) for u in both], ln_var, link)
                for u in both:
                    dve.wait_ge(ln_rstd[u], it * 5 + 1)
                    normed(u, lambda t: tiles_of(it * U + u, t), h0[u], h0_set[u])
                for u in both:
                    dve.wait_ge(mm_ps[u], it + 1)
                    for t in range(TB):
                        link.step(v.tensor_tensor_reduce(
                            out=junk[u][:, :], in0=h0[u][:, t, :],
                            in1=bank[u][1 + t // 2][:, (t % 2) * 2 * D:(t % 2) * 2 * D + D],
                            scale=1.0, scalar=0.0, op0=ALU.mult, op1=ALU.add, accum_out=sdot[u][:, t:t + 1]))
                        link.settle()
                for u in both:
                    v.tensor_scalar(nsc[u][:, :], sdot[u][:, :], -float(D) ** 0.5, None, ALU.mult)\
                     .then_inc(sc_set[u], 1)
                for u in both:
                    dve.wait_ge(esc_set[u], it + 1)
                    link.step(v.reciprocal(rsc[u][:, :], esc[u][:, :]))
                link.settle()
                for u in both:
                    link.step(v.tensor_tensor(psc[u][:, :], esc[u][:, :], rsc[u][:, :], ALU.mult))
                link.settle()
                for u in both:
                    dve.wait_ge(h0b_set[u], it + 1)
                    for t in range(TB):
                        at = (t % 2) * 2 * D + D
                        link.step(v.scalar_tensor_tensor(out=y[u][:, t, :], in0=bank[u][1 + t // 2][:, at:at + D],
                                                         scalar=psc[u][:, t:t + 1], in1=h0b[u][:, t, :],
                                                         op0=ALU.mult, op1=ALU.add))
                link.settle()
                stats([(u, lambda t, u=u: y[u][:, t, :]) for u in both], ln_var, link)

                def affine(nth, gain, bias, dst, done):
                    for u in both:
                        scaled(u, gain, link)
                    link.settle()
                    for u in both:
                        dve.wait_ge(ln_rstd[u], it * 5 + nth)
                        for t in range(TB):
                            ins = v.scalar_tensor_tensor(out=dst(u, t), in0=y[u][:, t, :],
                                                         scalar=rstd[u][:, t:t + 1], in1=bias(u, t),
                                                         op0=ALU.mult, op1=ALU.add)
                            if done is None:
                                link.step(ins)
                        if done is not None:
                            ins.then_inc(done[u], 1)

                affine(2, "g1", lambda u, t: bc["b1"][:, :], lambda u, t: x1[u][:, t, :], x1_set)
                for u in both:
                    dve.wait_ge(q_ps[u], it + 1)
                    v.tensor_scalar(qT[u][:, :], bank[u][1], col_bq2[:, :], float(DH) ** -0.5,
                                    ALU.add, ALU.mult).then_inc(q_sb[u], 1)
                for t in range(TB):
                    for u in both:
                        dve.wait_ge(s_ps[u], it * TB + t + 1)
                        v.tensor_reduce(nmax[u][:, t, :].rearrange("p (k j) -> p k j", j=2),
                                        quad[u][:, :, 0:2 * M].rearrange("p k (j m) -> p k j m", j=2),
                                        AX.X, ALU.max, negate=True).then_inc(max_set[u], 1)
                for u in both:
                    dve.wait_ge(nm_ps[u], it + 1)
                    v.tensor_copy(nmT[u][0:H, :], bank[u][0][0:H, :]).then_inc(nm_sb[u], 1)
                for u in both:
                    dve.wait_ge(avT_ps[u], it + 1)
                    o = quad[u][:, 0:2, :].rearrange("p k (a q) -> p (k a) q", q=Q)
                    link.step(v.reciprocal(rden[u][:, :, :].rearrange("p t h -> p (t h)").unsqueeze(2),
                                           o[:, :, DH:DH + 1]))
                link.settle()
                for u in both:
                    o = quad[u][:, 0:2, :].rearrange("p k (a q) -> p (k a) q", q=Q)
                    v.tensor_tensor(y[u][:, :, :].rearrange("p t (h d) -> p (t h) d", d=DH), o[:, :, 0:DH],
                                    rden[u][:, :, :].rearrange("p t h -> p (t h)").unsqueeze(2)
                                    .to_broadcast([P, TB * H, DH]), ALU.mult).then_inc(ca_set[u], 1)
                for u in both:
                    dve.wait_ge(y2_ps[u], it + 1)
                    link.step(v.tensor_tensor(flat3(y[u][:, :, :]), bank[u][3], flat3(x1[u][:, :, :]), ALU.add))
                link.settle()
                stats([(u, lambda t, u=u: y[u][:, t, :]) for u in both], ln_var, link)
                affine(3, "g2", lambda u, t: bc["b2"][:, :], lambda u, t: x2[u][:, t, :], x2_set)
                for u in both:
                    dve.wait_ge(x2_set[u], it + 1)
                    dve.wait_ge(y3_ps[u], it + 1)
                    link.step(v.tensor_tensor(flat3(y[u][:, :, :]), bank[u][1], flat3(x2[u][:, :, :]), ALU.add))
                link.settle()
                stats([(u, lambda t, u=u: y[u][:, t, :]) for u in both], ln_var, link)
                for u in both:
                    dve.wait_ge(x0b_set[u], it + 1)
                affine(4, "g3", lambda u, t: tiles_of(it * U + u, t), lambda u, t: tiles_of(it * U + u, t), None)
                link.settle()
                stats([(u, lambda t, u=u: tiles_of(it * U + u, t)) for u in both], ln_var, link)
                for u in both:
                    dve.wait_ge(ln_rstd[u], it * 5 + 5)
                    normed(u, lambda t: tiles_of(it * U + u, t), y[u], n_set[u])
                for u in both:
                    b = it * U + u
                    dve.wait_ge(lg_ps[u], it + 1)
                    v.tensor_copy(lg_all[:, bass.ds(b * TB, TB), :],
                                  bank[u][1][:, 0:TB * E].rearrange("p (t e) -> p t e", e=E)).then_inc(lg_set[u], 1)
                assert link.n == DVE_STEPS, link.n

            r = Chain(dve, dve_rout)
            for u in range(U):
                dve.wait_ge(lg_set[u], TURNS)
            lgf = lg_all[:, :, :]
            over_e = lambda ap: ap.unsqueeze(2).to_broadcast([P, NT, E])
            of_e = lambda ap: ap.unsqueeze(1).to_broadcast([P, NT, E])
            r.link(v.tensor_reduce(m0, lgf, AX.X, ALU.max))
            v.tensor_tensor(te(lgm), lgf, over_e(m0), ALU.subtract).then_inc(max0_set, 1)
            dve.wait_ge(ex_set, 1)
            r.link(v.tensor_reduce(ssum, te(pr), AX.X, ALU.add))
            r.link(v.reciprocal(rs16, ssum))
            r.link(v.tensor_tensor(te(pr), te(pr), over_e(rs16), ALU.mult))
            for k in range(K2):
                r.link(v.tensor_reduce(wk[k], te(pr), AX.X, ALU.max))
                r.link(v.tensor_tensor(te(key), te(pr), over_e(wk[k]), ALU.is_equal))
                r.link(v.tensor_tensor(te(key), te(key), of_e(down8[:, :]), ALU.mult))
                r.link(v.tensor_reduce(kmax, te(key), AX.X, ALU.max))
                r.link(v.tensor_tensor(te(oh[k]), te(key), over_e(kmax), ALU.is_equal))
                if k == 0:
                    r.link(v.scalar_tensor_tensor(out=pr, in0=oh[0], scalar=-4.0, in1=pr,
                                                  op0=ALU.mult, op1=ALU.add))
            v.tensor_tensor(picks, oh[0], oh[1], ALU.add).then_inc(picks_set, 1)
            r.link(v.tensor_tensor(ws, wk[0], wk[1], ALU.add))
            r.link(v.reciprocal(wrs, ws))
            for k in range(K2):
                r.link(v.tensor_tensor(row_buf[k][:, :, W_COL:W_COL + 1].rearrange("p t o -> p (t o)"),
                                       wk[k], wrs, ALU.mult))
            dve.wait_ge(rank_ps, 1)
            rank = bank[0][3]
            r.link(v.tensor_copy(et(tot), rank[:, NT * E:2 * NT * E].rearrange("p (t e) -> p e t", e=E)))
            r.link(v.tensor_tensor_scan(incl, smask[:, :, :].rearrange("p e t -> p (e t)"), tot, 0.0,
                                        ALU.mult, ALU.add))
            r.step(v.tensor_copy(cnt.unsqueeze(2), et(incl)[:, :, NT - 1:NT]))
            r.link(v.tensor_tensor(tmp, incl, tot, ALU.subtract))
            r.link(v.tensor_tensor(te(slot), rank[:, 0:NT * E].rearrange("p (t e) -> p t e", e=E),
                                   tmp.rearrange("p (e t) -> p t e", t=NT), ALU.add))
            r.link(v.tensor_tensor(te(slot), te(slot), of_e(ebase[:, :]), ALU.add))
            for k in range(K2):
                r.link(v.tensor_tensor(key, slot, oh[k], ALU.mult))
                r.link(v.tensor_reduce(sl16, te(key), AX.X, ALU.add))
                ins = v.tensor_copy(idx[:, k, :], sl16)
                if k < K2 - 1:
                    r.link(ins)
            ins.then_inc(slots_set, 1)
            r.step(v.tensor_copy(cnti[:, :], cnt))
            r.link(v.tensor_tensor(et(cmp), cnt.unsqueeze(2).to_broadcast([P, E, NT]),
                                   thr[:, :].unsqueeze(1).to_broadcast([P, E, NT]), ALU.is_gt))
            r.link(v.tensor_reduce(ntl, et(cmp), AX.X, ALU.add))
            r.link(v.tensor_tensor_scan(tend, onef[:, 0:E], ntl, 0.0, ALU.mult, ALU.add))
            r.step(v.tensor_tensor(tcmp, tend.unsqueeze(1).to_broadcast([P, TILES, E]),
                                   tile_c[:, :].unsqueeze(2).to_broadcast([P, TILES, E]), ALU.is_le))
            r.link(v.tensor_tensor(tval, tend, ntl, ALU.subtract))
            r.step(v.tensor_reduce(teid, tcmp, AX.X, ALU.add))
            r.link(v.scalar_tensor_tensor(out=tval, in0=tval, scalar=-float(P), in1=ebase[:, :],
                                          op0=ALU.mult, op1=ALU.add))
            r.link(v.tensor_tensor(tcmp, teid.unsqueeze(2).to_broadcast([P, TILES, E]),
                                   upto8[:, :].unsqueeze(1).to_broadcast([P, TILES, E]), ALU.is_equal))
            r.link(v.tensor_tensor(tcmp, tcmp, tval.unsqueeze(1).to_broadcast([P, TILES, E]), ALU.mult))
            r.link(v.tensor_reduce(toff, tcmp, AX.X, ALU.add))
            r.step(v.scalar_tensor_tensor(out=toff, in0=tile_c[:, :], scalar=float(P), in1=toff,
                                          op0=ALU.mult, op1=ALU.add))
            r.link(v.tensor_scalar(tdum, teid, float(E), None, ALU.is_ge))
            r.link(v.scalar_tensor_tensor(out=toff, in0=tdum, scalar=float(E * REG - K2 * NT * P), in1=toff,
                                          op0=ALU.mult, op1=ALU.add))
            r.link(v.tensor_scalar(teid, teid, float(E - 1), None, ALU.min))
            r.link(v.tensor_copy(meta[:, 1, :], toff))
            v.tensor_copy(meta[:, 0, :], teid).then_inc(meta_set, 1)
            with dve.Fori(0, TURNS) as it:
                for u in range(U):
                    dve.wait_ge(sh_ps[u], it + 1)
                    v.tensor_scalar(flat3(nT_all[:, bass.ds((it * U + u) * TB, TB), :]), bank[u][2], sig[:, :], None,
                                    ALU.mult).then_inc(sh_set[u], 1)

            def copy_weights(j, k):
                e = dve.value_load(meta[0:1, 0, bass.ds(j, 1)], min_val=0, max_val=E - 1)
                v.tensor_copy(wbuf[:, k % WB, :], w1g[:, bass.ds(e, 1), :].rearrange("p e c -> p (e c)"))\
                 .then_inc(w_sb, 1)

            def copy_tokens(j, k):
                dve.wait_ge(xt_ps, j + 1)
                v.tensor_copy(xtT[k % 2], bank[k % 2][0][:, 0:P]).then_inc(xt_sb, 1)

            def weigh(j, k):
                dve.wait_ge(dn_ps, j + 1)
                v.tensor_scalar(yt[k % RU], bank[k % 2][3][:, 0:D], xt[k % RU][:, W_COL:W_COL + 1], None,
                                ALU.mult).then_inc(y_set[k % RU], 1)

            def dve_step(j, k):
                copy_tokens(j + 1, k + 1)
                weigh(j - 1, k - 1)
                copy_weights(j + 2, k + 2)

            dve.wait_ge(meta_set, 1)
            dve.wait_ge(gate_used, E // GH)
            for j in range(WB - 1):
                copy_weights(j, j)
            copy_tokens(0, 0)
            copy_tokens(1, 1)
            copy_weights(2, 2)
            with dve.Fori(0, ETURNS) as it:
                for k in range(1, RU + 1):
                    dve_step(it * RU + k, k)
            for j in range(ETURNS * RU + 1, TILES - 2):
                dve_step(j, j)
            copy_tokens(TILES - 1, TILES - 1)
            for j in range(TILES - 3, TILES):
                weigh(j, j)
            with dve.Fori(0, TURNS) as it:
                link = Chain(dve, dve_comb, COMB_STEPS, it)
                both = range(U)
                tiles = lambda ap, u: ap[:, bass.ds((it * U + u) * TB, TB), :]
                for u in both:
                    dve.wait_ge(yk_in[u], 16 * K2 * (it + 1))
                    link.step(v.tensor_tensor(yk[0][u], yk[0][u], yk[1][u], ALU.add))
                link.settle()
                for u in both:
                    link.step(v.tensor_tensor(yk[1][u], tiles(x_all, u),
                                              bc["b4"][:, :].unsqueeze(1).to_broadcast([P, TB, D]), ALU.add))
                    link.step(v.tensor_tensor(yk[0][u], yk[0][u], tiles(nT_all, u), ALU.add))
                link.settle()
                stats([(u, lambda t, u=u: yk[0][u][:, t, :]) for u in both], cv_var, link)
                for u in both:
                    for t in range(TB):
                        link.step(v.scalar_tensor_tensor(out=yk[0][u][:, t, :], in0=yk[0][u][:, t, :],
                                                         scalar=mv[u][:, t, 0:1], in1=bc["g4"][:, :],
                                                         op0=ALU.subtract, op1=ALU.mult))
                link.settle()
                for u in both:
                    dve.wait_ge(cv_rstd[u], it + 1)
                    for t in range(TB):
                        ins = v.scalar_tensor_tensor(out=fin[u][:, t, :], in0=yk[0][u][:, t, :],
                                                     scalar=rstd[u][:, t:t + 1], in1=yk[1][u][:, t, :],
                                                     op0=ALU.mult, op1=ALU.add)
                    ins.then_inc(fin_set[u], 1)
                for u in both:
                    dve.wait_ge(fin_out[u], (it + 1) * 16)
                assert link.n == COMB_STEPS, link.n

        @block.tensor
        def _(pe):
            t_ = nc.tensor

            def mul(out, lhsT, rhs, start=True, stop=True):
                return t_.matmul(out, lhsT, rhs, start=start, stop=stop, skip_group_check=True)

            pe.wait_ge(prep_done, 1)
            pe.wait_ge(in_w, 16 * 6)
            weights = [wsao, winp[:, 0], winp[:, 1], winp[:, 2], wmo] + [wl1[:, c] for c in range(FFC)] \
                + [wl2[:, c * P:(c + 1) * P] for c in range(FFC)]
            for i, w in enumerate(weights):
                ins = t_.transpose(bank[0][i // 4][:, (i % 4) * P:(i % 4 + 1) * P], w, ident[:, :])
                if i % 4 == 3 or i == NTR - 1:
                    ins.then_inc(wt_ps, 1)
            pe.wait_ge(in_ctx, 16 * 2)
            for b in range(B):
                at = (b % 2) * M
                t_.transpose(bank[1][b // 2][:, at:at + P], ctx_main[:, b, :], ident[:, :])
                ins = t_.transpose(bank[1][b // 2][:, at + P:at + M], ctx_tail[:, b, :], ident[0:MT, 0:MT])
                if b % 2:
                    ins.then_inc(cT_ps, 1)
            pe.wait_ge(wt_sb, 1)
            pe.wait_ge(in_col, 16 * N_COL)
            mul(bank[1][2][:, 0:D], wqkv[:, 0], wqkv[:, 1])
            mul(bank[1][2][:, D:2 * D], wqkv[:, 2], wt[:, T_SAO, :])
            mul(bank[1][3][:, 0:1], wqkv[:, 0], qkvb[:, 1:2], stop=False)
            mul(bank[1][3][:, 0:1], wqkv[:, 1], qkvb[:, 0:1], start=False)
            mul(bank[1][3][:, 1:2], wt[:, T_SAO, :], qkvb[:, 2:3]).then_inc(mm_pr, 1)
            pe.wait_ge(b1_set, 1)
            pe.wait_ge(mm_sb, 1)
            t_.transpose(bank[1][2][:, 0:E * FC], b1row[:, :], ident[0:E * FC, 0:E * FC]).then_inc(b1_ps, 1)
            pe.wait_ge(wt_sb, 4)
            for k in range(2):
                pe.wait_ge(cT_sb, k + 1)
                mul(bank[0][2 + k][:, 0:2 * M], wt[:, T_K, :],
                    cT[:, 2 * k:2 * k + 2, :].rearrange("p b m -> p (b m)")).then_inc(k_ps, 1)
            for b in range(B):
                ins = mul(bank[0][0][:, b * D:(b + 1) * D], cT[:, b, 0:P], wt[:, T_V, :])
            ins.then_inc(v_ps, 1)
            for b in range(B):
                ins = mul(bank[0][1][:, b * D:(b + 1) * D], cTr[:, b, :, :].rearrange("p r m -> p (r m)"),
                          wt[:, T_V, :])
            ins.then_inc(v_ps, 1)

            def transpose4(u, k, src, done):
                for t in range(TB):
                    ins = t_.transpose(bank[u][k][:, t * P:(t + 1) * P], src(t), ident[:, :])
                ins.then_inc(done, 1)

            def biased(out, at, n, stop=False):
                return mul(out, one2[:, :], brow[:, at:at + n], stop=stop)

            pe.wait_ge(k_sb, 2)
            pe.wait_ge(v_sb, 3)
            pe.wait_ge(mm_sb, 1)
            pe.wait_ge(brow_set, 16 * 2 * (len(SEGS) + 1))
            pe.wait_ge(dve_prep, PREP_STEPS)
            pe.wait_ge(in_late, 16 * 3)
            with pe.Fori(0, TURNS) as it:
                both = range(U)
                for u in both:
                    pe.wait_ge(h0_set[u], it + 1)
                    transpose4(u, 0, lambda t: h0[u][:, t, :], tr_ps[u])
                for u in both:
                    pe.wait_ge(tr_sb[u], it * 5 + 1)
                    for t in range(TB):
                        o = bank[u][1 + t // 2][:, (t % 2) * 2 * D:(t % 2 + 1) * 2 * D]
                        biased(o, C_QK, 2 * D)
                        ins = mul(o, actT[u][:, t * P:(t + 1) * P], mm[:, :], start=False)
                    ins.then_inc(mm_ps[u], 1)
                for u in both:
                    pe.wait_ge(x1_set[u], it + 1)
                    transpose4(u, 0, lambda t: x1[u][:, t, :], tr_ps[u])
                for u in both:
                    pe.wait_ge(tr_sb[u], it * 5 + 2)
                    mul(bank[u][1], wt[:, T_Q, :], actT[u][:, :]).then_inc(q_ps[u], 1)
                for t in range(TB):
                    for u in both:
                        if t == 0:
                            pe.wait_ge(qr_sb[u], it + 1)
                            pe.wait_ge(kb_set[u], it * 5 + 5)
                        else:
                            pe.wait_ge(max_set[u], it * TB + t)
                        for k in range(4):
                            ins = mul(quad[u][:, k, 0:2 * M], qTr[u][:, t * P:(t + 1) * P],
                                      kbr[u][:, 2 * k:2 * k + 2, :].rearrange("p h m -> p (h m)"))
                        ins.then_inc(s_ps[u], 1)
                for u in both:
                    pe.wait_ge(max_set[u], it * TB + TB)
                    for t in range(TB):
                        ins = t_.transpose(bank[u][0][0:H, t * P:(t + 1) * P], nmax[u][:, t, :], ident[:, :])
                    ins.then_inc(nm_ps[u], 1)
                for gr in range(2):
                    for r in range(3):
                        n = gr * 3 + r
                        for u in both:
                            if n == 0:
                                pe.wait_ge(nm_sb[u], it + 1)
                            if n >= 2:
                                pe.wait_ge(e_set[u], it * 6 + n - 1)
                            if n == 4:
                                pe.wait_ge(av_sb[u], it * 2 + 1)
                            for i in range(2 if r < 2 else 1):
                                o = bank[u][2 * (n % 2) + i]
                                if r < 2:
                                    h = gr * HG + 2 * r + i
                                    keys, pick = kb[u][:, h * P:(h + 1) * P], sel[:, h, :]
                                else:
                                    keys = kb[u][:, H * P + gr * P:H * P + (gr + 1) * P]
                                    pick = selt[:, gr * HG:(gr + 1) * HG, :].rearrange("p h m -> p (h m)")
                                mul(o, pick, nmT[u][:, :], stop=False)
                                ins = mul(o, keys, qT[u][:, :], start=False)
                            ins.then_inc(st_ps[u], 1)
                    for u in both:
                        pe.wait_ge(e_set[u], it * 6 + gr * 3 + 3)
                        for i in range(HG):
                            h = gr * HG + i
                            o = bank[u][1 + 2 * gr][i * Q:(i + 1) * Q, :]
                            mul(o, vm[u][:, h * Q:(h + 1) * Q], pT[u][:, i, :], stop=False)
                        for i in range(HG):
                            h = gr * HG + i
                            o = bank[u][1 + 2 * gr][i * Q:(i + 1) * Q, :]
                            ins = mul(o, vt[u][:, h * Q:(h + 1) * Q], pT[u][:, HG, :], start=False)
                        ins.then_inc(av_ps[u], 1)
                for u in both:
                    pe.wait_ge(av_sb[u], it * 2 + 2)
                    for t in range(TB):
                        for gr in range(2):
                            at = (t % 2) * 2 * P + gr * P
                            ins = t_.transpose(bank[u][t // 2][:, at:at + P], av[u][gr][:, t * P:(t + 1) * P],
                                               ident[:, :])
                    ins.then_inc(avT_ps[u], 1)
                for u in both:
                    pe.wait_ge(ca_set[u], it + 1)
                    transpose4(u, 2, lambda t: y[u][:, t, :], tr_ps[u])
                for u in both:
                    pe.wait_ge(tr_sb[u], it * 5 + 3)
                    for t in range(TB):
                        o = bank[u][3][:, t * P:(t + 1) * P]
                        biased(o, C_MO, D)
                        ins = mul(o, actT[u][:, t * P:(t + 1) * P], wt[:, T_MO, :], start=False)
                    ins.then_inc(y2_ps[u], 1)
                for u in both:
                    pe.wait_ge(x2_set[u], it + 1)
                    transpose4(u, 0, lambda t: x2[u][:, t, :], tr_ps[u])
                for u in both:
                    pe.wait_ge(tr_sb[u], it * 5 + 4)
                    for c in range(FFC):
                        mul(bank[u][c], wt[:, T_L1 + c, :], actT[u][:, :]).then_inc(l1_ps[u], 1)
                for u in both:
                    pe.wait_ge(l1_sb[u], it * FFC + FFC)
                    for t in range(TB):
                        o = bank[u][1][:, t * P:(t + 1) * P]
                        biased(o, C_L2, D)
                        for c in range(FFC):
                            ins = mul(o, pT[u][:, c, t * P:(t + 1) * P], wt[:, T_L2 + c, :],
                                      start=False, stop=c == FFC - 1)
                    ins.then_inc(y3_ps[u], 1)
                for u in both:
                    pe.wait_ge(n_set[u], it + 1)
                    transpose4(u, 0, lambda t: y[u][:, t, :], tr_ps[u])
                for u in both:
                    pe.wait_ge(tr_sb[u], it * 5 + 5)
                    for t in range(TB):
                        o = bank[u][1][:, t * E:(t + 1) * E]
                        biased(o, C_BR, E)
                        ins = mul(o, actT[u][:, t * P:(t + 1) * P], wr[:, :], start=False)
                    ins.then_inc(lg_ps[u], 1)
                for u in both:
                    pe.wait_ge(nT_set[u], it + 1)
            for u in range(U):
                pe.wait_ge(nT_set[u], TURNS)
                pe.wait_ge(lg_set[u], TURNS)
            pe.wait_ge(picks_set, 1)
            mul(bank[0][3][:, 0:NT * E], before[:, :], picks)
            mul(bank[0][3][:, NT * E:2 * NT * E], onef[:, :], picks).then_inc(rank_ps, 1)
            with pe.Fori(0, TURNS) as it:
                for u in range(U):
                    for c in range(FSC):
                        ins = mul(bank[u][c], sw1s[:, c * P:(c + 1) * P],
                                  flat3(nT_all[:, bass.ds((it * U + u) * TB, TB), :]))
                    ins.then_inc(hs_ps[u], 1)
                for u in range(U):
                    pe.wait_ge(hs_set[u], it + 1)
                    for t in range(TB):
                        o = bank[u][2][:, t * P:(t + 1) * P]
                        biased(o, C_SB2, D)
                        for c in range(FSC):
                            ins = mul(o, hs[u][:, c, t * P:(t + 1) * P], sw2s[:, c, :],
                                      start=False, stop=c == FSC - 1)
                    ins.then_inc(sh_ps[u], 1)
                for u in range(U):
                    pe.wait_ge(sh_set[u], it + 1)
            pe.wait_ge(slots_set, 1)
            pe.wait_ge(meta_set, 1)
            pe.wait_ge(in_w2, 16 * E)

            def up(j, k):
                pe.wait_ge(w_sb, j + 1)
                pe.wait_ge(xt_sb, j + 1)
                for c in range(FC):
                    ins = mul(bank[k % 2][1 + c // 2][:, c % 2 * P:(c % 2 + 1) * P],
                              wbuf[:, k % WB, c * P:(c + 1) * P], xtT[k % 2])
                    if c % 2:
                        ins.then_inc(up_ps, 1)

            def turn_tokens(j, k, uses):
                pe.wait_ge(xt_in[k % RU], 16 * uses)
                t_.transpose(bank[k % 2][0][:, 0:P], xt[k % RU][:, 0:D], ident[:, :]).then_inc(xt_ps, 1)

            def down(j, k):
                e = pe.value_load(meta[0:1, 0, bass.ds(j, 1)], min_val=0, max_val=E - 1)
                o = bank[k % 2][3][:, 0:D]
                mul(o, one2[:, :], brow[:, bass.ds(e * D + C_B2, D)], stop=False)
                for c in range(FC):
                    pe.wait_ge(h_set, j * FC + c + 1)
                    ins = mul(o, hT[k % 2][:, c * P:(c + 1) * P], w2s[:, bass.ds(e * F + c * D, D)],
                              start=False, stop=c == FC - 1)
                ins.then_inc(dn_ps, 1)

            def pe_step(j, k, uses):
                up(j, k)
                turn_tokens(j + 1, k + 1, uses)
                down(j - 1, k - 1)

            turn_tokens(0, 0, 1)
            up(0, 0)
            turn_tokens(1, 1, 1)
            with pe.Fori(0, ETURNS) as it:
                for k in range(1, RU + 1):
                    pe_step(it * RU + k, k, it + (k + 1) // RU + 1)
            for j in range(ETURNS * RU + 1, TILES - 1):
                pe_step(j, j, (j + 1) // RU + 1)
            up(TILES - 1, TILES - 1)
            down(TILES - 2, TILES - 2)
            pe.wait_ge(y_set[(TILES - 3) % RU], (TILES - 3) // RU + 1)
            down(TILES - 1, TILES - 1)


_NAMES = [
    "x", "ctx_1024",
    *("L0_xattn_" + n for n in (
        "qkv_w", "qkv_b", "sa_out_w", "sa_out_b", "in_proj_w", "in_proj_b", "mha_out_w", "mha_out_b",
        "lin1_w", "lin1_b", "lin2_w", "lin2_b", "ln1_g", "ln1_b", "ln2_g", "ln2_b", "ln3_g", "ln3_b")),
    *("L0_ffn_" + n for n in (
        "router_w", "router_b", "w1", "b1", "gate", "w2", "b2", "sw1", "sb1", "sgate", "sw2", "sb2",
        "shared_weight", "ln_g", "ln_b")),
]


def kernel(**inputs):
    import numpy as np
    import concourse.bacc as bacc
    from concourse.bass_utils import run_bass_kernel_spmd

    nc = bacc.Bacc("TRN2", target_bir_lowering=False, num_devices=1)
    arrays, args = {}, []
    for name in _NAMES:
        a = np.ascontiguousarray(inputs[name])
        if a.ndim == 0:
            a = a.reshape(1)
        arrays[f"in_{name}"] = a
        args.append(nc.dram_tensor(f"in_{name}", a.shape, mybir.dt.from_np(a.dtype), kind="ExternalInput").ap())
    shape = inputs["x"].shape
    args.append(nc.dram_tensor("out_x", shape, F32, kind="ExternalOutput").ap())
    xattn_moe_kernel(nc, *args)
    r = run_bass_kernel_spmd(nc, [arrays], core_ids=[0])
    return r.results[0]["out_x"]
```

```python
from contextlib import ExitStack

import concourse.bass as bass
from concourse import mybir

ALU = mybir.AluOpType
ACT = mybir.ActivationFunctionType
AX = mybir.AxisListType
F32 = mybir.dt.float32
F32R = mybir.dt.float32r
U32 = mybir.dt.uint32
I32 = mybir.dt.int32

P = 128
EPS = 1e-5


class Chain:

    def __init__(self, eng, sem):
        self.eng, self.sem, self.n = eng, sem, 0

    def step(self, instruction):
        instruction.then_inc(self.sem, 1)
        self.n += 1

    def settle(self):
        self.eng.wait_ge(self.sem, self.n)

    def link(self, instruction):
        self.step(instruction)
        self.settle()


def xattn_moe_kernel(
    nc, x, ctx_1024, qkv_w, qkv_b, sa_out_w, sa_out_b, in_proj_w, in_proj_b, mha_out_w, mha_out_b,
    lin1_w, lin1_b, lin2_w, lin2_b, ln1_g, ln1_b, ln2_g, ln2_b, ln3_g, ln3_b,
    router_w, router_b, w1, b1, gate, w2, b2, sw1, sb1, sgate, sw2, sb2, shared_weight, ln_g, ln_b,
    out,
):
    B, S, D = x.shape
    M = ctx_1024.shape[1]
    E, _, F = w1.shape
    FF = lin1_w.shape[0]
    FS = sw1.shape[1]
    H = 8
    DH = D // H
    TB = S // P
    NT = B * TB
    MT = M - P
    HG = 4
    Q = P // HG
    MP = P + Q
    FC = F // P
    FFC = FF // P
    FSC = FS // P
    WE = F + FC
    K2 = 2
    TOKENS = NT * P
    REG = TOKENS + P
    TILES = 40
    ROW = 132
    W_COL, I_COL = D, D + 1
    U = 2
    TU = TB // 2
    UL = TU * P
    G = NT // TU
    NS = 4
    RU = 6
    WB = 3
    assert D == P and S % P == 0 and B % U == 0 and H * DH == P
    assert RU % WB == 0 and RU % 2 == 0
    assert G == E and TB * K2 == 8
    assert TILES >= K2 * NT + E - 1 and DH < Q and MT <= Q

    C_B2 = 0
    C_SB2 = C_B2 + E * D
    C_BR = C_SB2 + D
    C_L2 = C_BR + E
    C_MO = C_L2 + D
    C_QK = C_MO + D
    C_END = C_QK + 2 * D

    IDLE = TILES - K2 * NT
    assert NT == IDLE + E
    rows = nc.dram_tensor("dispatched_rows", [E * REG + IDLE * P, ROW], F32).ap()
    pads = nc.dram_tensor("padding_rows", [E * P, ROW], F32).ap()
    results = nc.dram_tensor("expert_results", [K2 * TOKENS + NT * P, D], F32).ap()

    with ExitStack() as ctx:
        def sb(name, shape, dt=F32):
            return ctx.enter_context(nc.sbuf_tensor(name, shape, dt))

        def sem(name):
            return ctx.enter_context(nc.semaphore(name))

        def sides(name, n=U):
            return [sem(f"{name}{u}") for u in range(n)]

        def pair(name, shape, dt=F32):
            return [sb(f"{name}{u}", shape, dt) for u in range(U)]

        def four(name, shape, dt=F32):
            return [sb(f"{name}{u}", shape, dt) for u in range(NS)]

        SL = TB * P
        GS = HG + 2
        space = sb("space", [P, NS * GS * UL])
        pT = [space[:, u * GS * UL:(u + 1) * GS * UL].rearrange("p (g n) -> p g n", n=UL) for u in range(NS)]
        kb = pair("kb", [P, H * MP])
        kbr = pair("kbr", [P, H, M], F32R)

        class Space:

            def __init__(self, ap):
                self.ap, self.at = ap, 0

            def cut(self, n, p=P):
                self.at += n
                assert self.at <= self.ap.shape[1]
                return self.ap[0:p, self.at - n:self.at]

        half = NS * GS * UL // 2
        flat = [space[:, u * half:(u + 1) * half] for u in range(U)]

        early = Space(flat[0])
        wqkv = early.cut(3 * D).rearrange("p (k c) -> p k c", k=3)
        wsao = early.cut(D)
        winp = early.cut(3 * D).rearrange("p (k c) -> p k c", k=3)
        wmo = early.cut(D)
        wl1 = early.cut(FFC * D).rearrange("p (k c) -> p k c", k=FFC)
        wl2 = early.cut(FF)
        early = Space(flat[1])
        ctx_main = early.cut(B * D).rearrange("p (b c) -> p b c", b=B)
        ctx_tail = early.cut(B * D, MT).rearrange("p (b c) -> p b c", b=B)
        sel0 = early.cut(H * P).rearrange("p (h c) -> p h c", h=H)

        w1g = sb("w1g", [P, E, WE])
        wbuf = sb("wbuf", [P, WB, WE])
        w2s = sb("w2s", [P, E * F])
        row32 = w2s[0:2, 0:C_END]
        GH = 2
        gate_bc = sb("gate_bc", [P, GH * F])
        sw1s = sb("sw1s", [P, FS])
        sw2s = sb("sw2s", [P, FSC, D])
        wr = sb("wr", [P, E])
        T_SAO, T_Q, T_K, T_V, T_MO, T_L1, T_L2 = 0, 1, 2, 3, 4, 5, 5 + FFC
        NTR = T_L2 + FFC
        wt = sb("wt", [P, NTR, D])
        mm = sb("mm", [P, 2 * D])
        cT = sb("cT", [P, B, M])
        cTr = sb("cTr", [P, B, HG, Q])
        kT = sb("kT", [P, B, MP])
        vmain = sb("vmain", [P, B, H * Q])
        vtail = sb("vtail", [P, B, H * Q])
        R_IN, R_L1 = 3, 6
        R_SG = R_L1 + FFC
        R_SB = R_SG + FSC
        R_B1 = R_SB + FSC
        R_G = R_B1 + E * FC
        NR = R_G + E * FC
        vrow = sb("vrow", [NR, P])
        vcol = sb("vcol", [P, NR])
        col_bq2, col_bk2 = vcol[:, R_IN:R_IN + 1], vcol[:, R_IN + 1:R_IN + 2]
        col_l1b, col_sg = vcol[:, R_L1:R_SG], vcol[:, R_SG:R_SB]
        col_sbg = sb("col_sbg", [P, FSC])
        col_bqs = sb("col_bqs", [P, 1])
        col_sw = sb("col_sw", [P, 1])
        sig = sb("sig", [P, 1])
        qkvb2 = sb("qkvb2", [P, 3, 2])
        BC = ("sab", "vb2", "g1", "b1", "g2", "b2", "g3", "b3", "g4", "b4")
        bc = {name: sb("bc_" + name, [P, D]) for name in BC}
        mrow = sb("mrow", [2, 1])
        brow = sb("brow", [P, C_END], F32R)
        ident = sb("ident", [P, P])
        before = sb("before", [P, P])
        onef = sb("onef", [P, P])
        one2 = sb("one2", [P, P], F32R)
        mask8 = sb("mask8", [P, H])
        mask32 = sb("mask32", [P, H])
        sel = sb("sel", [P, H, P], F32R)
        selt = sb("selt", [P, H, Q], F32R)
        nhalf = sb("nhalf", [P, TB])
        down8 = sb("down8", [P, E])
        upto8 = sb("upto8", [P, E])
        ebase = sb("ebase", [P, E])
        thr = sb("thr", [P, NT])
        tile_c = sb("tile_c", [P, TILES])
        smask = sb("smask", [P, E, TB])
        base = sb("base", [P, E])
        x_all = sb("x_all", [P, NT, D])
        nT_all = sb("nT_all", [P, NT, D])
        row_buf = [sb(f"row_buf{k}", [P, NT, ROW]) for k in range(K2)]
        lg_all = sb("lg_all", [P, NT, E])
        st = four("st", [P, TU, 6])
        mv = four("mv", [P, TU, 2])
        ve = four("ve", [P, TU])
        rstd = four("rstd", [P, TU])
        nmr = four("nmr", [P, TU])
        h0 = four("h0_", [P, TU, D])
        h0b = four("h0b", [P, TU, D])
        y = four("y", [P, TU, D])
        actT = four("actT", [P, UL])
        sdot = four("sdot", [P, TU])
        nsc = four("nsc", [P, TU])
        esc = four("esc", [P, TU])
        rsc = four("rsc", [P, TU])
        psc = four("psc", [P, TU])
        qT = four("qT", [P, UL])
        qTr = four("qTr", [P, UL], F32R)
        vm = pair("vm", [P, H * Q])
        vt = pair("vt", [P, H * Q])
        nmax = four("nmax", [P, TU, H])
        nmT = four("nmT", [P, UL], F32R)
        rden = four("rden", [P, TU, H])
        x1, x2 = h0, h0b
        assert 2 * HG == H
        flat3 = lambda ap: ap.rearrange("p t d -> p (t d)")
        av = [[flat3(h0b[u][:, :, :]), flat3(y[u][:, :, :])] for u in range(NS)]
        junk = four("junk", [P, D])
        xt = [kb[0][:, k * ROW:(k + 1) * ROW] for k in range(RU)]
        yt = [h0b[k % NS][:, k // NS, :] for k in range(RU)]
        hs = [flat[u][:, 0:FSC * SL].rearrange("p (c n) -> p c n", c=FSC) for u in range(U)]
        hT = [flat[u][:, 0:SL] for u in range(U)]
        xtT = [actT[u][:, 0:P] for u in range(U)]
        route = Space(sb("route", [P, 10 * TB * E + 9 * TB]))
        lgm, pr, oh0, oh1, key, picks, tot, incl, slot, tmp = [route.cut(TB * E) for _ in range(10)]
        m0, ssum, rs4, kmax, ws, wrs, wk0, wk1, sl4 = [route.cut(TB) for _ in range(9)]
        late = Space(flat[1][:, FSC * SL:])
        cmp = late.cut(NT * E)
        tcmp = late.cut(TILES * E).rearrange("p (j e) -> p j e", j=TILES)
        teid, toff, tdum = [late.cut(TILES) for _ in range(3)]
        cnt, ntl, tend, tval = [late.cut(E) for _ in range(4)]
        oh = [oh0, oh1]
        wk = [wk0, wk1]
        te = lambda ap: ap.rearrange("p (t e) -> p t e", e=E)
        et = lambda ap: ap.rearrange("p (e t) -> p e t", t=TB)
        idx = sb("idx", [P, K2, NT], U32)
        meta = sb("meta", [P, 2, TILES], I32)
        cnti = sb("cnti", [P, E], I32)
        res = [flat[k][:, SL:SL + NT * D].rearrange("p (t d) -> p t d", d=D) for k in range(K2)]

        psum = ctx.enter_context(nc.psum_tensor("psum", [P, 2 * NS, 512], F32))
        bank = [[psum[:, 4 * u + k, :] for k in range(4)] for u in range(U)]
        duo = [[psum[:, 2 * u + k, :] for k in range(2)] for u in range(NS)]

        in_x0, in_x, in_w, in_l = sem("in_x0"), sem("in_x"), sem("in_w"), sem("in_l")
        in_ctx, in_vec, in_rest, in_late = sem("in_ctx"), sem("in_vec"), sem("in_rest"), sem("in_late")
        in_row, vc_ps = sem("in_row"), sem("vc_ps")
        in_w1, in_w2, in_gate, gate_used = sem("in_w1"), sem("in_w2"), sem("in_gate"), sem("gate_used")
        ident_set, zeros_set, consts_set, pool_link = sem("ident_set"), sem("zeros_set"), sem("consts_set"), sem("pool_link")
        wt_ps, wt_sb, wt_act, cT_ps, cT_sb = sem("wt_ps"), sem("wt_sb"), sem("wt_act"), sem("cT_ps"), sem("cT_sb")
        k_ps, k_sb, v_ps, v_sb = sem("k_ps"), sem("k_sb"), sem("v_ps"), sem("v_sb")
        qb_set, mm_pr, mm_sb, brow_set = sem("qb_set"), sem("mm_pr"), sem("mm_sb"), sem("brow_set")
        sel_set, act_prep, unread = sem("sel_set"), sem("act_prep"), sem("unread")
        dve_link, dve_comb = sem("dve_link"), sem("dve_comb")
        ln_var, ln_rstd = sides("ln_var", 5), sides("ln_rstd", 5)
        tr_ps, tr_sb = sides("tr_ps", 5), sides("tr_sb", 5)
        h0_set, h0b_set, x0b_set, mm_ps = sem("h0_set"), sem("h0b_set"), sem("x0b_set"), sem("mm_ps")
        sc_set, esc_set, x1_set, q_ps = sem("sc_set"), sem("esc_set"), sem("x1_set"), sem("q_ps")
        q_sb, kbr_set, kb_set = sem("q_sb"), sem("kbr_set"), sem("kb_set")
        nm_ps, nm_sb, nmr0_set, nmr4_set = sem("nm_ps"), sem("nm_sb"), sem("nmr0_set"), sem("nmr4_set")
        s_ps, max_set, av_ps, av_sb = sides("s_ps"), sides("max_set"), sides("av_ps"), sides("av_sb")
        st_ps, e_set = sides("st_ps", 5), sides("e_set", 5)
        avT_ps, ca_set, y2_ps, x2_set = sem("avT_ps"), sem("ca_set"), sem("y2_ps"), sem("x2_set")
        l1_ps, l1_sb, y3_ps, n_set = sem("l1_ps"), sem("l1_sb"), sem("y3_ps"), sem("n_set")
        row_set, nT_set, lg_ps, lg_set = sem("row_set"), sem("nT_set"), sem("lg_ps"), sem("lg_set")
        max0_set, ex_set, picks_set, rank_ps = sem("max0_set"), sem("ex_set"), sem("picks_set"), sem("rank_ps")
        dve_rout, slots_set, meta_set = sem("dve_rout"), sem("slots_set"), sem("meta_set")
        rows_out, pads_out, pads_set = sem("rows_out"), sem("pads_out"), sem("pads_set")
        hs_ps, hs_set, sh_ps, sh_set = sides("hs_ps"), sides("hs_set"), sides("sh_ps"), sides("sh_set")
        xt_in, y_set, y_out = ([sem(f"{s}{k}") for k in range(RU)] for s in ("xt_in", "y_set", "y_out"))
        xt_ps, xt_sb, w_sb, up_ps = sem("xt_ps"), sem("xt_sb"), sem("w_sb"), sem("up_ps")
        h_set, dn_ps = sem("h_set"), sem("dn_ps")
        res_in, sum_set = sides("res_in", B), sem("sum_set")
        xb_set, fin_set, fin_out, cv_var, cv_rstd = (sem(s) for s in ("xb_set", "fin_set", "fin_out", "cv_var", "cv_rstd"))

        TURNS = B // U
        OFF = 17
        PE_AT = dict(prep1=2, prep2=6, h0T=6, mm=10, x1T=20, q=21, s0=22, s1=23, nm=27, n01=30, n2=32, av0=33, n3=33, n4=33, av1=38, avT=39, caT=40, y2=41, x2T=49, l1=50, l2=55, nT=65, router=67, rank=70)
        ACT_AT = dict(prep=12, sig=16, h0=9, h0T=9, esc=13, x1T=23, q=25, nm=27, e0=31, e1=33, e2=35, av0=40, e3=40, e4=40, av1=41, caT=43, x2T=51, relu=56, n=62, nT=66, pr=71)
        DVE_AT = dict(ln0=2, h0=5, prep1=7, prep2=9, prep3=20, dot=10, y1=14, x1=15, m0=24, m1=24, ca=41, y2=43, x2=45, y3=55, xr=59, n=61, lg=66, r0=66, r1=67, r2=71)
        POOL_AT = dict(late=23, ln0=4, h0b=9, kbr=13, ln1=13, kb=15, vv=24, x0b=43, ln2=44, ln3=57, ln4=61, row=72, fold=34, sc0=73, sc1=77, sc2=77, sc3=81, sc4=84, sc5=87, sc6=90, sc7=91)
        SLOTS = (G - 1) * OFF + max(max(at.values()) for at in (PE_AT, ACT_AT, DVE_AT, POOL_AT)) + 1

        def pipeline(at):
            for slot in range(SLOTS):
                for g in range(G):
                    for name, when in at.items():
                        if slot - g * OFF == when:
                            yield name, g, g % NS

        ETURNS = TILES // RU
        assert TILES - ETURNS * RU >= 2
        N_ROW, N_VEC, N_REST = 7, 4, 12
        x_v = x.rearrange("b (t p) d -> p (b t) d", p=P)
        out_v = out.rearrange("b (t p) d -> p (b t) d", p=P)
        res_v = results.rearrange("(t p) d -> p t d", p=P)

        def column(v):
            return v.rearrange("(c p) -> p c", p=P)

        def apart(eng):
            eng.sem_inc(unread, 1)

        block = ctx.enter_context(nc.Block())

        @block.sync
        def _(sp):
            def load_x(b, done):
                sp.dma_start(x_all[:, b * TB:(b + 1) * TB, :], x_v[:, b * TB:(b + 1) * TB, :]).then_inc(done, 16)

            load_x(0, in_x0)
            sp.dma_start(wqkv, qkv_w.rearrange("(k p) c -> p k c", p=P)).then_inc(in_w, 16)
            sp.dma_start(wsao, sa_out_w).then_inc(in_w, 16)
            sp.dma_start(winp, in_proj_w.rearrange("(k p) c -> p k c", p=P)).then_inc(in_w, 16)
            sp.dma_start(ctx_main, ctx_1024[:, 0:P, :].rearrange("b m c -> m b c")).then_inc(in_ctx, 16)
            sp.dma_start(ctx_tail, ctx_1024[:, P:M, :].rearrange("b m c -> m b c")).then_inc(in_ctx, 16)
            sp.dma_start(wmo, mha_out_w).then_inc(in_l, 16)
            sp.dma_start(wl1, lin1_w.rearrange("(k p) c -> p k c", p=P)).then_inc(in_l, 16)
            sp.dma_start(wl2, lin2_w).then_inc(in_l, 16)
            load_x(1, in_x)
            for at, vec in ((C_B2, b2.rearrange("e d -> (e d)")), (C_SB2, sb2), (C_BR, router_b), (C_L2, lin2_b),
                            (C_MO, mha_out_b)):
                sp.dma_start(row32[:, at:at + vec.shape[0]], vec.partition_broadcast(2)).then_inc(in_rest, 16)
            for name, vec in dict(g2=ln2_g, b2=ln2_b, g3=ln3_g, b3=ln3_b, g4=ln_g, b4=ln_b).items():
                sp.dma_start(bc[name][:, :], vec.partition_broadcast(P)).then_inc(in_rest, 16)
            sp.dma_start(col_sw[:, :], shared_weight.partition_broadcast(P)).then_inc(in_rest, 16)
            for b in range(2, B):
                load_x(b, in_x)
            sp.dma_start(sw1s[:, :], sw1).then_inc(in_late, 16)
            sp.dma_start(sw2s[:, :, :], sw2.rearrange("(c p) d -> p c d", p=P)).then_inc(in_late, 16)
            sp.dma_start(wr[:, :], router_w).then_inc(in_late, 16)
            sp.wait_ge(pads_set, 1)
            sp.dma_start(rows[E * REG:, :].rearrange("(t p) r -> p t r", p=P),
                         row_buf[1][:, E:NT, :]).then_inc(pads_out, 16)
            sp.dma_start(pads.rearrange("(t p) r -> p t r", p=P), row_buf[1][:, 0:E, :]).then_inc(pads_out, 16)
            for e in range(E):
                sp.dma_start(w1g[:, e, 0:F], w1[e]).then_inc(in_w1, 16)
            for g in range(E // GH):
                if g:
                    sp.wait_ge(gate_used, g)
                sp.dma_start(gate_bc[:, :], gate[g * GH:(g + 1) * GH, :].rearrange("e f -> (e f)")
                             .partition_broadcast(P)).then_inc(in_gate, 16)
            sp.wait_ge(brow_set, 2)
            for e in range(E):
                sp.dma_start(w2s[:, e * F:(e + 1) * F].rearrange("p (c d) -> p c d", d=D),
                             w2[e].rearrange("(c p) d -> p c d", p=P)).then_inc(in_w2, 16)
            sp.wait_ge(meta_set, 1)
            for e in range(E):
                n = sp.value_load(cnti[0:1, e:e + 1], min_val=0, max_val=TOKENS)
                sp.dma_start(rows[bass.ds(n + e * REG, P), :], pads[e * P:(e + 1) * P, :]).then_inc(pads_out, 16)
            sp.wait_ge(pads_out, 16 * (E + 2))
            sp.wait_ge(rows_out, 16 * K2 * NT)

            def load_tile(j, k):
                at = sp.value_load(meta[0:1, 1, bass.ds(j, 1)], min_val=0, max_val=E * REG + (IDLE - 1) * P)
                sp.dma_start(xt[k], rows[bass.ds(at, P), :]).then_inc(xt_in[k], 16)

            for k in range(RU):
                load_tile(k, k)
            with sp.Fori(1, ETURNS) as it:
                for k in range(RU):
                    sp.wait_ge(y_out[k], it * 16)
                    load_tile(it * RU + k, k)
            for k in range(TILES - ETURNS * RU):
                sp.wait_ge(y_out[k], 16 * ETURNS)
                load_tile(ETURNS * RU + k, k)
            for k in range(RU):
                sp.wait_ge(y_out[k], 16 * len(range(k, TILES, RU)))

            for b in range(B):
                for k in range(K2):
                    sp.dma_start(res[k][:, b * TB:(b + 1) * TB, :],
                                 res_v[:, b * TB + k * NT:(b + 1) * TB + k * NT, :]).then_inc(res_in[b], 16)
            for g in range(G):
                sp.wait_ge(fin_set, g + 1)
                sp.dma_start(out_v[:, g * TU:(g + 1) * TU, :], res[0][:, g * TU:(g + 1) * TU, :]).then_inc(fin_out, 16)
            sp.wait_ge(fin_out, 16 * G)

        @block.gpsimd
        def _(pool):
            g = nc.gpsimd
            link = Chain(pool, pool_link)
            link.step(g.memset(ident[:, :], 0.0))
            link.step(g.memset(nhalf[:, :], -0.5))
            link.step(g.memset(mrow[:, :], 0.0))
            link.settle()
            g.affine_select(out=ident[:, :], in_=ident[:, :], compare_op=ALU.not_equal, fill=1.0,
                            base=0, pattern=[[-1, P]], channel_multiplier=1).then_inc(ident_set, 1)
            g.affine_select(out=mrow[:, :], in_=mrow[:, :], compare_op=ALU.not_equal, fill=-1.0,
                            base=-1, pattern=[[0, 1]], channel_multiplier=1)
            g.memset(brow[:, :].bitcast(F32), 0.0)
            g.memset(kT[:, :, :], 0.0)
            g.memset(cTr[:, :, :, :], 0.0)
            link.step(g.memset(vmain[:, :, :], 0.0))
            g.memset(vtail[:, :, :], 0.0)
            link.settle()
            g.memset(vmain[:, :, :].rearrange("p b (h q) -> p (b h) q", q=Q)[:, :, DH:DH + 1], 1.0)\
             .then_inc(zeros_set, 1)

            def constants():
                link.step(g.memset(before[:, :], 1.0))
                link.step(g.memset(sel0, 0.0))
                link.step(g.memset(mask8[:, :], 1.0))
                link.step(g.memset(mask32[:, :], 1.0))
                link.step(g.memset(smask[:, :, :], 1.0))
                link.step(g.memset(onef[:, :], 1.0))
                link.settle()
                link.step(g.affine_select(out=mask8[:, :], in_=mask8[:, :], compare_op=ALU.is_ge, fill=0.0,
                                          base=0, pattern=[[-DH, H]], channel_multiplier=1))
                m32 = mask32[:, :].rearrange("p (g h) -> p g h", g=2)
                link.step(g.affine_select(out=m32, in_=m32, compare_op=ALU.is_ge, fill=0.0,
                                          base=0, pattern=[[0, 2], [-Q, HG]], channel_multiplier=1))
                link.settle()
                link.step(g.affine_select(out=mask8[:, :], in_=mask8[:, :], compare_op=ALU.is_ge, fill=0.0,
                                          base=DH - 1, pattern=[[DH, H]], channel_multiplier=-1))
                link.step(g.affine_select(out=m32, in_=m32, compare_op=ALU.is_ge, fill=0.0,
                                          base=MT - 1, pattern=[[0, 2], [Q, HG]], channel_multiplier=-1))
                link.step(g.affine_select(out=before[:, :], in_=before[:, :], compare_op=ALU.is_gt, fill=0.0,
                                          base=0, pattern=[[1, P]], channel_multiplier=-1))
                link.step(g.affine_select(out=sel0, in_=sel0, compare_op=ALU.not_equal, fill=1.0,
                                          base=0, pattern=[[-1, H], [0, P]], channel_multiplier=1))
                link.step(g.memset(smask[:, :, 0:1], 0.0))
                ex = dict(allow_small_or_imprecise_dtypes=True)
                link.step(g.iota(down8[:, :], pattern=[[-1, E]], base=E, channel_multiplier=0, **ex))
                link.step(g.iota(upto8[:, :], pattern=[[1, E]], base=0, channel_multiplier=0, **ex))
                link.step(g.iota(ebase[:, :], pattern=[[REG, E]], base=0, channel_multiplier=0, **ex))
                link.step(g.iota(thr[:, :], pattern=[[P, NT]], base=0, channel_multiplier=0, **ex))
                link.step(g.iota(tile_c[:, :], pattern=[[1, TILES]], base=0, channel_multiplier=0, **ex))
                link.settle()
                g.memset(row_buf[0][:, :, I_COL + 1:ROW], 0.0).then_inc(consts_set, 1)
                link.link(g.memset(row_buf[1][:, :, :], 0.0))
                g.iota(row_buf[1][:, :, I_COL:I_COL + 1].bitcast(I32), pattern=[[P, NT]],
                       base=K2 * TOKENS, channel_multiplier=1).then_inc(pads_set, 1)

            def late_constants():
                pool.wait_ge(pads_out, 16 * 2)
                for k in range(K2):
                    link.step(g.iota(row_buf[k][:, :, I_COL:I_COL + 1].bitcast(I32), pattern=[[P, NT]],
                                     base=k * TOKENS, channel_multiplier=1))
                pool.wait_ge(v_sb, 1)
                link.link(g.memset(vtail[:, :, :].rearrange("p b (h q) -> p (b h) q", q=Q)[:, :, DH:DH + 1], 1.0))
                for b in range(B):
                    tail = vtail[:, b, :].rearrange("p (h q) -> p h q", q=Q)
                    link.step(g.tensor_tensor(tail, tail, mask32[:, :].unsqueeze(2).to_broadcast([P, H, Q]),
                                              ALU.mult))
                link.settle()

            def rstd_of(u, var_sem, rstd_sem, n):
                pool.wait_ge(var_sem, n)
                g.tensor_tensor(rstd[u][:, :], ve[u][:, :], nhalf[:, 0:TU], ALU.pow).then_inc(rstd_sem, 1)

            def wide(name):
                return bc[name][:, :].unsqueeze(1).to_broadcast([P, TU, D])

            for step, n, u in pipeline(POOL_AT):
                b, k = n // 2, (n // 2) % U
                last = n - 2 * U + 1
                kv = kT[:, b, :]
                if step in ("ln0", "ln1", "ln2", "ln3", "ln4"):
                    rstd_of(u, ln_var[int(step[2])], ln_rstd[int(step[2])], n + 1)
                    if step == "ln0" and n == 0:
                        constants()
                elif step == "late" and n == 0:
                    late_constants()
                elif step == "kbr" and n % 2 == 0:
                    if b == 0:
                        pool.wait_ge(k_sb, 2)
                    if b >= U:
                        pool.wait_ge(s_ps[1], (last + 1) * 4)
                    g.tensor_tensor(kbr[k][:, :, :], kv[:, 0:M].unsqueeze(1).to_broadcast([P, H, M]),
                                    mask8[:, :].unsqueeze(2).to_broadcast([P, H, M]), ALU.mult)\
                     .then_inc(kbr_set, 1)
                elif step == "kb" and n % 2 == 0:
                    if b >= U:
                        pool.wait_ge(st_ps[4], last + 1)
                    for at, m in ((0, P), (P, Q)):
                        g.tensor_tensor(kb[k][:, H * at:H * (at + m)].rearrange("p (h m) -> p h m", h=H),
                                        kv[:, at:at + m].unsqueeze(1).to_broadcast([P, H, m]),
                                        mask8[:, :].unsqueeze(2).to_broadcast([P, H, m]), ALU.mult)\
                         .then_inc(kb_set, 1)
                elif step == "vv" and n % 2 == 0:
                    if b >= U:
                        pool.wait_ge(av_ps[1], last + 1)
                    g.tensor_copy(vm[k][:, :], vmain[:, b, :]).then_inc(kb_set, 1)
                    g.tensor_copy(vt[k][:, :], vtail[:, b, :]).then_inc(kb_set, 1)
                elif step == "h0b":
                    if n == 0:
                        pool.wait_ge(in_vec, 16 * N_VEC)
                    pool.wait_ge(h0_set, n + 1)
                    g.tensor_tensor(h0b[u][:, :, :], h0[u][:, :, :], wide("sab"), ALU.add).then_inc(h0b_set, 1)
                elif step == "x0b":
                    if n == 0:
                        pool.wait_ge(in_rest, 16 * N_REST)
                    xs = x_all[:, n * TU:(n + 1) * TU, :]
                    g.tensor_tensor(xs, xs, wide("b3"), ALU.add).then_inc(x0b_set, 1)
                elif step == "fold":
                    pool.wait_ge(in_w1, 16 * E)
                    pool.wait_ge(in_gate, 16 * (n // GH + 1))
                    ins = g.tensor_tensor(w1g[:, n, 0:F], w1g[:, n, 0:F],
                                          gate_bc[:, (n % GH) * F:(n % GH + 1) * F], ALU.mult)
                    if n % GH == GH - 1:
                        ins.then_inc(gate_used, 1)
                elif step[0:2] == "sc" and n % 2:
                    t, c = b * TB + int(step[2]) // K2, int(step[2]) % K2
                    if step == "sc0":
                        pool.wait_ge(slots_set, b + 1)
                        pool.wait_ge(row_set, n + 1)
                    pool.indirect_dma_start(rows[:, :], bass.IndirectOffsetOnAxis(idx[:, c, t:t + 1], 0),
                                            row_buf[c][:, t, :], None).then_inc(rows_out, 16)
                elif step == "row":
                    pool.wait_ge(n_set, n + 1)
                    g.tensor_copy(row_buf[1][:, n * TU:(n + 1) * TU, 0:D], row_buf[0][:, n * TU:(n + 1) * TU, 0:D])\
                     .then_inc(row_set, 1)

            for b in range(B):
                xs = x_all[:, b * TB:(b + 1) * TB, :]
                g.tensor_tensor(xs, xs, bc["b4"][:, :].unsqueeze(1).to_broadcast([P, TB, D]), ALU.add)\
                 .then_inc(xb_set, 1)

            def store_tile(turn, k):
                pool.wait_ge(y_set[k], turn + 1)
                apart(pool)
                pool.indirect_dma_start(
                    results[:, :], bass.IndirectOffsetOnAxis(xt[k][:, I_COL:I_COL + 1].bitcast(U32), 0),
                    yt[k], None).then_inc(y_out[k], 16)

            with pool.Fori(0, ETURNS) as it:
                for k in range(RU):
                    store_tile(it, k)
            for k in range(TILES - ETURNS * RU):
                store_tile(ETURNS, k)
            def sum_results(n):
                if n % (TB // TU) == 0:
                    pool.wait_ge(res_in[n // (TB // TU)], 16 * K2)
                both = [res[k][:, n * TU:(n + 1) * TU, :] for k in range(K2)]
                g.tensor_tensor(both[0], both[0], both[1], ALU.add).then_inc(sum_set, 1)

            sum_results(0)
            for n in range(G):
                if n + 1 < G:
                    sum_results(n + 1)
                rstd_of(n % NS, cv_var, cv_rstd, n + 1)

        @block.scalar
        def _(act):
            a = nc.scalar
            rows_of = lambda vec: vec.rearrange("(c p) -> c p", p=P)
            for at, src in ((0, rows_of(qkv_b)), (R_IN, rows_of(in_proj_b)), (R_L1, rows_of(lin1_b)),
                            (R_SG, rows_of(sgate)), (R_SB, rows_of(sb1)),
                            (R_B1, b1.rearrange("e (c p) -> (e c) p", p=P)),
                            (R_G, gate.rearrange("e (c p) -> (e c) p", p=P))):
                act.dma_start(vrow[at:at + src.shape[0], :], src).then_inc(in_row, 16)
            for name, vec in (("vb2", in_proj_b[2 * D:3 * D]), ("sab", sa_out_b), ("g1", ln1_g), ("b1", ln1_b)):
                act.dma_start(bc[name][:, :], vec.partition_broadcast(P)).then_inc(in_vec, 16)

            def prepare():
                act.wait_ge(qb_set, 1)
                act.wait_ge(zeros_set, 1)
                for k in range(2):
                    act.wait_ge(k_ps, k + 1)
                    a.activation(kT[:, 2 * k:2 * k + 2, 0:M],
                                 bank[1][k][:, 0:2 * M].rearrange("p (b m) -> p b m", b=2),
                                 ACT.Identity, bias=col_bk2[:, :]).then_inc(k_sb, 1)
                for k in range(1, 4):
                    act.wait_ge(wt_ps, k + 1)
                    n = min(4, NTR - 4 * k)
                    a.copy(wt[:, 4 * k:4 * k + n, :],
                           bank[0][k][:, 0:n * P].rearrange("p (k c) -> p k c", c=P)).then_inc(wt_act, 1)

            def sigmoid_part():
                act.wait_ge(in_rest, 16 * N_REST)
                a.activation(sig[:, :], col_sw[:, :], ACT.Exp, scale=-1.0).then_inc(act_prep, 1)

            def evacuate(g, nth, src, dst):
                act.wait_ge(tr_ps[nth], g + 1)
                a.copy(dst, src).then_inc(tr_sb[nth], 1)

            def normed(u, src, dst, done):
                for t in range(TU):
                    ins = a.activation(dst(t), src(t), ACT.Identity, bias=nmr[u][:, t:t + 1],
                                       scale=rstd[u][:, t:t + 1])
                ins.then_inc(done, 1)

            for step, g, u in pipeline(ACT_AT):
                A, Bk = duo[u]
                if step == "prep":
                    if g == 0:
                        prepare()
                elif step == "sig":
                    if g == 0:
                        sigmoid_part()
                elif step in ("h0T", "x1T", "caT", "x2T"):
                    evacuate(g, ("h0T", "x1T", "caT", "x2T").index(step), A[:, 0:UL], actT[u][:, :])
                elif step == "esc":
                    act.wait_ge(sc_set, g + 1)
                    for t in range(TU):
                        ins = a.activation(esc[u][:, t:t + 1], sdot[u][:, t:t + 1], ACT.Exp,
                                           bias=nsc[u][:, t:t + 1], scale=float(D) ** 0.5)
                    ins.then_inc(esc_set, 1)
                elif step == "h0":
                    act.wait_ge(nmr0_set, g + 1)
                    normed(u, lambda t: x_all[:, g * TU + t, :], lambda t: h0[u][:, t, :], h0_set)
                elif step == "q":
                    act.wait_ge(q_ps, g + 1)
                    for ap in (qT[u], qTr[u]):
                        ins = a.activation(ap[:, :], A[:, UL:2 * UL], ACT.Identity, bias=col_bqs[:, :],
                                           scale=float(DH) ** -0.5)
                    ins.then_inc(q_sb, 1)
                elif step == "nm":
                    act.wait_ge(nm_ps, g + 1)
                    a.copy(nmT[u][0:H, :], A[0:H, 0:UL]).then_inc(nm_sb, 1)
                elif step == "n":
                    act.wait_ge(nmr4_set, g + 1)
                    normed(u, lambda t: x_all[:, g * TU + t, :], lambda t: row_buf[0][:, g * TU + t, 0:D], n_set)
                elif step in ("e0", "e1", "e2", "e3", "e4"):
                    n = int(step[1])
                    slot = (0, 2, 4, 0, 2)[n]
                    act.wait_ge(st_ps[n], g + 1)
                    a.activation(pT[u][:, slot:slot + 2, :].rearrange("p g n -> p (g n)"),
                                 (A, Bk, A, A, Bk)[n], ACT.Exp).then_inc(e_set[n], 1)
                elif step in ("av0", "av1"):
                    gr = int(step[2])
                    act.wait_ge(av_ps[gr], g + 1)
                    a.copy(av[u][gr], (Bk, A)[gr][:, 0:UL]).then_inc(av_sb[gr], 1)
                elif step == "relu":
                    for c in range(FFC):
                        if c % 2 == 0:
                            act.wait_ge(l1_ps, g * (FFC // 2) + c // 2 + 1)
                        a.activation(pT[u][:, c, :], (A, Bk)[c // 2][:, c % 2 * UL:(c % 2 + 1) * UL], ACT.Relu,
                                     bias=col_l1b[:, c:c + 1]).then_inc(l1_sb, 1)
                elif step == "pr" and g % 2:
                    act.wait_ge(max0_set, g // 2 + 1)
                    a.activation(pr, lgm, ACT.Exp).then_inc(ex_set, 1)
                elif step == "nT":
                    evacuate(g, 4, Bk[:, 0:UL], actT[u][:, :])
                    a.copy(flat3(nT_all[:, g * TU:(g + 1) * TU, :]), Bk[:, 0:UL]).then_inc(nT_set, 1)
            with act.Fori(0, TURNS) as it:
                for u in range(U):
                    act.wait_ge(hs_ps[u], it + 1)
                    for c in range(FSC):
                        ins = a.activation(hs[u][:, c, :], bank[u][c], ACT.Gelu,
                                           bias=col_sbg[:, c:c + 1], scale=col_sg[:, c:c + 1])
                    ins.then_inc(hs_set[u], 1)
            for u in range(U):
                act.wait_ge(sh_ps[u], TURNS)

            def gelu_tile(j, k):
                for c in range(FC):
                    if c % 2 == 0:
                        act.wait_ge(up_ps, j * (FC // 2) + c // 2 + 1)
                    a.activation(hT[k % 2][:, c * P:(c + 1) * P],
                                 bank[k % 2][1 + c // 2][:, c % 2 * P:(c % 2 + 1) * P], ACT.Gelu,
                                 bias=wbuf[:, k % WB, F + c:F + c + 1]).then_inc(h_set, 1)

            with act.Fori(0, ETURNS) as it:
                for k in range(RU):
                    gelu_tile(it * RU + k, k)
            for k in range(TILES - ETURNS * RU):
                gelu_tile(ETURNS * RU + k, k)

        @block.vector
        def _(dve):
            v = nc.vector
            link = Chain(dve, dve_link)
            link.link(v.memset(one2[:, :].bitcast(F32), 0.0))
            link.step(v.memset(one2[0:2, :].bitcast(F32), 1.0))
            for u in range(NS):
                v.memset(nmT[u][:, :].bitcast(F32), 0.0)

            def high_and_rest(at, n, done):
                cols = slice(at, at + n)
                link.link(v.tensor_copy(brow[0:2, cols], row32[:, cols]))
                v.scalar_tensor_tensor(out=brow[0:2, cols], in0=brow[0:2, cols].bitcast(F32), scalar=mrow[:, :],
                                       in1=row32[:, cols], op0=ALU.mult, op1=ALU.add).then_inc(done, 1)

            def prepare():
                dve.wait_ge(vc_ps, 1)
                link.link(v.tensor_copy(vcol[:, :], bank[1][3][:, 0:NR]))
                v.tensor_scalar(col_bqs[:, :], col_bq2, float(DH) ** -0.5, None, ALU.mult)
                v.tensor_copy(qkvb2[:, :, :], vcol[:, 0:3].unsqueeze(2).to_broadcast([P, 3, 2])).then_inc(qb_set, 1)
                dve.wait_ge(wt_ps, 1)
                v.tensor_copy(wt[:, 0:4, :], bank[0][0].rearrange("p (k c) -> p k c", c=P)).then_inc(wt_sb, 1)
                dve.wait_ge(zeros_set, 1)
                for k in range(2):
                    dve.wait_ge(cT_ps, k + 1)
                    src = bank[1][k][:, 0:2 * M].rearrange("p (b m) -> p b m", b=2)
                    v.tensor_copy(cT[:, 2 * k:2 * k + 2, :], src)
                    v.tensor_copy(cTr[:, 2 * k:2 * k + 2, :, 0:MT],
                                  src[:, :, P:M].unsqueeze(2).to_broadcast([P, 2, HG, MT])).then_inc(cT_sb, 1)
                dve.wait_ge(mm_pr, 1)
                link.link(v.tensor_copy(row32[:, C_QK:C_QK + 2 * D], bank[1][3][0:2, 0:2 * D]))
                high_and_rest(C_QK, 2 * D, brow_set)
                v.tensor_copy(mm[:, :], bank[1][2][:, 0:2 * D]).then_inc(mm_sb, 1)

            def prepare_rest():
                wide = lambda at: vcol[:, at:at + E * FC].rearrange("p (e c) -> p e c", c=FC)
                v.tensor_tensor(w1g[:, :, F:WE], wide(R_B1), wide(R_G), ALU.mult)
                bv = bc["vb2"][:, :].rearrange("p (h d) -> p h d", d=DH)
                dve.wait_ge(in_vec, 16 * N_VEC)
                dve.wait_ge(v_ps, 2)
                for b in range(B):
                    for k, dst in enumerate((vmain, vtail)):
                        ins = v.tensor_tensor(dst[:, b, :].rearrange("p (h q) -> p h q", q=Q)[:, :, 0:DH],
                                              bank[1][3 - k][:, b * D:(b + 1) * D]
                                              .rearrange("p (h d) -> p h d", d=DH), bv, ALU.add)
                ins.then_inc(v_sb, 1)

            def finish_preparing():
                dve.wait_ge(in_rest, 16 * N_REST)
                high_and_rest(0, C_QK, brow_set)
                dve.wait_ge(consts_set, 1)
                v.tensor_copy(sel[:, :, :], sel0)
                link.link(v.tensor_copy(selt[:, :, :], sel0[:, :, 0:Q]))
                v.memset(selt[:, :, MT:Q].bitcast(F32), 0.0).then_inc(sel_set, 1)
                link.step(v.tensor_tensor(col_sbg[:, :], vcol[:, R_SB:R_B1], col_sg, ALU.mult))
                dve.wait_ge(act_prep, 1)
                link.link(v.tensor_scalar(sig[:, :], sig[:, :], 1.0, None, ALU.add))
                link.step(v.reciprocal(sig[:, :], sig[:, :]))
                r.link(v.tensor_copy(base[:, :], ebase[:, :]))

            def stats(u, src, var_sem, link):
                for t in range(TU):
                    link.step(v.bn_stats(st[u][:, t, :], src(t)))
                link.settle()
                for t in range(TU):
                    link.step(v.bn_aggr(mv[u][:, t, :], st[u][:, t, :]))
                link.settle()
                v.tensor_scalar(ve[u][:, :], mv[u][:, :, 1], EPS, None, ALU.add).then_inc(var_sem, 1)

            def shift(u, done):
                v.scalar_tensor_tensor(out=nmr[u][:, :], in0=mv[u][:, :, 0], scalar=-1.0, in1=rstd[u][:, :],
                                       op0=ALU.mult, op1=ALU.mult).then_inc(done, 1)

            def scaled(u, src, gain):
                for t in range(TU):
                    link.step(v.scalar_tensor_tensor(out=y[u][:, t, :], in0=src(t), scalar=mv[u][:, t, 0:1],
                                                     in1=bc[gain][:, :], op0=ALU.subtract, op1=ALU.mult))

            def shifted(u, bias, dst):
                for t in range(TU):
                    ins = v.scalar_tensor_tensor(out=dst(t), in0=y[u][:, t, :], scalar=rstd[u][:, t:t + 1],
                                                 in1=bias(t), op0=ALU.mult, op1=ALU.add)
                return ins

            over_e = lambda ap: ap.unsqueeze(2).to_broadcast([P, TB, E])
            of_e = lambda ap: ap.unsqueeze(1).to_broadcast([P, TB, E])
            r = Chain(dve, dve_rout)

            def pick_experts(b):
                dve.wait_ge(ex_set, b + 1)
                r.link(v.tensor_reduce(ssum, te(pr), AX.X, ALU.add))
                r.link(v.reciprocal(rs4, ssum))
                r.link(v.tensor_tensor(te(pr), te(pr), over_e(rs4), ALU.mult))
                for k in range(K2):
                    r.link(v.tensor_reduce(wk[k], te(pr), AX.X, ALU.max))
                    r.link(v.tensor_tensor(te(key), te(pr), over_e(wk[k]), ALU.is_equal))
                    r.link(v.tensor_tensor(te(key), te(key), of_e(down8[:, :]), ALU.mult))
                    r.link(v.tensor_reduce(kmax, te(key), AX.X, ALU.max))
                    r.link(v.tensor_tensor(te(oh[k]), te(key), over_e(kmax), ALU.is_equal))
                    if k == 0:
                        r.link(v.scalar_tensor_tensor(out=pr, in0=oh[0], scalar=-4.0, in1=pr,
                                                      op0=ALU.mult, op1=ALU.add))
                v.tensor_tensor(picks, oh[0], oh[1], ALU.add).then_inc(picks_set, 1)
                r.link(v.tensor_tensor(ws, wk[0], wk[1], ALU.add))
                r.link(v.reciprocal(wrs, ws))
                for k in range(K2):
                    r.step(v.tensor_tensor(row_buf[k][:, b * TB:(b + 1) * TB, W_COL:W_COL + 1]
                                           .rearrange("p t o -> p (t o)"), wk[k], wrs, ALU.mult))

            def place_tokens(b, rank):
                dve.wait_ge(rank_ps, b + 1)
                r.link(v.tensor_copy(et(tot), rank[:, TB * E:2 * TB * E].rearrange("p (t e) -> p e t", e=E)))
                r.link(v.tensor_tensor_scan(incl, smask[:, :, :].rearrange("p e t -> p (e t)"), tot, 0.0,
                                            ALU.mult, ALU.add))
                r.link(v.tensor_tensor(tmp, incl, tot, ALU.subtract))
                r.link(v.tensor_tensor(te(slot), rank[:, 0:TB * E].rearrange("p (t e) -> p t e", e=E),
                                       tmp.rearrange("p (e t) -> p t e", t=TB), ALU.add))
                r.link(v.tensor_tensor(te(slot), te(slot), of_e(base[:, :]), ALU.add))
                r.step(v.tensor_tensor(base[:, :].unsqueeze(2), base[:, :].unsqueeze(2), et(incl)[:, :, TB - 1:TB],
                                       ALU.add))
                for k in range(K2):
                    r.link(v.tensor_tensor(key, slot, oh[k], ALU.mult))
                    r.link(v.tensor_reduce(sl4, te(key), AX.X, ALU.add))
                    ins = v.tensor_copy(idx[:, k, b * TB:(b + 1) * TB], sl4)
                    if k < K2 - 1:
                        r.link(ins)
                ins.then_inc(slots_set, 1)

            for step, g, u in pipeline(DVE_AT):
                A, Bk = duo[u]
                tile = lambda t: x_all[:, g * TU + t, :]
                yu = lambda t: y[u][:, t, :]
                if step == "prep1":
                    if g == 0:
                        prepare()
                elif step == "prep2":
                    if g == 0:
                        prepare_rest()
                elif step == "prep3":
                    if g == 0:
                        finish_preparing()
                elif step == "ln0":
                    if g == 0:
                        dve.wait_ge(in_x0, 16)
                    elif g == TB // TU:
                        dve.wait_ge(in_x, 16 * (B - 1))
                    stats(u, tile, ln_var[0], link)
                elif step == "h0":
                    dve.wait_ge(ln_rstd[0], g + 1)
                    shift(u, nmr0_set)
                elif step == "dot":
                    dve.wait_ge(mm_ps, g + 1)
                    for t in range(TU):
                        link.step(v.tensor_tensor_reduce(
                            out=junk[(u + 2 * t) % NS][:, :], in0=h0[u][:, t, :],
                            in1=Bk[:, t * 2 * D:t * 2 * D + D],
                            scale=1.0, scalar=0.0, op0=ALU.mult, op1=ALU.add, accum_out=sdot[u][:, t:t + 1]))
                    link.settle()
                    v.tensor_scalar(nsc[u][:, :], sdot[u][:, :], -float(D) ** 0.5, None, ALU.mult)\
                     .then_inc(sc_set, 1)
                elif step == "y1":
                    dve.wait_ge(esc_set, g + 1)
                    link.link(v.reciprocal(rsc[u][:, :], esc[u][:, :]))
                    link.link(v.tensor_tensor(psc[u][:, :], esc[u][:, :], rsc[u][:, :], ALU.mult))
                    dve.wait_ge(h0b_set, g + 1)
                    for t in range(TU):
                        link.step(v.scalar_tensor_tensor(out=yu(t), in0=Bk[:, t * 2 * D + D:(t + 1) * 2 * D],
                                                         scalar=psc[u][:, t:t + 1], in1=h0b[u][:, t, :],
                                                         op0=ALU.mult, op1=ALU.add))
                    link.settle()
                    stats(u, yu, ln_var[1], link)
                    scaled(u, yu, "g1")
                elif step == "x1":
                    dve.wait_ge(ln_rstd[1], g + 1)
                    link.settle()
                    shifted(u, lambda t: bc["b1"][:, :], lambda t: x1[u][:, t, :]).then_inc(x1_set, 1)
                elif step in ("m0", "m1"):
                    t = int(step[1])
                    for k in range(H // 2):
                        dve.wait_ge(s_ps[t], g * 4 + k + 1)
                        v.tensor_reduce(nmax[u][:, t, 2 * k:2 * k + 2],
                                        duo[u][k % 2][:, 0:2 * M].rearrange("p (j m) -> p j m", j=2),
                                        AX.X, ALU.max, negate=True).then_inc(max_set[t], 1)
                elif step == "ca":
                    dve.wait_ge(avT_ps, g + 1)
                    o = Bk.rearrange("p (a q) -> p a q", q=Q)
                    den = rden[u][:, :, :].rearrange("p t h -> p (t h)").unsqueeze(2)
                    link.link(v.reciprocal(den, o[:, :, DH:DH + 1]))
                    v.tensor_tensor(y[u][:, :, :].rearrange("p t (h d) -> p (t h) d", d=DH), o[:, :, 0:DH],
                                    den.to_broadcast([P, TU * H, DH]), ALU.mult).then_inc(ca_set, 1)
                elif step == "y2":
                    dve.wait_ge(y2_ps, g + 1)
                    stats(u, lambda t: Bk[:, t * D:(t + 1) * D], ln_var[2], link)
                    scaled(u, lambda t: Bk[:, t * D:(t + 1) * D], "g2")
                elif step == "x2":
                    dve.wait_ge(ln_rstd[2], g + 1)
                    link.settle()
                    shifted(u, lambda t: bc["b2"][:, :], lambda t: x2[u][:, t, :]).then_inc(x2_set, 1)
                elif step == "y3":
                    dve.wait_ge(y3_ps, g + 1)
                    stats(u, lambda t: A[:, t * D:(t + 1) * D], ln_var[3], link)
                    scaled(u, lambda t: A[:, t * D:(t + 1) * D], "g3")
                elif step == "xr":
                    dve.wait_ge(x0b_set, g + 1)
                    dve.wait_ge(ln_rstd[3], g + 1)
                    link.settle()
                    link.link(shifted(u, tile, tile))
                    stats(u, tile, ln_var[4], link)
                elif step == "n":
                    dve.wait_ge(ln_rstd[4], g + 1)
                    shift(u, nmr4_set)
                elif step == "lg":
                    dve.wait_ge(lg_ps, g + 1)
                    v.tensor_copy(lg_all[:, g * TU:(g + 1) * TU, :],
                                  A[:, 0:TU * E].rearrange("p (t e) -> p t e", e=E)).then_inc(lg_set, 1)
                elif step == "r0" and g % 2:
                    dve.wait_ge(lg_set, g + 1)
                    lgf = lg_all[:, g // 2 * TB:(g // 2 + 1) * TB, :]
                    r.link(v.tensor_reduce(m0, lgf, AX.X, ALU.max))
                    v.tensor_tensor(te(lgm), lgf, over_e(m0), ALU.subtract).then_inc(max0_set, 1)
                elif step == "r1" and g % 2:
                    pick_experts(g // 2)
                elif step == "r2" and g % 2:
                    place_tokens(g // 2, A)

            r.settle()
            r.link(v.tensor_tensor(cnt, base[:, :], ebase[:, :], ALU.subtract))
            r.step(v.tensor_copy(cnti[:, :], cnt))
            r.link(v.tensor_tensor(cmp.rearrange("p (e t) -> p e t", e=E), cnt.unsqueeze(2).to_broadcast([P, E, NT]),
                                   thr[:, :].unsqueeze(1).to_broadcast([P, E, NT]), ALU.is_gt))
            r.link(v.tensor_reduce(ntl, cmp.rearrange("p (e t) -> p e t", e=E), AX.X, ALU.add))
            r.link(v.tensor_tensor_scan(tend, onef[:, 0:E], ntl, 0.0, ALU.mult, ALU.add))
            r.step(v.tensor_tensor(tcmp, tend.unsqueeze(1).to_broadcast([P, TILES, E]),
                                   tile_c[:, :].unsqueeze(2).to_broadcast([P, TILES, E]), ALU.is_le))
            r.link(v.tensor_tensor(tval, tend, ntl, ALU.subtract))
            r.step(v.tensor_reduce(teid, tcmp, AX.X, ALU.add))
            r.link(v.scalar_tensor_tensor(out=tval, in0=tval, scalar=-float(P), in1=ebase[:, :],
                                          op0=ALU.mult, op1=ALU.add))
            r.link(v.tensor_tensor(tcmp, teid.unsqueeze(2).to_broadcast([P, TILES, E]),
                                   upto8[:, :].unsqueeze(1).to_broadcast([P, TILES, E]), ALU.is_equal))
            r.link(v.tensor_tensor(tcmp, tcmp, tval.unsqueeze(1).to_broadcast([P, TILES, E]), ALU.mult))
            r.link(v.tensor_reduce(toff, tcmp, AX.X, ALU.add))
            r.step(v.scalar_tensor_tensor(out=toff, in0=tile_c[:, :], scalar=float(P), in1=toff,
                                          op0=ALU.mult, op1=ALU.add))
            r.link(v.tensor_scalar(tdum, teid, float(E), None, ALU.is_ge))
            r.link(v.scalar_tensor_tensor(out=toff, in0=tdum, scalar=float(E * REG - K2 * NT * P), in1=toff,
                                          op0=ALU.mult, op1=ALU.add))
            r.link(v.tensor_scalar(teid, teid, float(E - 1), None, ALU.min))
            r.link(v.tensor_copy(meta[:, 1, :], toff))
            v.tensor_copy(meta[:, 0, :], teid).then_inc(meta_set, 1)
            with dve.Fori(0, TURNS) as it:
                for u in range(U):
                    dve.wait_ge(sh_ps[u], it + 1)
                    v.tensor_scalar(flat3(nT_all[:, bass.ds((it * U + u) * TB, TB), :]), bank[u][2], sig[:, :], None,
                                    ALU.mult).then_inc(sh_set[u], 1)

            def copy_weights(j, k):
                e = dve.value_load(meta[0:1, 0, bass.ds(j, 1)], min_val=0, max_val=E - 1)
                v.tensor_copy(wbuf[:, k % WB, :], w1g[:, bass.ds(e, 1), :].rearrange("p e c -> p (e c)"))\
                 .then_inc(w_sb, 1)

            def copy_tokens(j, k):
                dve.wait_ge(xt_ps, j + 1)
                v.tensor_copy(xtT[k % 2], bank[k % 2][0][:, 0:P]).then_inc(xt_sb, 1)

            def weigh(j, k):
                dve.wait_ge(dn_ps, j + 1)
                v.tensor_scalar(yt[k % RU], bank[k % 2][3][:, 0:D], xt[k % RU][:, W_COL:W_COL + 1], None,
                                ALU.mult).then_inc(y_set[k % RU], 1)

            def dve_step(j, k):
                copy_tokens(j + 1, k + 1)
                weigh(j - 1, k - 1)
                copy_weights(j + 2, k + 2)

            dve.wait_ge(meta_set, 1)
            dve.wait_ge(gate_used, E // GH)
            for j in range(WB - 1):
                copy_weights(j, j)
            copy_tokens(0, 0)
            copy_tokens(1, 1)
            copy_weights(2, 2)
            with dve.Fori(0, ETURNS) as it:
                for k in range(1, RU + 1):
                    dve_step(it * RU + k, k)
            for j in range(ETURNS * RU + 1, TILES - 2):
                dve_step(j, j)
            copy_tokens(TILES - 1, TILES - 1)
            for j in range(TILES - 3, TILES):
                weigh(j, j)
            def start(g):
                dve.wait_ge(sum_set, g + 1)
                own = res[0][:, g * TU:(g + 1) * TU, :]
                link.link(v.tensor_tensor(own, own, nT_all[:, g * TU:(g + 1) * TU, :], ALU.add))
                stats(g % NS, lambda t: res[0][:, g * TU + t, :], cv_var, link)
                for t in range(TU):
                    link.step(v.scalar_tensor_tensor(out=y[g % NS][:, t, :], in0=res[0][:, g * TU + t, :],
                                                     scalar=mv[g % NS][:, t, 0:1], in1=bc["g4"][:, :],
                                                     op0=ALU.subtract, op1=ALU.mult))

            def finish(g):
                dve.wait_ge(cv_rstd, g + 1)
                dve.wait_ge(xb_set, B)
                shifted(g % NS, lambda t: x_all[:, g * TU + t, :], lambda t: res[0][:, g * TU + t, :])\
                    .then_inc(fin_set, 1)

            for g in range(G):
                start(g)
                if g:
                    finish(g - 1)
            link.settle()
            finish(G - 1)

        @block.tensor
        def _(pe):
            t_ = nc.tensor

            def mul(out, lhsT, rhs, start=True, stop=True):
                return t_.matmul(out, lhsT, rhs, start=start, stop=stop, skip_group_check=True)

            def prepare():
                pe.wait_ge(ident_set, 1)
                pe.wait_ge(in_row, 16 * N_ROW)
                t_.transpose(bank[1][3][:, 0:NR], vrow[:, :], ident[0:NR, 0:NR]).then_inc(vc_ps, 1)
                pe.wait_ge(in_w, 16 * 3)
                for i, w in enumerate((wsao, winp[:, 0], winp[:, 1], winp[:, 2])):
                    ins = t_.transpose(bank[0][0][:, i * P:(i + 1) * P], w, ident[:, :])
                ins.then_inc(wt_ps, 1)
                pe.wait_ge(in_ctx, 16 * 2)
                for b in range(B):
                    at = (b % 2) * M
                    t_.transpose(bank[1][b // 2][:, at:at + P], ctx_main[:, b, :], ident[:, :])
                    ins = t_.transpose(bank[1][b // 2][:, at + P:at + M], ctx_tail[:, b, :], ident[0:MT, 0:MT])
                    if b % 2:
                        ins.then_inc(cT_ps, 1)
                pe.wait_ge(qb_set, 1)
                pe.wait_ge(wt_sb, 1)
                mul(bank[1][2][:, 0:D], wqkv[:, 0], wqkv[:, 1])
                mul(bank[1][2][:, D:2 * D], wqkv[:, 2], wt[:, T_SAO, :])
                mul(bank[1][3][0:2, 0:D], qkvb2[:, 1, :], wqkv[:, 0], stop=False)
                mul(bank[1][3][0:2, 0:D], qkvb2[:, 0, :], wqkv[:, 1], start=False)
                mul(bank[1][3][0:2, D:2 * D], qkvb2[:, 2, :], wt[:, T_SAO, :]).then_inc(mm_pr, 1)

            def prepare_rest():
                for k in range(2):
                    pe.wait_ge(cT_sb, k + 1)
                    mul(bank[1][k][:, 0:2 * M], wt[:, T_K, :],
                        cT[:, 2 * k:2 * k + 2, :].rearrange("p b m -> p (b m)")).then_inc(k_ps, 1)
                pe.wait_ge(mm_sb, 1)
                for b in range(B):
                    ins = mul(bank[1][3][:, b * D:(b + 1) * D], cT[:, b, 0:P], wt[:, T_V, :])
                ins.then_inc(v_ps, 1)
                for b in range(B):
                    ins = mul(bank[1][2][:, b * D:(b + 1) * D], cTr[:, b, :, :].rearrange("p r m -> p (r m)"),
                              wt[:, T_V, :])
                ins.then_inc(v_ps, 1)
                pe.wait_ge(in_l, 16 * 3)
                weights = [wmo] + [wl1[:, c] for c in range(FFC)] + [wl2[:, c * P:(c + 1) * P] for c in range(FFC)]
                for i, w in enumerate(weights, 4):
                    ins = t_.transpose(bank[0][i // 4][:, (i % 4) * P:(i % 4 + 1) * P], w, ident[:, :])
                    if i % 4 == 3 or i == NTR - 1:
                        ins.then_inc(wt_ps, 1)

            def turned(out, src, done):
                for t in range(TU):
                    ins = t_.transpose(out[:, t * P:(t + 1) * P], src(t), ident[:, :])
                ins.then_inc(done, 1)

            def biased(out, at, n, stop=False):
                return mul(out, one2[:, :], brow[:, at:at + n], stop=stop)

            for step, g, u in pipeline(PE_AT):
                A, Bk = duo[u]
                b, k = g // 2, (g // 2) % U
                columns = lambda t: slice(t * P, (t + 1) * P)
                if step == "prep1":
                    if g == 0:
                        prepare()
                elif step == "prep2":
                    if g == 0:
                        prepare_rest()
                elif step == "h0T":
                    if g >= NS:
                        pe.wait_ge(nT_set, g - NS + 1)
                        pe.wait_ge(lg_set, g - NS + 1)
                        if g % 2:
                            pe.wait_ge(slots_set, (g - NS) // 2 + 1)
                    pe.wait_ge(h0_set, g + 1)
                    turned(A, lambda t: h0[u][:, t, :], tr_ps[0])
                elif step == "mm":
                    pe.wait_ge(tr_sb[0], g + 1)
                    if g == 0:
                        pe.wait_ge(brow_set, 1)
                        pe.wait_ge(wt_act, 3)
                    for t in range(TU):
                        o = Bk[:, t * 2 * D:(t + 1) * 2 * D]
                        biased(o, C_QK, 2 * D)
                        ins = mul(o, actT[u][:, columns(t)], mm[:, :], start=False)
                    ins.then_inc(mm_ps, 1)
                elif step == "x1T":
                    pe.wait_ge(x1_set, g + 1)
                    turned(A, lambda t: x1[u][:, t, :], tr_ps[1])
                elif step == "q":
                    pe.wait_ge(tr_sb[1], g + 1)
                    mul(A[:, UL:2 * UL], wt[:, T_Q, :], actT[u][:, :]).then_inc(q_ps, 1)
                elif step in ("s0", "s1"):
                    t = int(step[1])
                    if t == 0:
                        pe.wait_ge(q_sb, g + 1)
                        pe.wait_ge(kbr_set, b + 1)
                    for i in range(H // 2):
                        if i > 1:
                            pe.wait_ge(max_set[t], g * 4 + i - 1)
                        elif t:
                            pe.wait_ge(max_set[0], g * 4 + i + 3)
                        mul(duo[u][i % 2][:, 0:2 * M], qTr[u][:, columns(t)],
                            kbr[k][:, 2 * i:2 * i + 2, :].rearrange("p h m -> p (h m)")).then_inc(s_ps[t], 1)
                elif step == "nm":
                    pe.wait_ge(max_set[1], (g + 1) * 4)
                    for t in range(TU):
                        ins = t_.transpose(A[0:H, columns(t)], nmax[u][:, t, :], ident[:, :])
                    ins.then_inc(nm_ps, 1)
                elif step in ("n01", "n2", "n3", "n4"):
                    for n in dict(n01=(0, 1), n2=(2,), n3=(3,), n4=(4,))[step]:
                        if n == 0 and g == 0:
                            pe.wait_ge(sel_set, 1)
                        if n == 0:
                            pe.wait_ge(nm_sb, g + 1)
                            pe.wait_ge(kb_set, (b + 1) * 4)
                        elif n == 2:
                            pe.wait_ge(e_set[0], g + 1)
                        elif n == 3:
                            pe.wait_ge(e_set[2], g + 1)
                        elif n == 4:
                            pe.wait_ge(av_sb[0], g + 1)
                        for i in range(2):
                            o = (A, Bk, A, A, Bk)[n][:, i * UL:(i + 1) * UL]
                            if n == 2:
                                keys = kb[k][:, H * P + i * P:H * P + (i + 1) * P]
                                pick = selt[:, i * HG:(i + 1) * HG, :].rearrange("p h m -> p (h m)")
                            else:
                                h = 2 * (n if n < 2 else n - 1) + i
                                keys, pick = kb[k][:, h * P:(h + 1) * P], sel[:, h, :]
                            mul(o, pick, nmT[u][:, :], stop=False)
                            ins = mul(o, keys, qT[u][:, :], start=False)
                        ins.then_inc(st_ps[n], 1)
                elif step in ("av0", "av1"):
                    gr = int(step[2])
                    pe.wait_ge(e_set[(2, 4)[gr]], g + 1)
                    for at in (0, 1):
                        for i in range(HG):
                            h = gr * HG + i
                            o = (Bk, A)[gr][i * Q:(i + 1) * Q, 0:UL]
                            if at == 0:
                                mul(o, vm[k][:, h * Q:(h + 1) * Q], pT[u][:, i, :], stop=False)
                            else:
                                ins = mul(o, vt[k][:, h * Q:(h + 1) * Q], pT[u][:, HG + gr, :], start=False)
                    ins.then_inc(av_ps[gr], 1)
                elif step == "avT":
                    pe.wait_ge(av_sb[1], g + 1)
                    for t in range(TU):
                        for gr in range(2):
                            at = t * 2 * P + gr * P
                            ins = t_.transpose(Bk[:, at:at + P], av[u][gr][:, columns(t)], ident[:, :])
                    ins.then_inc(avT_ps, 1)
                elif step == "caT":
                    pe.wait_ge(ca_set, g + 1)
                    turned(A, lambda t: y[u][:, t, :], tr_ps[2])
                elif step == "y2":
                    pe.wait_ge(tr_sb[2], g + 1)
                    if g == 0:
                        pe.wait_ge(brow_set, 2)
                    for t in range(TU):
                        biased(Bk[:, columns(t)], C_MO, D)
                        mul(Bk[:, columns(t)], actT[u][:, columns(t)], wt[:, T_MO, :], start=False, stop=False)
                        ins = mul(Bk[:, columns(t)], ident[:, :], x1[u][:, t, :], start=False)
                    ins.then_inc(y2_ps, 1)
                elif step == "x2T":
                    pe.wait_ge(x2_set, g + 1)
                    turned(A, lambda t: x2[u][:, t, :], tr_ps[3])
                elif step == "l1":
                    pe.wait_ge(tr_sb[3], g + 1)
                    for c in range(FFC):
                        ins = mul((A, Bk)[c // 2][:, c % 2 * UL:(c % 2 + 1) * UL], wt[:, T_L1 + c, :], actT[u][:, :])
                        if c % 2:
                            ins.then_inc(l1_ps, 1)
                elif step == "l2":
                    pe.wait_ge(l1_sb, (g + 1) * FFC)
                    for t in range(TU):
                        biased(A[:, columns(t)], C_L2, D)
                        for c in range(FFC):
                            mul(A[:, columns(t)], pT[u][:, c, columns(t)], wt[:, T_L2 + c, :],
                                start=False, stop=False)
                        ins = mul(A[:, columns(t)], ident[:, :], x2[u][:, t, :], start=False)
                    ins.then_inc(y3_ps, 1)
                elif step == "nT":
                    pe.wait_ge(n_set, g + 1)
                    turned(Bk, lambda t: row_buf[0][:, g * TU + t, 0:D], tr_ps[4])
                elif step == "router":
                    pe.wait_ge(tr_sb[4], g + 1)
                    if g == 0:
                        pe.wait_ge(in_late, 16 * 3)
                    for t in range(TU):
                        o = A[:, t * E:(t + 1) * E]
                        biased(o, C_BR, E)
                        ins = mul(o, actT[u][:, columns(t)], wr[:, :], start=False)
                    ins.then_inc(lg_ps, 1)
                elif step == "rank" and g % 2:
                    pe.wait_ge(picks_set, g // 2 + 1)
                    mul(A[:, 0:TB * E], before[:, :], picks)
                    mul(A[:, TB * E:2 * TB * E], onef[:, :], picks).then_inc(rank_ps, 1)
            pe.wait_ge(nT_set, G)
            pe.wait_ge(lg_set, G)
            with pe.Fori(0, TURNS) as it:
                for u in range(U):
                    for c in range(FSC):
                        ins = mul(bank[u][c], sw1s[:, c * P:(c + 1) * P],
                                  flat3(nT_all[:, bass.ds((it * U + u) * TB, TB), :]))
                    ins.then_inc(hs_ps[u], 1)
                for u in range(U):
                    pe.wait_ge(hs_set[u], it + 1)
                    if u == U - 1:
                        pe.wait_ge(slots_set, B)
                    for t in range(TB):
                        o = bank[u][2][:, t * P:(t + 1) * P]
                        biased(o, C_SB2, D)
                        for c in range(FSC):
                            ins = mul(o, hs[u][:, c, t * P:(t + 1) * P], sw2s[:, c, :],
                                      start=False, stop=c == FSC - 1)
                    ins.then_inc(sh_ps[u], 1)
                for u in range(U):
                    pe.wait_ge(sh_set[u], it + 1)
            pe.wait_ge(meta_set, 1)
            pe.wait_ge(in_w2, 16 * E)

            def up(j, k):
                pe.wait_ge(w_sb, j + 1)
                pe.wait_ge(xt_sb, j + 1)
                for c in range(FC):
                    ins = mul(bank[k % 2][1 + c // 2][:, c % 2 * P:(c % 2 + 1) * P],
                              wbuf[:, k % WB, c * P:(c + 1) * P], xtT[k % 2])
                    if c % 2:
                        ins.then_inc(up_ps, 1)

            def turn_tokens(j, k, uses):
                pe.wait_ge(xt_in[k % RU], 16 * uses)
                t_.transpose(bank[k % 2][0][:, 0:P], xt[k % RU][:, 0:D], ident[:, :]).then_inc(xt_ps, 1)

            def down(j, k):
                e = pe.value_load(meta[0:1, 0, bass.ds(j, 1)], min_val=0, max_val=E - 1)
                o = bank[k % 2][3][:, 0:D]
                mul(o, one2[:, :], brow[:, bass.ds(e * D + C_B2, D)], stop=False)
                for c in range(FC):
                    pe.wait_ge(h_set, j * FC + c + 1)
                    ins = mul(o, hT[k % 2][:, c * P:(c + 1) * P], w2s[:, bass.ds(e * F + c * D, D)],
                              start=False, stop=c == FC - 1)
                ins.then_inc(dn_ps, 1)

            def pe_step(j, k, uses):
                up(j, k)
                turn_tokens(j + 1, k + 1, uses)
                down(j - 1, k - 1)

            turn_tokens(0, 0, 1)
            up(0, 0)
            turn_tokens(1, 1, 1)
            with pe.Fori(0, ETURNS) as it:
                for k in range(1, RU + 1):
                    pe_step(it * RU + k, k, it + (k + 1) // RU + 1)
            for j in range(ETURNS * RU + 1, TILES - 1):
                pe_step(j, j, (j + 1) // RU + 1)
            up(TILES - 1, TILES - 1)
            down(TILES - 2, TILES - 2)
            pe.wait_ge(y_set[(TILES - 3) % RU], (TILES - 3) // RU + 1)
            down(TILES - 1, TILES - 1)


_NAMES = [
    "x", "ctx_1024",
    *("L0_xattn_" + n for n in (
        "qkv_w", "qkv_b", "sa_out_w", "sa_out_b", "in_proj_w", "in_proj_b", "mha_out_w", "mha_out_b",
        "lin1_w", "lin1_b", "lin2_w", "lin2_b", "ln1_g", "ln1_b", "ln2_g", "ln2_b", "ln3_g", "ln3_b")),
    *("L0_ffn_" + n for n in (
        "router_w", "router_b", "w1", "b1", "gate", "w2", "b2", "sw1", "sb1", "sgate", "sw2", "sb2",
        "shared_weight", "ln_g", "ln_b")),
]


def kernel(**inputs):
    import numpy as np
    import concourse.bacc as bacc
    from concourse.bass_utils import run_bass_kernel_spmd

    nc = bacc.Bacc("TRN2", target_bir_lowering=False, num_devices=1)
    arrays, args = {}, []
    for name in _NAMES:
        a = np.ascontiguousarray(inputs[name])
        if a.ndim == 0:
            a = a.reshape(1)
        arrays[f"in_{name}"] = a
        args.append(nc.dram_tensor(f"in_{name}", a.shape, mybir.dt.from_np(a.dtype), kind="ExternalInput").ap())
    shape = inputs["x"].shape
    args.append(nc.dram_tensor("out_x", shape, F32, kind="ExternalOutput").ap())
    xattn_moe_kernel(nc, *args)
    r = run_bass_kernel_spmd(nc, [arrays], core_ids=[0])
    return r.results[0]["out_x"]
```

```python
from contextlib import ExitStack

import concourse.bass as bass
from concourse import mybir

ALU = mybir.AluOpType
ACT = mybir.ActivationFunctionType
AX = mybir.AxisListType
F32 = mybir.dt.float32
F32R = mybir.dt.float32r
U32 = mybir.dt.uint32
I32 = mybir.dt.int32

P = 128
EPS = 1e-5


class Chain:

    def __init__(self, eng, sem):
        self.eng, self.sem, self.n = eng, sem, 0

    def step(self, instruction):
        instruction.then_inc(self.sem, 1)
        self.n += 1

    def settle(self):
        self.eng.wait_ge(self.sem, self.n)

    def link(self, instruction):
        self.step(instruction)
        self.settle()


def xattn_moe_kernel(
    nc, x, ctx_1024, qkv_w, qkv_b, sa_out_w, sa_out_b, in_proj_w, in_proj_b, mha_out_w, mha_out_b,
    lin1_w, lin1_b, lin2_w, lin2_b, ln1_g, ln1_b, ln2_g, ln2_b, ln3_g, ln3_b,
    router_w, router_b, w1, b1, gate, w2, b2, sw1, sb1, sgate, sw2, sb2, shared_weight, ln_g, ln_b,
    out,
):
    B, S, D = x.shape
    M = ctx_1024.shape[1]
    E, _, F = w1.shape
    FF = lin1_w.shape[0]
    FS = sw1.shape[1]
    H = 8
    DH = D // H
    TB = S // P
    NT = B * TB
    MT = M - P
    HG = 4
    Q = P // HG
    MP = P + Q
    FC = F // P
    FFC = FF // P
    FSC = FS // P
    WE = F + FC
    K2 = 2
    TOKENS = NT * P
    REG = TOKENS + P
    TILES = 40
    ROW = 132
    W_COL, I_COL = D, D + 1
    U = 2
    TU = TB // 2
    UL = TU * P
    G = NT // TU
    NS = 4
    RU = 6
    WB = 3
    assert D == P and S % P == 0 and B % U == 0 and H * DH == P
    assert RU % WB == 0 and RU % 2 == 0
    assert G == E and TB * K2 == 8 and B == 4 and FSC == 2
    assert TILES >= K2 * NT + E - 1 and DH < Q and MT <= Q

    C_B2 = 0
    C_SB2 = C_B2 + E * D
    C_BR = C_SB2 + D
    C_L2 = C_BR + E
    C_MO = C_L2 + D
    C_QK = C_MO + D
    C_END = C_QK + 2 * D

    IDLE = TILES - K2 * NT
    assert NT == IDLE + E
    rows = nc.dram_tensor("dispatched_rows", [E * REG + IDLE * P, ROW], F32).ap()
    pads = nc.dram_tensor("padding_rows", [E * P, ROW], F32).ap()
    results = nc.dram_tensor("expert_results", [K2 * TOKENS + NT * P, D], F32).ap()

    with ExitStack() as ctx:
        def sb(name, shape, dt=F32):
            return ctx.enter_context(nc.sbuf_tensor(name, shape, dt))

        def sem(name):
            return ctx.enter_context(nc.semaphore(name))

        def sides(name, n=U):
            return [sem(f"{name}{u}") for u in range(n)]

        def pair(name, shape, dt=F32):
            return [sb(f"{name}{u}", shape, dt) for u in range(U)]

        def four(name, shape, dt=F32):
            return [sb(f"{name}{u}", shape, dt) for u in range(NS)]

        SL = TB * P
        GS = HG + 2
        space = sb("space", [P, NS * GS * UL])
        pT = [space[:, u * GS * UL:(u + 1) * GS * UL].rearrange("p (g n) -> p g n", n=UL) for u in range(NS)]
        kb = pair("kb", [P, H * MP])
        kbr = pair("kbr", [P, H, M], F32R)

        class Space:

            def __init__(self, ap):
                self.ap, self.at = ap, 0

            def cut(self, n, p=P):
                self.at += n
                assert self.at <= self.ap.shape[1]
                return self.ap[0:p, self.at - n:self.at]

        half = NS * GS * UL // 2
        flat = [space[:, u * half:(u + 1) * half] for u in range(U)]

        early = Space(flat[0])
        wqkv = early.cut(3 * D).rearrange("p (k c) -> p k c", k=3)
        wsao = early.cut(D)
        winp = early.cut(3 * D).rearrange("p (k c) -> p k c", k=3)
        wmo = early.cut(D)
        wl1 = early.cut(FFC * D).rearrange("p (k c) -> p k c", k=FFC)
        wl2 = early.cut(FF)
        early = Space(flat[1])
        ctx_main = early.cut(B * D).rearrange("p (b c) -> p b c", b=B)
        ctx_tail = early.cut(B * D, MT).rearrange("p (b c) -> p b c", b=B)
        sel0 = early.cut(H * P).rearrange("p (h c) -> p h c", h=H)

        w1g = sb("w1g", [P, E, WE])
        wbuf = sb("wbuf", [P, WB, WE])
        w2s = sb("w2s", [P, E * F])
        row32 = w2s[0:2, 0:C_END]
        GH = 2
        gate_bc = sb("gate_bc", [P, GH * F])
        sw1s = sb("sw1s", [P, FS])
        sw2s = sb("sw2s", [P, FSC, D])
        wr = sb("wr", [P, E])
        T_SAO, T_Q, T_K, T_V, T_MO, T_L1, T_L2 = 0, 1, 2, 3, 4, 5, 5 + FFC
        NTR = T_L2 + FFC
        wt = sb("wt", [P, NTR, D])
        mm = sb("mm", [P, 2 * D])
        cT = sb("cT", [P, B, M])
        cTr = sb("cTr", [P, B, HG, Q])
        kT = sb("kT", [P, B, MP])
        vmain = sb("vmain", [P, B, H * Q])
        vtail = sb("vtail", [P, B, H * Q])
        R_IN, R_L1 = 3, 6
        R_SG = R_L1 + FFC
        R_SB = R_SG + FSC
        R_B1 = R_SB + FSC
        R_G = R_B1 + E * FC
        NR = R_G + E * FC
        vrow = sb("vrow", [NR, P])
        vcol = sb("vcol", [P, NR])
        col_bq2, col_bk2 = vcol[:, R_IN:R_IN + 1], vcol[:, R_IN + 1:R_IN + 2]
        col_l1b, col_sg = vcol[:, R_L1:R_SG], vcol[:, R_SG:R_SB]
        col_sbg = sb("col_sbg", [P, FSC])
        col_bqs = sb("col_bqs", [P, 1])
        col_sw = sb("col_sw", [P, 1])
        sig = sb("sig", [P, 1])
        qkvb2 = sb("qkvb2", [P, 3, 2])
        BC = ("sab", "vb2", "g1", "b1", "g2", "b2", "g3", "b3", "g4", "b4")
        bc = {name: sb("bc_" + name, [P, D]) for name in BC}
        mrow = sb("mrow", [2, 1])
        brow = sb("brow", [P, C_END], F32R)
        ident = sb("ident", [P, P])
        before = sb("before", [P, P])
        onef = sb("onef", [P, P])
        one2 = sb("one2", [P, P], F32R)
        mask8 = sb("mask8", [P, H])
        mask32 = sb("mask32", [P, H])
        sel = sb("sel", [P, H, P], F32R)
        selt = sb("selt", [P, H, Q], F32R)
        nhalf = sb("nhalf", [P, TB])
        down8 = sb("down8", [P, E])
        upto8 = sb("upto8", [P, E])
        ebase = sb("ebase", [P, E])
        thr = sb("thr", [P, NT])
        tile_c = sb("tile_c", [P, TILES])
        smask = {n: sb(f"smask{n}", [P, E, n]) for n in (TU, TB)}
        base = sb("base", [P, E])
        x_all = sb("x_all", [P, NT, D])
        nT_all = sb("nT_all", [P, NT, D])
        row_buf = [sb(f"row_buf{k}", [P, NT, ROW]) for k in range(K2)]
        lg_all = sb("lg_all", [P, NT, E])
        st = four("st", [P, TU, 6])
        mv = four("mv", [P, TU, 2])
        ve = four("ve", [P, TU])
        rstd = four("rstd", [P, TU])
        nmr = four("nmr", [P, TU])
        h0 = four("h0_", [P, TU, D])
        h0b = four("h0b", [P, TU, D])
        y = four("y", [P, TU, D])
        actT = four("actT", [P, UL])
        sdot = four("sdot", [P, TU])
        nsc = four("nsc", [P, TU])
        esc = four("esc", [P, TU])
        rsc = four("rsc", [P, TU])
        psc = four("psc", [P, TU])
        qT = four("qT", [P, UL])
        qTr = four("qTr", [P, UL], F32R)
        vm = pair("vm", [P, H * Q])
        vt = pair("vt", [P, H * Q])
        nmax = four("nmax", [P, TU, H])
        nmT = four("nmT", [P, UL], F32R)
        rden = four("rden", [P, TU, H])
        x1, x2 = h0, h0b
        assert 2 * HG == H
        flat3 = lambda ap: ap.rearrange("p t d -> p (t d)")
        av = [[flat3(h0b[u][:, :, :]), flat3(y[u][:, :, :])] for u in range(NS)]
        junk = four("junk", [P, D])
        xt = [kb[0][:, k * ROW:(k + 1) * ROW] for k in range(RU)]
        yt = [h0b[k % NS][:, k // NS, :] for k in range(RU)]
        hs = [flat[0][:, k * FSC * SL:(k + 1) * FSC * SL].rearrange("p (c n) -> p c n", c=FSC) for k in range(2)]
        hT = [flat[u][:, 0:SL] for u in range(U)]
        xtT = [actT[u][:, 0:P] for u in range(U)]
        route = Space(sb("route", [P, 10 * TB * E + 9 * TB]))
        lgm, pr, oh0, oh1, key, picks, tot, incl, slot, tmp = [route.cut(TB * E) for _ in range(10)]
        m0, ssum, rs4, kmax, ws, wrs, wk0, wk1, sl4 = [route.cut(TB) for _ in range(9)]
        late = Space(flat[1][:, FSC * SL:])
        cmp = late.cut(NT * E)
        tcmp = late.cut(TILES * E).rearrange("p (j e) -> p j e", j=TILES)
        teid, toff, tdum = [late.cut(TILES) for _ in range(3)]
        cnt, ntl, tend, tval = [late.cut(E) for _ in range(4)]
        oh = [oh0, oh1]
        wk = [wk0, wk1]
        idx = sb("idx", [P, K2, NT], U32)
        meta = sb("meta", [P, 2, TILES], I32)
        cnti = sb("cnti", [P, E], I32)
        res = [flat[k][:, SL:SL + NT * D].rearrange("p (t d) -> p t d", d=D) for k in range(K2)]

        psum = ctx.enter_context(nc.psum_tensor("psum", [P, 2 * NS, 512], F32))
        bank = [[psum[:, 4 * u + k, :] for k in range(4)] for u in range(U)]
        hid_bank = [bank[0][0:2], bank[0][2:4], bank[0][1::2], bank[1][0:2]]
        sh_bank = [bank[0][0], bank[0][2], bank[0][0], bank[0][2]]
        duo = [[psum[:, 2 * u + k, :] for k in range(2)] for u in range(NS)]

        in_x0, in_x, in_w, in_l = sem("in_x0"), sem("in_x"), sem("in_w"), sem("in_l")
        in_ctx, in_vec, in_rest, in_late = sem("in_ctx"), sem("in_vec"), sem("in_rest"), sem("in_late")
        in_row, vc_ps = sem("in_row"), sem("vc_ps")
        in_w1, in_w2, in_gate, gate_used = sem("in_w1"), sem("in_w2"), sem("in_gate"), sem("gate_used")
        ident_set, zeros_set = sem("ident_set"), sem("zeros_set")
        consts_set, pool_link = sem("consts_set"), sem("pool_link")
        wt_ps, wt_sb, wt_act, cT_ps, cT_sb = sem("wt_ps"), sem("wt_sb"), sem("wt_act"), sem("cT_ps"), sem("cT_sb")
        k_ps, k_sb, v_ps, v_sb = sem("k_ps"), sem("k_sb"), sem("v_ps"), sem("v_sb")
        qb_set, mm_pr, mm_sb, brow_set = sem("qb_set"), sem("mm_pr"), sem("mm_sb"), sem("brow_set")
        sel_set, act_prep, unread = sem("sel_set"), sem("act_prep"), sem("unread")
        dve_link = sem("dve_link")
        ln_var, ln_rstd = sides("ln_var", 5), sides("ln_rstd", 5)
        tr_ps, tr_sb = sides("tr_ps", 5), sides("tr_sb", 5)
        h0_set, h0b_set, x0b_set, mm_ps = sem("h0_set"), sem("h0b_set"), sem("x0b_set"), sem("mm_ps")
        sc_set, esc_set, x1_set, q_ps = sem("sc_set"), sem("esc_set"), sem("x1_set"), sem("q_ps")
        q_sb, kbr_set, kb_set = sem("q_sb"), sem("kbr_set"), sem("kb_set")
        nm_ps, nm_sb, nmr0_set, nmr4_set = sem("nm_ps"), sem("nm_sb"), sem("nmr0_set"), sem("nmr4_set")
        s_ps, max_set, av_ps, av_sb = sides("s_ps"), sides("max_set"), sides("av_ps"), sides("av_sb")
        st_ps, e_set = sides("st_ps", 5), sides("e_set", 5)
        avT_ps, ca_set, y2_ps, x2_set = sem("avT_ps"), sem("ca_set"), sem("y2_ps"), sem("x2_set")
        l1_ps, l1_sb, y3_ps, n_set = sem("l1_ps"), sem("l1_sb"), sem("y3_ps"), sem("n_set")
        row_set, nT_set, lg_ps, lg_set = sem("row_set"), sem("nT_set"), sem("lg_ps"), sem("lg_set")
        max0_set, ex_set, picks_set, rank_ps = sem("max0_set"), sem("ex_set"), sem("picks_set"), sem("rank_ps")
        dve_rout, slots_set, cnti_set, meta_set = sem("dve_rout"), sem("slots_set"), sem("cnti_set"), sem("meta_set")
        rows_out, pads_out, pool_pads, pads_set = sem("rows_out"), sem("pads_out"), sem("pool_pads"), sem("pads_set")
        hs_ps, hs_set, sh_ps, sh_set = sem("hs_ps"), sem("hs_set"), sem("sh_ps"), sem("sh_set")
        xt_in, y_set, y_out = ([sem(f"{s}{k}") for k in range(RU)] for s in ("xt_in", "y_set", "y_out"))
        xt_ps, xt_sb, w_sb, up_ps = sem("xt_ps"), sem("xt_sb"), sem("w_sb"), sem("up_ps")
        h_set, dn_ps = sem("h_set"), sem("dn_ps")
        res_in, sum_ps = sides("res_in", B), sem("sum_ps")
        xb_set, fin_set, fin_out, cv_var = sem("xb_set"), sem("fin_set"), sem("fin_out"), sem("cv_var")
        cv_rstd, cv_nmr, z_set, zg_set = sem("cv_rstd"), sem("cv_nmr"), sem("z_set"), sem("zg_set")

        OFF = 40
        PE_AT = dict(prep1=20, prep2=23, h0T=23, mm=38, x1T=47, q=50, s0=60, s1=69, nm=73, n01=83, n2=85,
                     av0=86, n3=87, n4=88, av1=93, avT=102, caT=110, y2=118, x2T=125, l1=126, l2=127, nT=151,
                     router=159, hid=164, rank=167)
        ACT_AT = dict(prep=40, sig=38, h0=22, h0T=37, esc=40, x1T=56, q=58, nm=78, e0=79, e1=83, e2=90, av0=96,
                      e3=98, e4=98, av1=102, caT=114, x2T=120, relu=136, n=145, nT=155, pr=159)
        DVE_AT = dict(ln0=13, h0=18, prep1=18, prep2=29, prep3=56, dot=34, y1=46, x1=51, m0=60, m1=68, ca=104,
                      y2=113, x2=121, y3=132, xr=135, n=144, lg=156, r0=157, r1=166, r2=170)
        POOL_AT = dict(late=82, ln0=38, h0b=55, kbr=65, ln1=65, kb=68, vv=83, x0b=97, ln2=144, ln3=153,
                       ln4=162, row=208, fold=145, sc0=213, sc1=226, sc2=226, sc3=228, sc4=234, sc5=250,
                       sc6=255, sc7=265)
        SLOTS = (G - 1) * OFF + max(max(at.values()) for at in (PE_AT, ACT_AT, DVE_AT, POOL_AT)) + 1

        ROUTED = {g: range((g - 1) * TU, (g + 1) * TU) for g in range(1, G - TB // TU, TB // TU)}
        ROUTED.update({g: range(g * TU, (g + 1) * TU) for g in range(G - TB // TU, G)})
        nth = {g: i for i, g in enumerate(ROUTED)}

        def pipeline(at):
            for slot in range(SLOTS):
                for g in range(G):
                    for name, when in at.items():
                        if slot - g * OFF == when:
                            yield name, g, g % NS

        ETURNS = TILES // RU
        assert TILES - ETURNS * RU >= 2
        N_ROW, N_VEC, N_REST = 7, 4, 12
        x_v = x.rearrange("b (t p) d -> p (b t) d", p=P)
        out_v = out.rearrange("b (t p) d -> p (b t) d", p=P)
        res_v = results.rearrange("(t p) d -> p t d", p=P)

        def apart(eng):
            eng.sem_inc(unread, 1)

        EP = 5

        def pad_rows(eng, e, done):
            n = eng.value_load(cnti[0:1, e:e + 1], min_val=0, max_val=TOKENS)
            eng.dma_start(rows[bass.ds(n + e * REG, P), :], pads[e * P:(e + 1) * P, :]).then_inc(done, 16)

        block = ctx.enter_context(nc.Block())

        @block.sync
        def _(sp):
            def load_x(b, done):
                sp.dma_start(x_all[:, b * TB:(b + 1) * TB, :], x_v[:, b * TB:(b + 1) * TB, :]).then_inc(done, 16)

            load_x(0, in_x0)
            sp.dma_start(wqkv, qkv_w.rearrange("(k p) c -> p k c", p=P)).then_inc(in_w, 16)
            sp.dma_start(wsao, sa_out_w).then_inc(in_w, 16)
            sp.dma_start(winp, in_proj_w.rearrange("(k p) c -> p k c", p=P)).then_inc(in_w, 16)
            sp.dma_start(ctx_main, ctx_1024[:, 0:P, :].rearrange("b m c -> m b c")).then_inc(in_ctx, 16)
            sp.dma_start(ctx_tail, ctx_1024[:, P:M, :].rearrange("b m c -> m b c")).then_inc(in_ctx, 16)
            sp.dma_start(wmo, mha_out_w).then_inc(in_l, 16)
            sp.dma_start(wl1, lin1_w.rearrange("(k p) c -> p k c", p=P)).then_inc(in_l, 16)
            sp.dma_start(wl2, lin2_w).then_inc(in_l, 16)
            load_x(1, in_x)
            for at, vec in ((C_B2, b2.rearrange("e d -> (e d)")), (C_SB2, sb2), (C_BR, router_b), (C_L2, lin2_b),
                            (C_MO, mha_out_b)):
                sp.dma_start(row32[:, at:at + vec.shape[0]], vec.partition_broadcast(2)).then_inc(in_rest, 16)
            for name, vec in dict(g2=ln2_g, b2=ln2_b, g3=ln3_g, b3=ln3_b, g4=ln_g, b4=ln_b).items():
                sp.dma_start(bc[name][:, :], vec.partition_broadcast(P)).then_inc(in_rest, 16)
            sp.dma_start(col_sw[:, :], shared_weight.partition_broadcast(P)).then_inc(in_rest, 16)
            for b in range(2, B):
                load_x(b, in_x)
            sp.dma_start(sw1s[:, :], sw1).then_inc(in_late, 16)
            sp.dma_start(sw2s[:, :, :], sw2.rearrange("(c p) d -> p c d", p=P)).then_inc(in_late, 16)
            sp.dma_start(wr[:, :], router_w).then_inc(in_late, 16)
            sp.wait_ge(pads_set, 1)
            sp.dma_start(rows[E * REG:, :].rearrange("(t p) r -> p t r", p=P),
                         row_buf[1][:, E:NT, :]).then_inc(pads_out, 16)
            sp.dma_start(pads.rearrange("(t p) r -> p t r", p=P), row_buf[1][:, 0:E, :]).then_inc(pads_out, 16)
            for e in range(E):
                sp.dma_start(w1g[:, e, 0:F], w1[e]).then_inc(in_w1, 16)
            for g in range(E // GH):
                if g:
                    sp.wait_ge(gate_used, g)
                sp.dma_start(gate_bc[:, :], gate[g * GH:(g + 1) * GH, :].rearrange("e f -> (e f)")
                             .partition_broadcast(P)).then_inc(in_gate, 16)
            sp.wait_ge(brow_set, 2)
            for e in range(E):
                sp.dma_start(w2s[:, e * F:(e + 1) * F].rearrange("p (c d) -> p c d", d=D),
                             w2[e].rearrange("(c p) d -> p c d", p=P)).then_inc(in_w2, 16)
            sp.wait_ge(cnti_set, 1)
            for e in range(EP):
                pad_rows(sp, e, pads_out)
            sp.wait_ge(meta_set, 1)
            sp.wait_ge(pads_out, 16 * (EP + 2))
            sp.wait_ge(pool_pads, 16 * (E - EP))
            sp.wait_ge(rows_out, 16 * K2 * NT)

            def load_tile(j, k):
                at = sp.value_load(meta[0:1, 1, bass.ds(j, 1)], min_val=0, max_val=E * REG + (IDLE - 1) * P)
                sp.dma_start(xt[k], rows[bass.ds(at, P), :]).then_inc(xt_in[k], 16)

            for k in range(RU):
                load_tile(k, k)
            with sp.Fori(1, ETURNS) as it:
                for k in range(RU):
                    sp.wait_ge(y_out[k], it * 16)
                    load_tile(it * RU + k, k)
            for k in range(TILES - ETURNS * RU):
                sp.wait_ge(y_out[k], 16 * ETURNS)
                load_tile(ETURNS * RU + k, k)
            for k in range(RU):
                sp.wait_ge(y_out[k], 16 * len(range(k, TILES, RU)))

            for b in range(B):
                for k in range(K2):
                    sp.dma_start(res[k][:, b * TB:(b + 1) * TB, :],
                                 res_v[:, b * TB + k * NT:(b + 1) * TB + k * NT, :]).then_inc(res_in[b], 16)
            for g in range(G):
                sp.wait_ge(fin_set, g + 1)
                sp.dma_start(out_v[:, g * TU:(g + 1) * TU, :], res[0][:, g * TU:(g + 1) * TU, :]).then_inc(fin_out, 16)
            sp.wait_ge(fin_out, 16 * G)

        @block.gpsimd
        def _(pool):
            g = nc.gpsimd
            link = Chain(pool, pool_link)
            link.step(g.memset(ident[:, :], 0.0))
            link.step(g.memset(nhalf[:, :], -0.5))
            link.step(g.memset(mrow[:, :], 0.0))
            link.settle()
            g.affine_select(out=ident[:, :], in_=ident[:, :], compare_op=ALU.not_equal, fill=1.0,
                            base=0, pattern=[[-1, P]], channel_multiplier=1).then_inc(ident_set, 1)
            g.affine_select(out=mrow[:, :], in_=mrow[:, :], compare_op=ALU.not_equal, fill=-1.0,
                            base=-1, pattern=[[0, 1]], channel_multiplier=1)
            g.memset(brow[:, :].bitcast(F32), 0.0)
            g.memset(kT[:, :, :], 0.0)
            g.memset(cTr[:, :, :, :], 0.0)
            link.step(g.memset(vmain[:, :, :], 0.0))
            g.memset(vtail[:, :, :], 0.0)
            link.settle()
            g.memset(vmain[:, :, :].rearrange("p b (h q) -> p (b h) q", q=Q)[:, :, DH:DH + 1], 1.0)\
             .then_inc(zeros_set, 1)

            def constants():
                link.step(g.memset(before[:, :], 1.0))
                link.step(g.memset(sel0, 0.0))
                link.step(g.memset(mask8[:, :], 1.0))
                link.step(g.memset(mask32[:, :], 1.0))
                for n in smask:
                    link.step(g.memset(smask[n][:, :, :], 1.0))
                link.step(g.memset(onef[:, :], 1.0))
                link.settle()
                link.step(g.affine_select(out=mask8[:, :], in_=mask8[:, :], compare_op=ALU.is_ge, fill=0.0,
                                          base=0, pattern=[[-DH, H]], channel_multiplier=1))
                m32 = mask32[:, :].rearrange("p (g h) -> p g h", g=2)
                link.step(g.affine_select(out=m32, in_=m32, compare_op=ALU.is_ge, fill=0.0,
                                          base=0, pattern=[[0, 2], [-Q, HG]], channel_multiplier=1))
                link.settle()
                link.step(g.affine_select(out=mask8[:, :], in_=mask8[:, :], compare_op=ALU.is_ge, fill=0.0,
                                          base=DH - 1, pattern=[[DH, H]], channel_multiplier=-1))
                link.step(g.affine_select(out=m32, in_=m32, compare_op=ALU.is_ge, fill=0.0,
                                          base=MT - 1, pattern=[[0, 2], [Q, HG]], channel_multiplier=-1))
                link.step(g.affine_select(out=before[:, :], in_=before[:, :], compare_op=ALU.is_gt, fill=0.0,
                                          base=0, pattern=[[1, P]], channel_multiplier=-1))
                link.step(g.affine_select(out=sel0, in_=sel0, compare_op=ALU.not_equal, fill=1.0,
                                          base=0, pattern=[[-1, H], [0, P]], channel_multiplier=1))
                for n in smask:
                    link.step(g.memset(smask[n][:, :, 0:1], 0.0))
                ex = dict(allow_small_or_imprecise_dtypes=True)
                link.step(g.iota(down8[:, :], pattern=[[-1, E]], base=E, channel_multiplier=0, **ex))
                link.step(g.iota(upto8[:, :], pattern=[[1, E]], base=0, channel_multiplier=0, **ex))
                link.step(g.iota(ebase[:, :], pattern=[[REG, E]], base=0, channel_multiplier=0, **ex))
                link.step(g.iota(thr[:, :], pattern=[[P, NT]], base=0, channel_multiplier=0, **ex))
                link.step(g.iota(tile_c[:, :], pattern=[[1, TILES]], base=0, channel_multiplier=0, **ex))
                link.settle()
                g.memset(row_buf[0][:, :, I_COL + 1:ROW], 0.0).then_inc(consts_set, 1)
                link.link(g.memset(row_buf[1][:, :, :], 0.0))
                g.iota(row_buf[1][:, :, I_COL:I_COL + 1].bitcast(I32), pattern=[[P, NT]],
                       base=K2 * TOKENS, channel_multiplier=1).then_inc(pads_set, 1)

            def late_constants():
                pool.wait_ge(pads_out, 16 * 2)
                for k in range(K2):
                    link.step(g.iota(row_buf[k][:, :, I_COL:I_COL + 1].bitcast(I32), pattern=[[P, NT]],
                                     base=k * TOKENS, channel_multiplier=1))
                pool.wait_ge(v_sb, 1)
                link.link(g.memset(vtail[:, :, :].rearrange("p b (h q) -> p (b h) q", q=Q)[:, :, DH:DH + 1], 1.0))
                for b in range(B):
                    tail = vtail[:, b, :].rearrange("p (h q) -> p h q", q=Q)
                    link.step(g.tensor_tensor(tail, tail, mask32[:, :].unsqueeze(2).to_broadcast([P, H, Q]),
                                              ALU.mult))
                link.settle()

            def rstd_of(u, var_sem, rstd_sem, n):
                pool.wait_ge(var_sem, n)
                g.tensor_tensor(rstd[u][:, :], ve[u][:, :], nhalf[:, 0:TU], ALU.pow).then_inc(rstd_sem, 1)

            def wide(name):
                return bc[name][:, :].unsqueeze(1).to_broadcast([P, TU, D])

            for step, n, u in pipeline(POOL_AT):
                b, k = n // 2, (n // 2) % U
                last = n - 2 * U + 1
                kv = kT[:, b, :]
                if step in ("ln0", "ln1", "ln2", "ln3", "ln4"):
                    rstd_of(u, ln_var[int(step[2])], ln_rstd[int(step[2])], n + 1)
                    if step == "ln0" and n == 0:
                        constants()
                elif step == "late" and n == 0:
                    late_constants()
                elif step == "kbr" and n % 2 == 0:
                    if b == 0:
                        pool.wait_ge(k_sb, 2)
                    if b >= U:
                        pool.wait_ge(s_ps[1], (last + 1) * 4)
                    g.tensor_tensor(kbr[k][:, :, :], kv[:, 0:M].unsqueeze(1).to_broadcast([P, H, M]),
                                    mask8[:, :].unsqueeze(2).to_broadcast([P, H, M]), ALU.mult)\
                     .then_inc(kbr_set, 1)
                elif step == "kb" and n % 2 == 0:
                    if b >= U:
                        pool.wait_ge(st_ps[4], last + 1)
                    for at, m in ((0, P), (P, Q)):
                        g.tensor_tensor(kb[k][:, H * at:H * (at + m)].rearrange("p (h m) -> p h m", h=H),
                                        kv[:, at:at + m].unsqueeze(1).to_broadcast([P, H, m]),
                                        mask8[:, :].unsqueeze(2).to_broadcast([P, H, m]), ALU.mult)\
                         .then_inc(kb_set, 1)
                elif step == "vv" and n % 2 == 0:
                    if b >= U:
                        pool.wait_ge(av_ps[1], last + 1)
                    g.tensor_copy(vm[k][:, :], vmain[:, b, :]).then_inc(kb_set, 1)
                    g.tensor_copy(vt[k][:, :], vtail[:, b, :]).then_inc(kb_set, 1)
                elif step == "h0b":
                    if n == 0:
                        pool.wait_ge(in_vec, 16 * N_VEC)
                    pool.wait_ge(h0_set, n + 1)
                    g.tensor_tensor(h0b[u][:, :, :], h0[u][:, :, :], wide("sab"), ALU.add).then_inc(h0b_set, 1)
                elif step == "x0b":
                    if n == 0:
                        pool.wait_ge(in_rest, 16 * N_REST)
                    xs = x_all[:, n * TU:(n + 1) * TU, :]
                    g.tensor_tensor(xs, xs, wide("b3"), ALU.add).then_inc(x0b_set, 1)
                elif step == "fold":
                    pool.wait_ge(in_w1, 16 * E)
                    pool.wait_ge(in_gate, 16 * (n // GH + 1))
                    ins = g.tensor_tensor(w1g[:, n, 0:F], w1g[:, n, 0:F],
                                          gate_bc[:, (n % GH) * F:(n % GH + 1) * F], ALU.mult)
                    if n % GH == GH - 1:
                        ins.then_inc(gate_used, 1)
                elif step[0:2] == "sc" and n in ROUTED and int(step[2]) < K2 * len(ROUTED[n]):
                    t, c = ROUTED[n][0] + int(step[2]) // K2, int(step[2]) % K2
                    if step == "sc0":
                        pool.wait_ge(slots_set, nth[n] + 1)
                        pool.wait_ge(row_set, n + 1)
                    pool.indirect_dma_start(rows[:, :], bass.IndirectOffsetOnAxis(idx[:, c, t:t + 1], 0),
                                            row_buf[c][:, t, :], None).then_inc(rows_out, 16)
                elif step == "row":
                    pool.wait_ge(n_set, n + 1)
                    g.tensor_copy(row_buf[1][:, n * TU:(n + 1) * TU, 0:D], row_buf[0][:, n * TU:(n + 1) * TU, 0:D])\
                     .then_inc(row_set, 1)

            pool.wait_ge(cnti_set, 1)
            for e in range(EP, E):
                pad_rows(pool, e, pool_pads)
            for b in range(B):
                xs = x_all[:, b * TB:(b + 1) * TB, :]
                g.tensor_tensor(xs, xs, bc["b4"][:, :].unsqueeze(1).to_broadcast([P, TB, D]), ALU.add)\
                 .then_inc(xb_set, 1)

            def store_tile(turn, k):
                pool.wait_ge(y_set[k], turn + 1)
                apart(pool)
                pool.indirect_dma_start(
                    results[:, :], bass.IndirectOffsetOnAxis(xt[k][:, I_COL:I_COL + 1].bitcast(U32), 0),
                    yt[k], None).then_inc(y_out[k], 16)

            with pool.Fori(0, ETURNS) as it:
                for k in range(RU):
                    store_tile(it, k)
            for k in range(TILES - ETURNS * RU):
                store_tile(ETURNS, k)
            def gained(n):
                pool.wait_ge(z_set, n + 1)
                z = y[n % NS][:, :, :]
                g.tensor_tensor(z, z, wide("g4"), ALU.mult).then_inc(zg_set, 1)

            for n in range(G):
                rstd_of(n % NS, cv_var, cv_rstd, n + 1)
                if n:
                    gained(n - 1)
            gained(G - 1)

        @block.scalar
        def _(act):
            a = nc.scalar
            rows_of = lambda vec: vec.rearrange("(c p) -> c p", p=P)
            for at, src in ((0, rows_of(qkv_b)), (R_IN, rows_of(in_proj_b)), (R_L1, rows_of(lin1_b)),
                            (R_SG, rows_of(sgate)), (R_SB, rows_of(sb1)),
                            (R_B1, b1.rearrange("e (c p) -> (e c) p", p=P)),
                            (R_G, gate.rearrange("e (c p) -> (e c) p", p=P))):
                act.dma_start(vrow[at:at + src.shape[0], :], src).then_inc(in_row, 16)
            for name, vec in (("vb2", in_proj_b[2 * D:3 * D]), ("sab", sa_out_b), ("g1", ln1_g), ("b1", ln1_b)):
                act.dma_start(bc[name][:, :], vec.partition_broadcast(P)).then_inc(in_vec, 16)

            def prepare():
                act.wait_ge(qb_set, 1)
                act.wait_ge(zeros_set, 1)
                for k in range(2):
                    act.wait_ge(k_ps, k + 1)
                    a.activation(kT[:, 2 * k:2 * k + 2, 0:M],
                                 bank[1][k][:, 0:2 * M].rearrange("p (b m) -> p b m", b=2),
                                 ACT.Identity, bias=col_bk2[:, :]).then_inc(k_sb, 1)
                for k in range(1, 4):
                    act.wait_ge(wt_ps, k + 1)
                    n = min(4, NTR - 4 * k)
                    a.copy(wt[:, 4 * k:4 * k + n, :],
                           bank[0][k][:, 0:n * P].rearrange("p (k c) -> p k c", c=P)).then_inc(wt_act, 1)

            def sigmoid_part():
                act.wait_ge(in_rest, 16 * N_REST)
                a.activation(sig[:, :], col_sw[:, :], ACT.Exp, scale=-1.0).then_inc(act_prep, 1)

            def evacuate(g, nth, src, dst):
                act.wait_ge(tr_ps[nth], g + 1)
                a.copy(dst, src).then_inc(tr_sb[nth], 1)

            def normed(u, src, dst, done):
                for t in range(TU):
                    ins = a.activation(dst(t), src(t), ACT.Identity, bias=nmr[u][:, t:t + 1],
                                       scale=rstd[u][:, t:t + 1])
                ins.then_inc(done, 1)

            for step, g, u in pipeline(ACT_AT):
                A, Bk = duo[u]
                if step == "prep":
                    if g == 0:
                        prepare()
                elif step == "sig":
                    if g == 0:
                        sigmoid_part()
                elif step in ("h0T", "x1T", "caT", "x2T"):
                    evacuate(g, ("h0T", "x1T", "caT", "x2T").index(step), A[:, 0:UL], actT[u][:, :])
                elif step == "esc":
                    act.wait_ge(sc_set, g + 1)
                    for t in range(TU):
                        ins = a.activation(esc[u][:, t:t + 1], sdot[u][:, t:t + 1], ACT.Exp,
                                           bias=nsc[u][:, t:t + 1], scale=float(D) ** 0.5)
                    ins.then_inc(esc_set, 1)
                elif step == "h0":
                    act.wait_ge(nmr0_set, g + 1)
                    normed(u, lambda t: x_all[:, g * TU + t, :], lambda t: h0[u][:, t, :], h0_set)
                elif step == "q":
                    act.wait_ge(q_ps, g + 1)
                    for ap in (qT[u], qTr[u]):
                        ins = a.activation(ap[:, :], A[:, UL:2 * UL], ACT.Identity, bias=col_bqs[:, :],
                                           scale=float(DH) ** -0.5)
                    ins.then_inc(q_sb, 1)
                elif step == "nm":
                    act.wait_ge(nm_ps, g + 1)
                    a.copy(nmT[u][0:H, :], A[0:H, 0:UL]).then_inc(nm_sb, 1)
                elif step == "n":
                    act.wait_ge(nmr4_set, g + 1)
                    normed(u, lambda t: x_all[:, g * TU + t, :], lambda t: row_buf[0][:, g * TU + t, 0:D], n_set)
                elif step in ("e0", "e1", "e2", "e3", "e4"):
                    n = int(step[1])
                    slot = (0, 2, 4, 0, 2)[n]
                    act.wait_ge(st_ps[n], g + 1)
                    a.activation(pT[u][:, slot:slot + 2, :].rearrange("p g n -> p (g n)"),
                                 (A, Bk, A, A, Bk)[n], ACT.Exp).then_inc(e_set[n], 1)
                elif step in ("av0", "av1"):
                    gr = int(step[2])
                    act.wait_ge(av_ps[gr], g + 1)
                    a.copy(av[u][gr], (Bk, A)[gr][:, 0:UL]).then_inc(av_sb[gr], 1)
                elif step == "relu":
                    for c in range(FFC):
                        if c % 2 == 0:
                            act.wait_ge(l1_ps, g * (FFC // 2) + c // 2 + 1)
                        a.activation(pT[u][:, c, :], (A, Bk)[c // 2][:, c % 2 * UL:(c % 2 + 1) * UL], ACT.Relu,
                                     bias=col_l1b[:, c:c + 1]).then_inc(l1_sb, 1)
                elif step == "pr" and g in ROUTED:
                    act.wait_ge(max0_set, nth[g] + 1)
                    cols = slice(0, len(ROUTED[g]) * E)
                    a.activation(pr[:, cols], lgm[:, cols], ACT.Exp).then_inc(ex_set, 1)
                elif step == "nT":
                    evacuate(g, 4, Bk[:, 0:UL], actT[u][:, :])
                    a.copy(flat3(nT_all[:, g * TU:(g + 1) * TU, :]), Bk[:, 0:UL]).then_inc(nT_set, 1)
            def gelu_hidden(b):
                act.wait_ge(hs_ps, b + 1)
                for c in range(FSC):
                    ins = a.activation(hs[b % 2][:, c, :], hid_bank[b][c], ACT.Gelu,
                                       bias=col_sbg[:, c:c + 1], scale=col_sg[:, c:c + 1])
                ins.then_inc(hs_set, 1)

            def weigh_shared(b):
                act.wait_ge(sh_ps, b + 1)
                a.activation(flat3(nT_all[:, b * TB:(b + 1) * TB, :]), sh_bank[b], ACT.Identity,
                             scale=sig[:, :]).then_inc(sh_set, 1)

            gelu_hidden(0)
            for b in range(1, B):
                gelu_hidden(b)
                weigh_shared(b - 1)
            weigh_shared(B - 1)

            def gelu_tile(j, k):
                for c in range(FC):
                    if c % 2 == 0:
                        act.wait_ge(up_ps, j * (FC // 2) + c // 2 + 1)
                    a.activation(hT[k % 2][:, c * P:(c + 1) * P],
                                 bank[k % 2][1 + c // 2][:, c % 2 * P:(c % 2 + 1) * P], ACT.Gelu,
                                 bias=wbuf[:, k % WB, F + c:F + c + 1]).then_inc(h_set, 1)

            with act.Fori(0, ETURNS) as it:
                for k in range(RU):
                    gelu_tile(it * RU + k, k)
            for k in range(TILES - ETURNS * RU):
                gelu_tile(ETURNS * RU + k, k)
            for g in range(G):
                act.wait_ge(cv_nmr, g + 1)
                if g >= NS:
                    act.wait_ge(fin_set, g - NS + 1)
                normed(g % NS, lambda t: psum[:, g, t * D:(t + 1) * D], lambda t: y[g % NS][:, t, :], z_set)

        @block.vector
        def _(dve):
            v = nc.vector
            link = Chain(dve, dve_link)
            link.link(v.memset(one2[:, :].bitcast(F32), 0.0))
            link.step(v.memset(one2[0:2, :].bitcast(F32), 1.0))
            for u in range(NS):
                v.memset(nmT[u][:, :].bitcast(F32), 0.0)

            def high_and_rest(at, n, done):
                cols = slice(at, at + n)
                link.link(v.tensor_copy(brow[0:2, cols], row32[:, cols]))
                v.scalar_tensor_tensor(out=brow[0:2, cols], in0=brow[0:2, cols].bitcast(F32), scalar=mrow[:, :],
                                       in1=row32[:, cols], op0=ALU.mult, op1=ALU.add).then_inc(done, 1)

            def prepare():
                dve.wait_ge(vc_ps, 1)
                link.link(v.tensor_copy(vcol[:, :], bank[1][3][:, 0:NR]))
                v.tensor_scalar(col_bqs[:, :], col_bq2, float(DH) ** -0.5, None, ALU.mult)
                v.tensor_copy(qkvb2[:, :, :], vcol[:, 0:3].unsqueeze(2).to_broadcast([P, 3, 2])).then_inc(qb_set, 1)
                dve.wait_ge(wt_ps, 1)
                v.tensor_copy(wt[:, 0:4, :], bank[0][0].rearrange("p (k c) -> p k c", c=P)).then_inc(wt_sb, 1)
                dve.wait_ge(zeros_set, 1)
                for k in range(2):
                    dve.wait_ge(cT_ps, k + 1)
                    src = bank[1][k][:, 0:2 * M].rearrange("p (b m) -> p b m", b=2)
                    v.tensor_copy(cT[:, 2 * k:2 * k + 2, :], src)
                    v.tensor_copy(cTr[:, 2 * k:2 * k + 2, :, 0:MT],
                                  src[:, :, P:M].unsqueeze(2).to_broadcast([P, 2, HG, MT])).then_inc(cT_sb, 1)
                dve.wait_ge(mm_pr, 1)
                link.link(v.tensor_copy(row32[:, C_QK:C_QK + 2 * D], bank[1][3][0:2, 0:2 * D]))
                high_and_rest(C_QK, 2 * D, brow_set)
                v.tensor_copy(mm[:, :], bank[1][2][:, 0:2 * D]).then_inc(mm_sb, 1)

            def prepare_rest():
                wide = lambda at: vcol[:, at:at + E * FC].rearrange("p (e c) -> p e c", c=FC)
                v.tensor_tensor(w1g[:, :, F:WE], wide(R_B1), wide(R_G), ALU.mult)
                bv = bc["vb2"][:, :].rearrange("p (h d) -> p h d", d=DH)
                dve.wait_ge(in_vec, 16 * N_VEC)
                dve.wait_ge(v_ps, 2)
                for b in range(B):
                    for k, dst in enumerate((vmain, vtail)):
                        ins = v.tensor_tensor(dst[:, b, :].rearrange("p (h q) -> p h q", q=Q)[:, :, 0:DH],
                                              bank[1][3 - k][:, b * D:(b + 1) * D]
                                              .rearrange("p (h d) -> p h d", d=DH), bv, ALU.add)
                ins.then_inc(v_sb, 1)

            def finish_preparing():
                dve.wait_ge(in_rest, 16 * N_REST)
                high_and_rest(0, C_QK, brow_set)
                dve.wait_ge(consts_set, 1)
                v.tensor_copy(sel[:, :, :], sel0)
                link.link(v.tensor_copy(selt[:, :, :], sel0[:, :, 0:Q]))
                v.memset(selt[:, :, MT:Q].bitcast(F32), 0.0).then_inc(sel_set, 1)
                link.step(v.tensor_tensor(col_sbg[:, :], vcol[:, R_SB:R_B1], col_sg, ALU.mult))
                dve.wait_ge(act_prep, 1)
                link.link(v.tensor_scalar(sig[:, :], sig[:, :], 1.0, None, ALU.add))
                link.step(v.reciprocal(sig[:, :], sig[:, :]))
                r.link(v.tensor_copy(base[:, :], ebase[:, :]))

            def stats(u, src, var_sem, link):
                for t in range(TU):
                    link.step(v.bn_stats(st[u][:, t, :], src(t)))
                link.settle()
                for t in range(TU):
                    link.step(v.bn_aggr(mv[u][:, t, :], st[u][:, t, :]))
                link.settle()
                v.tensor_scalar(ve[u][:, :], mv[u][:, :, 1], EPS, None, ALU.add).then_inc(var_sem, 1)

            def shift(u, done):
                v.scalar_tensor_tensor(out=nmr[u][:, :], in0=mv[u][:, :, 0], scalar=-1.0, in1=rstd[u][:, :],
                                       op0=ALU.mult, op1=ALU.mult).then_inc(done, 1)

            def scaled(u, src, gain):
                for t in range(TU):
                    link.step(v.scalar_tensor_tensor(out=y[u][:, t, :], in0=src(t), scalar=mv[u][:, t, 0:1],
                                                     in1=bc[gain][:, :], op0=ALU.subtract, op1=ALU.mult))

            def shifted(u, bias, dst):
                for t in range(TU):
                    ins = v.scalar_tensor_tensor(out=dst(t), in0=y[u][:, t, :], scalar=rstd[u][:, t:t + 1],
                                                 in1=bias(t), op0=ALU.mult, op1=ALU.add)
                return ins

            r = Chain(dve, dve_rout)

            class Group:

                def __init__(self, g):
                    self.tiles, self.i, n = ROUTED[g], nth[g], len(ROUTED[g])
                    self.n, self.cols, self.own = n, slice(0, n * E), slice(self.tiles[0], self.tiles[0] + n)

                def by_tile(self, ap):
                    return ap[:, self.cols].rearrange("p (t e) -> p t e", e=E)

                def by_expert(self, ap):
                    return ap[:, self.cols].rearrange("p (e t) -> p e t", t=self.n)

                def over_e(self, ap):
                    return ap[:, 0:self.n].unsqueeze(2).to_broadcast([P, self.n, E])

                def of_e(self, ap):
                    return ap.unsqueeze(1).to_broadcast([P, self.n, E])

            def less_maximum(q):
                r.link(v.tensor_reduce(m0[:, 0:q.n], lg_all[:, q.own, :], AX.X, ALU.max))
                v.tensor_tensor(q.by_tile(lgm), lg_all[:, q.own, :], q.over_e(m0), ALU.subtract).then_inc(max0_set, 1)

            def pick_experts(q):
                te, n = q.by_tile, slice(0, q.n)
                dve.wait_ge(ex_set, q.i + 1)
                r.link(v.tensor_reduce(ssum[:, n], te(pr), AX.X, ALU.add))
                r.link(v.reciprocal(rs4[:, n], ssum[:, n]))
                r.link(v.tensor_tensor(te(pr), te(pr), q.over_e(rs4), ALU.mult))
                for k in range(K2):
                    r.link(v.tensor_reduce(wk[k][:, n], te(pr), AX.X, ALU.max))
                    r.link(v.tensor_tensor(te(key), te(pr), q.over_e(wk[k]), ALU.is_equal))
                    r.link(v.tensor_tensor(te(key), te(key), q.of_e(down8[:, :]), ALU.mult))
                    r.link(v.tensor_reduce(kmax[:, n], te(key), AX.X, ALU.max))
                    r.link(v.tensor_tensor(te(oh[k]), te(key), q.over_e(kmax), ALU.is_equal))
                    if k == 0:
                        r.link(v.scalar_tensor_tensor(out=pr[:, q.cols], in0=oh[0][:, q.cols], scalar=-4.0,
                                                      in1=pr[:, q.cols], op0=ALU.mult, op1=ALU.add))
                v.tensor_tensor(picks[:, q.cols], oh[0][:, q.cols], oh[1][:, q.cols], ALU.add).then_inc(picks_set, 1)
                r.link(v.tensor_tensor(ws[:, n], wk[0][:, n], wk[1][:, n], ALU.add))
                r.link(v.reciprocal(wrs[:, n], ws[:, n]))
                for k in range(K2):
                    r.step(v.tensor_tensor(row_buf[k][:, q.own, W_COL:W_COL + 1].rearrange("p t o -> p (t o)"),
                                           wk[k][:, n], wrs[:, n], ALU.mult))

            def place_tokens(q, rank):
                ranks = rank[:, 0:q.n * E].rearrange("p (t e) -> p t e", e=E)
                sums = rank[:, q.n * E:2 * q.n * E].rearrange("p (t e) -> p e t", e=E)
                dve.wait_ge(rank_ps, q.i + 1)
                r.link(v.tensor_copy(q.by_expert(tot), sums))
                r.link(v.tensor_tensor_scan(incl[:, q.cols], smask[q.n][:, :, :].rearrange("p e t -> p (e t)"),
                                            tot[:, q.cols], 0.0, ALU.mult, ALU.add))
                r.link(v.tensor_tensor(tmp[:, q.cols], incl[:, q.cols], tot[:, q.cols], ALU.subtract))
                r.link(v.tensor_tensor(q.by_tile(slot), ranks,
                                       tmp[:, q.cols].rearrange("p (e t) -> p t e", t=q.n), ALU.add))
                r.link(v.tensor_tensor(q.by_tile(slot), q.by_tile(slot), q.of_e(base[:, :]), ALU.add))
                r.step(v.tensor_tensor(base[:, :].unsqueeze(2), base[:, :].unsqueeze(2),
                                       q.by_expert(incl)[:, :, q.n - 1:q.n], ALU.add))
                for k in range(K2):
                    r.link(v.tensor_tensor(key[:, q.cols], slot[:, q.cols], oh[k][:, q.cols], ALU.mult))
                    r.link(v.tensor_reduce(sl4[:, 0:q.n], q.by_tile(key), AX.X, ALU.add))
                    ins = v.tensor_copy(idx[:, k, q.own], sl4[:, 0:q.n])
                    if k < K2 - 1:
                        r.link(ins)
                ins.then_inc(slots_set, 1)

            for step, g, u in pipeline(DVE_AT):
                A, Bk = duo[u]
                tile = lambda t: x_all[:, g * TU + t, :]
                yu = lambda t: y[u][:, t, :]
                if step == "prep1":
                    if g == 0:
                        prepare()
                elif step == "prep2":
                    if g == 0:
                        prepare_rest()
                elif step == "prep3":
                    if g == 0:
                        finish_preparing()
                elif step == "ln0":
                    if g == 0:
                        dve.wait_ge(in_x0, 16)
                    elif g == TB // TU:
                        dve.wait_ge(in_x, 16 * (B - 1))
                    stats(u, tile, ln_var[0], link)
                elif step == "h0":
                    dve.wait_ge(ln_rstd[0], g + 1)
                    shift(u, nmr0_set)
                elif step == "dot":
                    dve.wait_ge(mm_ps, g + 1)
                    for t in range(TU):
                        link.step(v.tensor_tensor_reduce(
                            out=junk[(u + 2 * t) % NS][:, :], in0=h0[u][:, t, :],
                            in1=Bk[:, t * 2 * D:t * 2 * D + D],
                            scale=1.0, scalar=0.0, op0=ALU.mult, op1=ALU.add, accum_out=sdot[u][:, t:t + 1]))
                    link.settle()
                    v.tensor_scalar(nsc[u][:, :], sdot[u][:, :], -float(D) ** 0.5, None, ALU.mult)\
                     .then_inc(sc_set, 1)
                elif step == "y1":
                    dve.wait_ge(esc_set, g + 1)
                    link.link(v.reciprocal(rsc[u][:, :], esc[u][:, :]))
                    link.link(v.tensor_tensor(psc[u][:, :], esc[u][:, :], rsc[u][:, :], ALU.mult))
                    dve.wait_ge(h0b_set, g + 1)
                    for t in range(TU):
                        link.step(v.scalar_tensor_tensor(out=yu(t), in0=Bk[:, t * 2 * D + D:(t + 1) * 2 * D],
                                                         scalar=psc[u][:, t:t + 1], in1=h0b[u][:, t, :],
                                                         op0=ALU.mult, op1=ALU.add))
                    link.settle()
                    stats(u, yu, ln_var[1], link)
                    scaled(u, yu, "g1")
                elif step == "x1":
                    dve.wait_ge(ln_rstd[1], g + 1)
                    link.settle()
                    shifted(u, lambda t: bc["b1"][:, :], lambda t: x1[u][:, t, :]).then_inc(x1_set, 1)
                elif step in ("m0", "m1"):
                    t = int(step[1])
                    for k in range(H // 2):
                        dve.wait_ge(s_ps[t], g * 4 + k + 1)
                        v.tensor_reduce(nmax[u][:, t, 2 * k:2 * k + 2],
                                        duo[u][k % 2][:, 0:2 * M].rearrange("p (j m) -> p j m", j=2),
                                        AX.X, ALU.max, negate=True).then_inc(max_set[t], 1)
                elif step == "ca":
                    dve.wait_ge(avT_ps, g + 1)
                    o = Bk.rearrange("p (a q) -> p a q", q=Q)
                    den = rden[u][:, :, :].rearrange("p t h -> p (t h)").unsqueeze(2)
                    link.link(v.reciprocal(den, o[:, :, DH:DH + 1]))
                    v.tensor_tensor(y[u][:, :, :].rearrange("p t (h d) -> p (t h) d", d=DH), o[:, :, 0:DH],
                                    den.to_broadcast([P, TU * H, DH]), ALU.mult).then_inc(ca_set, 1)
                elif step == "y2":
                    dve.wait_ge(y2_ps, g + 1)
                    stats(u, lambda t: Bk[:, t * D:(t + 1) * D], ln_var[2], link)
                    scaled(u, lambda t: Bk[:, t * D:(t + 1) * D], "g2")
                elif step == "x2":
                    dve.wait_ge(ln_rstd[2], g + 1)
                    link.settle()
                    shifted(u, lambda t: bc["b2"][:, :], lambda t: x2[u][:, t, :]).then_inc(x2_set, 1)
                elif step == "y3":
                    dve.wait_ge(y3_ps, g + 1)
                    stats(u, lambda t: A[:, t * D:(t + 1) * D], ln_var[3], link)
                    scaled(u, lambda t: A[:, t * D:(t + 1) * D], "g3")
                elif step == "xr":
                    dve.wait_ge(x0b_set, g + 1)
                    dve.wait_ge(ln_rstd[3], g + 1)
                    link.settle()
                    link.link(shifted(u, tile, tile))
                    stats(u, tile, ln_var[4], link)
                elif step == "n":
                    dve.wait_ge(ln_rstd[4], g + 1)
                    shift(u, nmr4_set)
                elif step == "lg":
                    dve.wait_ge(lg_ps, g + 1)
                    v.tensor_copy(lg_all[:, g * TU:(g + 1) * TU, :],
                                  A[:, 0:TU * E].rearrange("p (t e) -> p t e", e=E)).then_inc(lg_set, 1)
                elif step == "r0" and g in ROUTED:
                    dve.wait_ge(lg_set, g + 1)
                    less_maximum(Group(g))
                elif step == "r1" and g in ROUTED:
                    pick_experts(Group(g))
                elif step == "r2" and g in ROUTED:
                    place_tokens(Group(g), A)

            r.settle()
            r.link(v.tensor_tensor(cnt, base[:, :], ebase[:, :], ALU.subtract))
            v.tensor_copy(cnti[:, :], cnt).then_inc(cnti_set, 1)
            r.link(v.tensor_tensor(cmp.rearrange("p (e t) -> p e t", e=E), cnt.unsqueeze(2).to_broadcast([P, E, NT]),
                                   thr[:, :].unsqueeze(1).to_broadcast([P, E, NT]), ALU.is_gt))
            r.link(v.tensor_reduce(ntl, cmp.rearrange("p (e t) -> p e t", e=E), AX.X, ALU.add))
            r.link(v.tensor_tensor_scan(tend, onef[:, 0:E], ntl, 0.0, ALU.mult, ALU.add))
            r.step(v.tensor_tensor(tcmp, tend.unsqueeze(1).to_broadcast([P, TILES, E]),
                                   tile_c[:, :].unsqueeze(2).to_broadcast([P, TILES, E]), ALU.is_le))
            r.link(v.tensor_tensor(tval, tend, ntl, ALU.subtract))
            r.step(v.tensor_reduce(teid, tcmp, AX.X, ALU.add))
            r.link(v.scalar_tensor_tensor(out=tval, in0=tval, scalar=-float(P), in1=ebase[:, :],
                                          op0=ALU.mult, op1=ALU.add))
            r.link(v.tensor_tensor(tcmp, teid.unsqueeze(2).to_broadcast([P, TILES, E]),
                                   upto8[:, :].unsqueeze(1).to_broadcast([P, TILES, E]), ALU.is_equal))
            r.link(v.tensor_tensor(tcmp, tcmp, tval.unsqueeze(1).to_broadcast([P, TILES, E]), ALU.mult))
            r.link(v.tensor_reduce(toff, tcmp, AX.X, ALU.add))
            r.step(v.scalar_tensor_tensor(out=toff, in0=tile_c[:, :], scalar=float(P), in1=toff,
                                          op0=ALU.mult, op1=ALU.add))
            r.link(v.tensor_scalar(tdum, teid, float(E), None, ALU.is_ge))
            r.link(v.scalar_tensor_tensor(out=toff, in0=tdum, scalar=float(E * REG - K2 * NT * P), in1=toff,
                                          op0=ALU.mult, op1=ALU.add))
            r.link(v.tensor_scalar(teid, teid, float(E - 1), None, ALU.min))
            r.link(v.tensor_copy(meta[:, 1, :], toff))
            v.tensor_copy(meta[:, 0, :], teid).then_inc(meta_set, 1)
            def copy_weights(j, k):
                e = dve.value_load(meta[0:1, 0, bass.ds(j, 1)], min_val=0, max_val=E - 1)
                v.tensor_copy(wbuf[:, k % WB, :], w1g[:, bass.ds(e, 1), :].rearrange("p e c -> p (e c)"))\
                 .then_inc(w_sb, 1)

            def copy_tokens(j, k):
                dve.wait_ge(xt_ps, j + 1)
                v.tensor_copy(xtT[k % 2], bank[k % 2][0][:, 0:P]).then_inc(xt_sb, 1)

            def weigh(j, k):
                dve.wait_ge(dn_ps, j + 1)
                v.tensor_scalar(yt[k % RU], bank[k % 2][3][:, 0:D], xt[k % RU][:, W_COL:W_COL + 1], None,
                                ALU.mult).then_inc(y_set[k % RU], 1)

            def dve_step(j, k):
                copy_tokens(j + 1, k + 1)
                weigh(j - 1, k - 1)
                copy_weights(j + 2, k + 2)

            dve.wait_ge(meta_set, 1)
            dve.wait_ge(gate_used, E // GH)
            for j in range(WB - 1):
                copy_weights(j, j)
            copy_tokens(0, 0)
            copy_tokens(1, 1)
            copy_weights(2, 2)
            with dve.Fori(0, ETURNS) as it:
                for k in range(1, RU + 1):
                    dve_step(it * RU + k, k)
            for j in range(ETURNS * RU + 1, TILES - 2):
                dve_step(j, j)
            copy_tokens(TILES - 1, TILES - 1)
            for j in range(TILES - 3, TILES):
                weigh(j, j)
            def start(g):
                dve.wait_ge(sum_ps, g + 1)
                stats(g % NS, lambda t: psum[:, g, t * D:(t + 1) * D], cv_var, link)

            def middle(g):
                dve.wait_ge(cv_rstd, g + 1)
                shift(g % NS, cv_nmr)

            def finish(g):
                dve.wait_ge(zg_set, g + 1)
                dve.wait_ge(xb_set, B)
                own = slice(g * TU, (g + 1) * TU)
                v.tensor_tensor(res[0][:, own, :], y[g % NS][:, :, :], x_all[:, own, :], ALU.add).then_inc(fin_set, 1)

            for g in range(G + 2):
                if g < G:
                    start(g)
                if 0 < g <= G:
                    middle(g - 1)
                if g > 1:
                    finish(g - 2)

        @block.tensor
        def _(pe):
            t_ = nc.tensor

            def mul(out, lhsT, rhs, start=True, stop=True):
                return t_.matmul(out, lhsT, rhs, start=start, stop=stop, skip_group_check=True)

            def prepare():
                pe.wait_ge(ident_set, 1)
                pe.wait_ge(in_row, 16 * N_ROW)
                t_.transpose(bank[1][3][:, 0:NR], vrow[:, :], ident[0:NR, 0:NR]).then_inc(vc_ps, 1)
                pe.wait_ge(in_w, 16 * 3)
                for i, w in enumerate((wsao, winp[:, 0], winp[:, 1], winp[:, 2])):
                    ins = t_.transpose(bank[0][0][:, i * P:(i + 1) * P], w, ident[:, :])
                ins.then_inc(wt_ps, 1)
                pe.wait_ge(in_ctx, 16 * 2)
                for b in range(B):
                    at = (b % 2) * M
                    t_.transpose(bank[1][b // 2][:, at:at + P], ctx_main[:, b, :], ident[:, :])
                    ins = t_.transpose(bank[1][b // 2][:, at + P:at + M], ctx_tail[:, b, :], ident[0:MT, 0:MT])
                    if b % 2:
                        ins.then_inc(cT_ps, 1)
                pe.wait_ge(qb_set, 1)
                pe.wait_ge(wt_sb, 1)
                mul(bank[1][2][:, 0:D], wqkv[:, 0], wqkv[:, 1])
                mul(bank[1][2][:, D:2 * D], wqkv[:, 2], wt[:, T_SAO, :])
                mul(bank[1][3][0:2, 0:D], qkvb2[:, 1, :], wqkv[:, 0], stop=False)
                mul(bank[1][3][0:2, 0:D], qkvb2[:, 0, :], wqkv[:, 1], start=False)
                mul(bank[1][3][0:2, D:2 * D], qkvb2[:, 2, :], wt[:, T_SAO, :]).then_inc(mm_pr, 1)

            def prepare_rest():
                for k in range(2):
                    pe.wait_ge(cT_sb, k + 1)
                    mul(bank[1][k][:, 0:2 * M], wt[:, T_K, :],
                        cT[:, 2 * k:2 * k + 2, :].rearrange("p b m -> p (b m)")).then_inc(k_ps, 1)
                pe.wait_ge(mm_sb, 1)
                for b in range(B):
                    ins = mul(bank[1][3][:, b * D:(b + 1) * D], cT[:, b, 0:P], wt[:, T_V, :])
                ins.then_inc(v_ps, 1)
                for b in range(B):
                    ins = mul(bank[1][2][:, b * D:(b + 1) * D], cTr[:, b, :, :].rearrange("p r m -> p (r m)"),
                              wt[:, T_V, :])
                ins.then_inc(v_ps, 1)
                pe.wait_ge(in_l, 16 * 3)
                weights = [wmo] + [wl1[:, c] for c in range(FFC)] + [wl2[:, c * P:(c + 1) * P] for c in range(FFC)]
                for i, w in enumerate(weights, 4):
                    ins = t_.transpose(bank[0][i // 4][:, (i % 4) * P:(i % 4 + 1) * P], w, ident[:, :])
                    if i % 4 == 3 or i == NTR - 1:
                        ins.then_inc(wt_ps, 1)

            def turned(out, src, done):
                for t in range(TU):
                    ins = t_.transpose(out[:, t * P:(t + 1) * P], src(t), ident[:, :])
                ins.then_inc(done, 1)

            def biased(out, at, n, stop=False):
                return mul(out, one2[:, :], brow[:, at:at + n], stop=stop)

            def hidden(b):
                for c in range(FSC):
                    ins = mul(hid_bank[b][c], sw1s[:, c * P:(c + 1) * P], flat3(nT_all[:, b * TB:(b + 1) * TB, :]))
                ins.then_inc(hs_ps, 1)

            def shared(b):
                pe.wait_ge(hs_set, b + 1)
                if b >= 2:
                    pe.wait_ge(sh_set, b - 1)
                for t in range(TB):
                    o = sh_bank[b][:, t * P:(t + 1) * P]
                    biased(o, C_SB2, D)
                    for c in range(FSC):
                        ins = mul(o, hs[b % 2][:, c, t * P:(t + 1) * P], sw2s[:, c, :],
                                  start=False, stop=c == FSC - 1)
                ins.then_inc(sh_ps, 1)

            for step, g, u in pipeline(PE_AT):
                A, Bk = duo[u]
                b, k = g // 2, (g // 2) % U
                columns = lambda t: slice(t * P, (t + 1) * P)
                if step == "prep1":
                    if g == 0:
                        prepare()
                elif step == "prep2":
                    if g == 0:
                        prepare_rest()
                elif step == "h0T":
                    if g >= NS:
                        pe.wait_ge(nT_set, g - NS + 1)
                        pe.wait_ge(lg_set, g - NS + 1)
                        if g - NS in ROUTED:
                            pe.wait_ge(slots_set, nth[g - NS] + 1)
                    pe.wait_ge(h0_set, g + 1)
                    turned(A, lambda t: h0[u][:, t, :], tr_ps[0])
                elif step == "mm":
                    pe.wait_ge(tr_sb[0], g + 1)
                    if g == 0:
                        pe.wait_ge(brow_set, 1)
                        pe.wait_ge(wt_act, 3)
                    for t in range(TU):
                        o = Bk[:, t * 2 * D:(t + 1) * 2 * D]
                        biased(o, C_QK, 2 * D)
                        ins = mul(o, actT[u][:, columns(t)], mm[:, :], start=False)
                    ins.then_inc(mm_ps, 1)
                elif step == "x1T":
                    pe.wait_ge(x1_set, g + 1)
                    turned(A, lambda t: x1[u][:, t, :], tr_ps[1])
                elif step == "q":
                    pe.wait_ge(tr_sb[1], g + 1)
                    mul(A[:, UL:2 * UL], wt[:, T_Q, :], actT[u][:, :]).then_inc(q_ps, 1)
                elif step in ("s0", "s1"):
                    t = int(step[1])
                    if t == 0:
                        pe.wait_ge(q_sb, g + 1)
                        pe.wait_ge(kbr_set, b + 1)
                    for i in range(H // 2):
                        if i > 1:
                            pe.wait_ge(max_set[t], g * 4 + i - 1)
                        elif t:
                            pe.wait_ge(max_set[0], g * 4 + i + 3)
                        mul(duo[u][i % 2][:, 0:2 * M], qTr[u][:, columns(t)],
                            kbr[k][:, 2 * i:2 * i + 2, :].rearrange("p h m -> p (h m)")).then_inc(s_ps[t], 1)
                elif step == "nm":
                    pe.wait_ge(max_set[1], (g + 1) * 4)
                    for t in range(TU):
                        ins = t_.transpose(A[0:H, columns(t)], nmax[u][:, t, :], ident[:, :])
                    ins.then_inc(nm_ps, 1)
                elif step in ("n01", "n2", "n3", "n4"):
                    for n in dict(n01=(0, 1), n2=(2,), n3=(3,), n4=(4,))[step]:
                        if n == 0 and g == 0:
                            pe.wait_ge(sel_set, 1)
                        if n == 0:
                            pe.wait_ge(nm_sb, g + 1)
                            pe.wait_ge(kb_set, (b + 1) * 4)
                        elif n == 2:
                            pe.wait_ge(e_set[0], g + 1)
                        elif n == 3:
                            pe.wait_ge(e_set[2], g + 1)
                        elif n == 4:
                            pe.wait_ge(av_sb[0], g + 1)
                        for i in range(2):
                            o = (A, Bk, A, A, Bk)[n][:, i * UL:(i + 1) * UL]
                            if n == 2:
                                keys = kb[k][:, H * P + i * P:H * P + (i + 1) * P]
                                pick = selt[:, i * HG:(i + 1) * HG, :].rearrange("p h m -> p (h m)")
                            else:
                                h = 2 * (n if n < 2 else n - 1) + i
                                keys, pick = kb[k][:, h * P:(h + 1) * P], sel[:, h, :]
                            mul(o, pick, nmT[u][:, :], stop=False)
                            ins = mul(o, keys, qT[u][:, :], start=False)
                        ins.then_inc(st_ps[n], 1)
                elif step in ("av0", "av1"):
                    gr = int(step[2])
                    pe.wait_ge(e_set[(2, 4)[gr]], g + 1)
                    for at in (0, 1):
                        for i in range(HG):
                            h = gr * HG + i
                            o = (Bk, A)[gr][i * Q:(i + 1) * Q, 0:UL]
                            if at == 0:
                                mul(o, vm[k][:, h * Q:(h + 1) * Q], pT[u][:, i, :], stop=False)
                            else:
                                ins = mul(o, vt[k][:, h * Q:(h + 1) * Q], pT[u][:, HG + gr, :], start=False)
                    ins.then_inc(av_ps[gr], 1)
                elif step == "avT":
                    pe.wait_ge(av_sb[1], g + 1)
                    for t in range(TU):
                        for gr in range(2):
                            at = t * 2 * P + gr * P
                            ins = t_.transpose(Bk[:, at:at + P], av[u][gr][:, columns(t)], ident[:, :])
                    ins.then_inc(avT_ps, 1)
                elif step == "caT":
                    pe.wait_ge(ca_set, g + 1)
                    turned(A, lambda t: y[u][:, t, :], tr_ps[2])
                elif step == "y2":
                    pe.wait_ge(tr_sb[2], g + 1)
                    if g == 0:
                        pe.wait_ge(brow_set, 2)
                    for t in range(TU):
                        biased(Bk[:, columns(t)], C_MO, D)
                        mul(Bk[:, columns(t)], actT[u][:, columns(t)], wt[:, T_MO, :], start=False, stop=False)
                        ins = mul(Bk[:, columns(t)], ident[:, :], x1[u][:, t, :], start=False)
                    ins.then_inc(y2_ps, 1)
                elif step == "x2T":
                    pe.wait_ge(x2_set, g + 1)
                    turned(A, lambda t: x2[u][:, t, :], tr_ps[3])
                elif step == "l1":
                    pe.wait_ge(tr_sb[3], g + 1)
                    for c in range(FFC):
                        ins = mul((A, Bk)[c // 2][:, c % 2 * UL:(c % 2 + 1) * UL], wt[:, T_L1 + c, :], actT[u][:, :])
                        if c % 2:
                            ins.then_inc(l1_ps, 1)
                elif step == "l2":
                    pe.wait_ge(l1_sb, (g + 1) * FFC)
                    for t in range(TU):
                        biased(A[:, columns(t)], C_L2, D)
                        for c in range(FFC):
                            mul(A[:, columns(t)], pT[u][:, c, columns(t)], wt[:, T_L2 + c, :],
                                start=False, stop=False)
                        ins = mul(A[:, columns(t)], ident[:, :], x2[u][:, t, :], start=False)
                    ins.then_inc(y3_ps, 1)
                elif step == "nT":
                    pe.wait_ge(n_set, g + 1)
                    turned(Bk, lambda t: row_buf[0][:, g * TU + t, 0:D], tr_ps[4])
                elif step == "router":
                    pe.wait_ge(tr_sb[4], g + 1)
                    if g == 0:
                        pe.wait_ge(in_late, 16 * 3)
                    for t in range(TU):
                        o = A[:, t * E:(t + 1) * E]
                        biased(o, C_BR, E)
                        ins = mul(o, actT[u][:, columns(t)], wr[:, :], start=False)
                    ins.then_inc(lg_ps, 1)
                elif step == "hid" and g == G - 1:
                    pe.wait_ge(nT_set, TB // TU * (B - 1))
                    pe.wait_ge(lg_set, TB // TU * (B - 1))
                    pe.wait_ge(slots_set, nth[G - TB // TU - 1] + 1)
                    for batch in range(2):
                        hidden(batch)
                elif step == "rank" and g in ROUTED:
                    cols = len(ROUTED[g]) * E
                    pe.wait_ge(picks_set, nth[g] + 1)
                    mul(A[:, 0:cols], before[:, :], picks[:, 0:cols])
                    mul(A[:, cols:2 * cols], onef[:, :], picks[:, 0:cols]).then_inc(rank_ps, 1)
            shared(0)
            pe.wait_ge(hs_set, 2)
            hidden(2)
            shared(1)
            pe.wait_ge(nT_set, G)
            pe.wait_ge(lg_set, G)
            hidden(3)
            shared(2)
            shared(3)
            pe.wait_ge(slots_set, len(ROUTED))
            pe.wait_ge(sh_set, B)
            pe.wait_ge(meta_set, 1)
            pe.wait_ge(in_w2, 16 * E)

            def up(j, k):
                pe.wait_ge(w_sb, j + 1)
                pe.wait_ge(xt_sb, j + 1)
                for c in range(FC):
                    ins = mul(bank[k % 2][1 + c // 2][:, c % 2 * P:(c % 2 + 1) * P],
                              wbuf[:, k % WB, c * P:(c + 1) * P], xtT[k % 2])
                    if c % 2:
                        ins.then_inc(up_ps, 1)

            def turn_tokens(j, k, uses):
                pe.wait_ge(xt_in[k % RU], 16 * uses)
                t_.transpose(bank[k % 2][0][:, 0:P], xt[k % RU][:, 0:D], ident[:, :]).then_inc(xt_ps, 1)

            def down(j, k):
                e = pe.value_load(meta[0:1, 0, bass.ds(j, 1)], min_val=0, max_val=E - 1)
                o = bank[k % 2][3][:, 0:D]
                mul(o, one2[:, :], brow[:, bass.ds(e * D + C_B2, D)], stop=False)
                for c in range(FC):
                    pe.wait_ge(h_set, j * FC + c + 1)
                    ins = mul(o, hT[k % 2][:, c * P:(c + 1) * P], w2s[:, bass.ds(e * F + c * D, D)],
                              start=False, stop=c == FC - 1)
                ins.then_inc(dn_ps, 1)

            def pe_step(j, k, uses):
                up(j, k)
                turn_tokens(j + 1, k + 1, uses)
                down(j - 1, k - 1)

            turn_tokens(0, 0, 1)
            up(0, 0)
            turn_tokens(1, 1, 1)
            with pe.Fori(0, ETURNS) as it:
                for k in range(1, RU + 1):
                    pe_step(it * RU + k, k, it + (k + 1) // RU + 1)
            for j in range(ETURNS * RU + 1, TILES - 1):
                pe_step(j, j, (j + 1) // RU + 1)
            up(TILES - 1, TILES - 1)
            down(TILES - 2, TILES - 2)
            pe.wait_ge(y_set[(TILES - 3) % RU], (TILES - 3) // RU + 1)
            down(TILES - 1, TILES - 1)

            for k in (TILES - 2, TILES - 1):
                pe.wait_ge(y_set[k % RU], k // RU + 1)

            def add_rows(g, ap, start=False, stop=False):
                return mul(psum[:, g, 0:UL], ident[:, :], flat3(ap[:, g * TU:(g + 1) * TU, :]), start, stop)

            for g in range(G):
                add_rows(g, nT_all, start=True)
            for g in range(G):
                pe.wait_ge(res_in[g // (TB // TU)], 16 * K2)
                add_rows(g, res[0])
                add_rows(g, res[1], stop=True).then_inc(sum_ps, 1)


_NAMES = [
    "x", "ctx_1024",
    *("L0_xattn_" + n for n in (
        "qkv_w", "qkv_b", "sa_out_w", "sa_out_b", "in_proj_w", "in_proj_b", "mha_out_w", "mha_out_b",
        "lin1_w", "lin1_b", "lin2_w", "lin2_b", "ln1_g", "ln1_b", "ln2_g", "ln2_b", "ln3_g", "ln3_b")),
    *("L0_ffn_" + n for n in (
        "router_w", "router_b", "w1", "b1", "gate", "w2", "b2", "sw1", "sb1", "sgate", "sw2", "sb2",
        "shared_weight", "ln_g", "ln_b")),
]


def kernel(**inputs):
    import numpy as np
    import concourse.bacc as bacc
    from concourse.bass_utils import run_bass_kernel_spmd

    nc = bacc.Bacc("TRN2", target_bir_lowering=False, num_devices=1)
    arrays, args = {}, []
    for name in _NAMES:
        a = np.ascontiguousarray(inputs[name])
        if a.ndim == 0:
            a = a.reshape(1)
        arrays[f"in_{name}"] = a
        args.append(nc.dram_tensor(f"in_{name}", a.shape, mybir.dt.from_np(a.dtype), kind="ExternalInput").ap())
    shape = inputs["x"].shape
    args.append(nc.dram_tensor("out_x", shape, F32, kind="ExternalOutput").ap())
    xattn_moe_kernel(nc, *args)
    r = run_bass_kernel_spmd(nc, [arrays], core_ids=[0])
    return r.results[0]["out_x"]
```
